# Optimizing a Trainium2 kernel written in Bass

```python
import numpy as np
import jax
import jax.numpy as jnp

def _softmax(x, axis=-1):
    return jax.nn.softmax(x, axis=axis)

def _gelu(x):
    return jax.nn.gelu(x, approximate=True)

def _silu(x):
    return jax.nn.silu(x)

def _sigmoid(x):
    return jax.nn.sigmoid(x)

def _layernorm(x, axis=-1, eps=1e-05):
    m = jnp.mean(x, axis=axis, keepdims=True)
    v = jnp.var(x, axis=axis, keepdims=True)
    return (x - m) / jnp.sqrt(v + eps)

def _scatter_add(tgt, idx, src, axis=0):
    return tgt.at[idx].add(src)

def _segment_sum(src, seg, n):
    return jax.ops.segment_sum(src, seg, n)
kernel_name = 'mk_gps_d2_gnn_r8_e49906'

def setup_inputs(seed: int=0):
    np.random.seed(seed)
    _w = jnp.asarray

    def _rec_inputs():
        import jax
        import jax.numpy as jnp
        _gk = jax.random.key(seed)
        x = -0.0001126 + 1 * jax.random.normal(jax.random.fold_in(_gk, 1), (1250, 768), jnp.float32)
        src = jax.random.randint(jax.random.fold_in(_gk, 2), (20000,), 0, 1250, jnp.int32)
        dst = jax.random.randint(jax.random.fold_in(_gk, 3), (20000,), 0, 1250, jnp.int32)
        _o = jnp.argsort(dst, stable=True)
        src = src[_o]
        dst = dst[_o]
        return (x, src, dst)
    x, src, dst = _rec_inputs()

    def _L0_gnn_setup():
        import jax, jax.numpy as jnp
        import numpy as np
        N_NODES = 1250
        NEG_SLOPE = 0.2
        EPS = 1e-16

        def gat_layer(x, W, att_src, att_dst, bias, src, dst, heads, out_ch, concat):
            n = x.shape[0]
            h = (x @ W.T).reshape(n, heads, out_ch)
            a_src = jnp.einsum('nhc,hc->nh', h, att_src)
            a_dst = jnp.einsum('nhc,hc->nh', h, att_dst)
            e = a_src[src] + a_dst[dst]
            e = jax.nn.leaky_relu(e, NEG_SLOPE)
            m = jax.ops.segment_max(e, dst, num_segments=n)
            ex = jnp.exp(e - m[dst])
            denom = jax.ops.segment_sum(ex, dst, num_segments=n)
            alpha = ex / (denom[dst] + EPS)
            msg = alpha[:, :, None] * h[src]
            out = jax.ops.segment_sum(msg, dst, num_segments=n)
            if concat:
                out = out.reshape(n, heads * out_ch)
            else:
                out = out.mean(axis=1)
            return out + bias
        key = jax.random.key(seed)
        ks = jax.random.split(key, 12)
        x = jax.random.normal(ks[0], (N_NODES, 768), dtype=jnp.float32)
        edge_index = jax.random.randint(ks[1], (2, 20000), 0, N_NODES, dtype=jnp.int64)
        s1 = 1.0 / np.sqrt(768.0)
        W1 = jax.random.normal(ks[2], (8 * 128, 768), dtype=jnp.float32) * s1
        att_src1 = jax.random.normal(ks[3], (8, 128), dtype=jnp.float32) * (1.0 / np.sqrt(128.0))
        att_dst1 = jax.random.normal(ks[4], (8, 128), dtype=jnp.float32) * (1.0 / np.sqrt(128.0))
        b1 = jnp.zeros((8 * 128,), dtype=jnp.float32)
        s2 = 1.0 / np.sqrt(1024.0)
        W2 = jax.random.normal(ks[5], (1 * 768, 1024), dtype=jnp.float32) * s2
        att_src2 = jax.random.normal(ks[6], (1, 768), dtype=jnp.float32) * (1.0 / np.sqrt(768.0))
        att_dst2 = jax.random.normal(ks[7], (1, 768), dtype=jnp.float32) * (1.0 / np.sqrt(768.0))
        b2 = jnp.zeros((768,), dtype=jnp.float32)
        return {'x': x, 'edge_index': edge_index, 'W1': W1, 'att_src1': att_src1, 'att_dst1': att_dst1, 'b1': b1, 'W2': W2, 'att_src2': att_src2, 'att_dst2': att_dst2, 'b2': b2}
    _L0_gnn_all = _L0_gnn_setup()
    _L0_gnn_in = {k: v for k, v in _L0_gnn_all.items() if k in ('W1', 'att_src1', 'att_dst1', 'b1', 'W2', 'att_src2', 'att_dst2', 'b2')}
    del _L0_gnn_all

    def _L0_mix_setup():
        import jax, jax.numpy as jnp
        import numpy as np
        DIM = 768
        HEADS = 12
        HEAD_DIM = DIM // HEADS
        M = int(DIM * 0.5)
        HIDDEN = int(DIM * 4.0)
        SCALE = HEAD_DIM ** (-0.25)
        EPSILON = 1e-08
        LN_EPS = 1e-05

        def _orf(key):

            def one(k):
                a = jax.random.normal(k, (M, HEAD_DIM))
                q, _ = jnp.linalg.qr(a)
                return q.T
            ks = jax.random.split(key, HEADS)
            return jax.vmap(one)(ks) * np.sqrt(M)

        def _layernorm(x, g, b):
            mu = jnp.mean(x, axis=-1, keepdims=True)
            var = jnp.mean(jnp.square(x - mu), axis=-1, keepdims=True)
            return (x - mu) * jax.lax.rsqrt(var + LN_EPS) * g + b

        def _feature_map(x, w):
            xs = x * SCALE
            proj = jnp.einsum('bhnc,hcm->bhnm', xs, w)
            sq = 0.5 * jnp.sum(xs * xs, axis=-1, keepdims=True)
            return jnp.exp(proj - sq) / np.sqrt(M)

        def _performer_attn(x, qkv_w, qkv_b, w_orf, proj_w, proj_b):
            B, N, _ = x.shape
            qkv = x @ qkv_w + qkv_b
            qkv = qkv.reshape(B, N, 3, HEADS, HEAD_DIM)
            qkv = jnp.transpose(qkv, (2, 0, 3, 1, 4))
            q = _feature_map(qkv[0], w_orf)
            k = _feature_map(qkv[1], w_orf)
            v = qkv[2]
            k_sum = jnp.sum(k, axis=2)
            D = jnp.einsum('bhnm,bhm->bhn', q, k_sum)[..., None] + EPSILON
            ktv = jnp.einsum('bhnm,bhnc->bhmc', k, v)
            out = jnp.einsum('bhnm,bhmc->bhnc', q, ktv) / D
            out = jnp.transpose(out, (0, 2, 1, 3)).reshape(B, N, DIM)
            return out @ proj_w + proj_b
        key = jax.random.key(seed)
        ks = jax.random.split(key, 8)
        s = 0.02
        return {'x': jax.random.normal(ks[0], (32, 1024, DIM), jnp.float32), 'ln1_g': jnp.ones((DIM,), jnp.float32), 'ln1_b': jnp.zeros((DIM,), jnp.float32), 'qkv_w': jax.random.normal(ks[1], (DIM, 3 * DIM), jnp.float32) * s, 'qkv_b': jnp.zeros((3 * DIM,), jnp.float32), 'w_orf': _orf(ks[2]).astype(jnp.float32), 'proj_w': jax.random.normal(ks[3], (DIM, DIM), jnp.float32) * s, 'proj_b': jnp.zeros((DIM,), jnp.float32), 'ln2_g': jnp.ones((DIM,), jnp.float32), 'ln2_b': jnp.zeros((DIM,), jnp.float32), 'fc1_w': jax.random.normal(ks[4], (DIM, HIDDEN), jnp.float32) * s, 'fc1_b': jnp.zeros((HIDDEN,), jnp.float32), 'fc2_w': jax.random.normal(ks[5], (HIDDEN, DIM), jnp.float32) * s, 'fc2_b': jnp.zeros((DIM,), jnp.float32)}
    _L0_mix_all = _L0_mix_setup()
    _L0_mix_in = {k: v for k, v in _L0_mix_all.items() if k in ('ln1_g', 'ln1_b', 'qkv_w', 'qkv_b', 'w_orf', 'proj_w', 'proj_b', 'ln2_g', 'ln2_b', 'fc1_w', 'fc1_b', 'fc2_w', 'fc2_b')}
    del _L0_mix_all

    def _L0_ffn_setup():
        import jax, jax.numpy as jnp
        import numpy as np
        B, T, D = (2, 256, 768)
        S, R, M, K = (8, 16, 64, 4)
        H, G = (32, 256)

        def _ssinf3(x, P, C, W1, b1, W2, b2, G1, g1b, G2, g2b):
            shp = x.shape
            xf = x.reshape(-1, shp[-1])
            z = jnp.einsum('nd,sdr->nsr', xf, P)
            scores = jnp.einsum('nsr,smr->nsm', z, C)
            topv, topi = jax.lax.top_k(scores, K)
            w = jax.nn.softmax(topv, axis=-1)
            sidx = jnp.arange(S)[None, :, None]
            W1g = W1[sidx, topi]
            b1g = b1[sidx, topi]
            W2g = W2[sidx, topi]
            b2g = b2[sidx, topi]
            h = jax.nn.gelu(jnp.einsum('nsr,nskrh->nskh', z, W1g) + b1g)
            yl = jnp.einsum('nskh,nskhr->nskr', h, W2g) + b2g
            comb = jnp.einsum('nskr,nsk->nsr', yl, w)
            comb = comb.reshape(xf.shape[0], S * R)
            out = jax.nn.gelu(comb @ G1 + g1b) @ G2 + g2b
            return out.reshape(shp)
        key = jax.random.key(seed)
        k = jax.random.split(key, 8)
        rn = lambda kk, shape, s: jax.random.normal(kk, shape, dtype=jnp.float32) * s
        return {'x': rn(k[0], (B, T, D), 1.0), 'P': rn(k[1], (S, D, R), D ** (-0.5)), 'C': rn(k[2], (S, M, R), R ** (-0.5)), 'W1': rn(k[3], (S, M, R, H), R ** (-0.5)), 'b1': jnp.zeros((S, M, H), jnp.float32), 'W2': rn(k[4], (S, M, H, R), H ** (-0.5)), 'b2': jnp.zeros((S, M, R), jnp.float32), 'G1': rn(k[5], (S * R, G), (S * R) ** (-0.5)), 'g1b': jnp.zeros((G,), jnp.float32), 'G2': rn(k[6], (G, D), G ** (-0.5)), 'g2b': jnp.zeros((D,), jnp.float32)}
    _L0_ffn_all = _L0_ffn_setup()
    _L0_ffn_in = {k: v for k, v in _L0_ffn_all.items() if k in ('P', 'C', 'W1', 'b1', 'W2', 'b2', 'G1', 'g1b', 'G2', 'g2b')}
    del _L0_ffn_all

    def _L1_gnn_setup():
        import jax, jax.numpy as jnp
        import numpy as np
        N = 2500
        E_RAND = 40000
        NEG_SLOPE = 0.2

        def gat_layer(x, W, a_src, a_dst, bias, src, dst, heads, out_c, concat):
            n = x.shape[0]
            h = (x @ W).reshape(n, heads, out_c)
            al_s = jnp.einsum('nhc,hc->nh', h, a_src)
            al_d = jnp.einsum('nhc,hc->nh', h, a_dst)
            e = jax.nn.leaky_relu(al_s[src] + al_d[dst], NEG_SLOPE)
            m = jax.ops.segment_max(e, dst, num_segments=n)
            ex = jnp.exp(e - m[dst])
            z = jax.ops.segment_sum(ex, dst, num_segments=n)
            alpha = ex / (z[dst] + 1e-16)
            msg = h[src] * alpha[:, :, None]
            out = jax.ops.segment_sum(msg, dst, num_segments=n)
            out = out.reshape(n, heads * out_c) if concat else out.mean(axis=1)
            return out + bias
        key = jax.random.key(seed)
        ks = jax.random.split(key, 10)
        x = jax.random.normal(ks[0], (N, 768), dtype=jnp.float32)
        src = jax.random.randint(ks[1], (E_RAND,), 0, N)
        dst = jax.random.randint(ks[2], (E_RAND,), 0, N)
        loop = jnp.arange(N)
        edge_index = jnp.stack([jnp.concatenate([src, loop]), jnp.concatenate([dst, loop])])
        s = 1.0 / np.sqrt(768.0)
        W1 = jax.random.normal(ks[3], (768, 768), dtype=jnp.float32) * s
        a_src1 = jax.random.normal(ks[4], (8, 96), dtype=jnp.float32) * 0.1
        a_dst1 = jax.random.normal(ks[5], (8, 96), dtype=jnp.float32) * 0.1
        b1 = jnp.zeros((768,), dtype=jnp.float32)
        W2 = jax.random.normal(ks[6], (768, 768), dtype=jnp.float32) * s
        a_src2 = jax.random.normal(ks[7], (1, 768), dtype=jnp.float32) * 0.1
        a_dst2 = jax.random.normal(ks[8], (1, 768), dtype=jnp.float32) * 0.1
        b2 = jnp.zeros((768,), dtype=jnp.float32)
        return {'x': x, 'edge_index': edge_index, 'W1': W1, 'a_src1': a_src1, 'a_dst1': a_dst1, 'b1': b1, 'W2': W2, 'a_src2': a_src2, 'a_dst2': a_dst2, 'b2': b2}
    _L1_gnn_all = _L1_gnn_setup()
    _L1_gnn_in = {k: v for k, v in _L1_gnn_all.items() if k in ('W1', 'a_src1', 'a_dst1', 'b1', 'W2', 'a_src2', 'a_dst2', 'b2')}
    del _L1_gnn_all

    def _L1_mix_setup():
        import jax, jax.numpy as jnp
        import numpy as np
        import math
        B, N, C = (8, 512, 768)
        H = 12
        DH = C // H
        M = 256
        LN_EPS = 1e-05

        def _phi(t, random_features):
            norm_sq = 0.5 * jnp.sum(t * t, axis=-1, keepdims=True)
            proj = jnp.einsum('bhnd,md->bhnm', t, random_features)
            return jnp.exp(proj - norm_sq) * (1.0 / math.sqrt(M))
        key = jax.random.key(seed)
        ks = jax.random.split(key, 7)
        x = jax.random.normal(ks[0], (B, N, C), dtype=jnp.float32)
        W_qkv = jax.random.normal(ks[1], (C, 3 * C), dtype=jnp.float32) * (1.0 / math.sqrt(C))
        W_proj = jax.random.normal(ks[2], (C, C), dtype=jnp.float32) * (1.0 / math.sqrt(C))
        b_proj = jnp.zeros((C,), dtype=jnp.float32)
        gamma = jnp.ones((C,), dtype=jnp.float32)
        beta = jnp.zeros((C,), dtype=jnp.float32)
        random_features = jax.random.normal(ks[3], (M, DH), dtype=jnp.float32) / math.sqrt(DH)
        return {'x': x, 'W_qkv': W_qkv, 'W_proj': W_proj, 'b_proj': b_proj, 'gamma': gamma, 'beta': beta, 'random_features': random_features}
    _L1_mix_all = _L1_mix_setup()
    _L1_mix_in = {k: v for k, v in _L1_mix_all.items() if k in ('W_qkv', 'W_proj', 'b_proj', 'gamma', 'beta', 'random_features')}
    del _L1_mix_all

    def _L1_ffn_setup():
        import jax, jax.numpy as jnp
        import numpy as np
        EPS_NORM = 1e-06
        EPS_Q = 1e-05

        def rmsnorm(x, g):
            return x * jax.lax.rsqrt(jnp.mean(x * x, axis=-1, keepdims=True) + EPS_NORM) * g

        def activation_quant(x):
            scale = 127.0 / jnp.maximum(jnp.max(jnp.abs(x), axis=-1, keepdims=True), EPS_Q)
            return jnp.clip(jnp.round(x * scale), -128, 127) / scale

        def weight_quant(w):
            scale = 1.0 / jnp.maximum(jnp.mean(jnp.abs(w)), EPS_Q)
            return jnp.clip(jnp.round(w * scale), -1, 1) / scale

        def bitlinear(x, w, g):
            x_norm = rmsnorm(x, g)
            x_q = x_norm + jax.lax.stop_gradient(activation_quant(x_norm) - x_norm)
            w_q = w + jax.lax.stop_gradient(weight_quant(w) - w)
            return jnp.einsum('bsd,od->bso', x_q, w_q)
        key = jax.random.key(seed)
        k1, k2, k3 = jax.random.split(key, 3)
        B, S, D, H = (8, 512, 768, 256)
        x = jax.random.normal(k1, (B, S, D), dtype=jnp.float32)
        w_in = jax.random.normal(k2, (2 * H, D), dtype=jnp.float32) * 0.002
        w_out = jax.random.normal(k3, (D, H), dtype=jnp.float32) * 0.002
        g_in = jnp.ones((D,), dtype=jnp.float32)
        g_out = jnp.ones((H,), dtype=jnp.float32)
        return {'x': x, 'w_in': w_in, 'g_in': g_in, 'w_out': w_out, 'g_out': g_out}
    _L1_ffn_all = _L1_ffn_setup()
    _L1_ffn_in = {k: v for k, v in _L1_ffn_all.items() if k in ('w_in', 'g_in', 'w_out', 'g_out')}
    del _L1_ffn_all
    return {'x': x, 'src': src, 'dst': dst, 'L0_gnn_W1': _L0_gnn_in['W1'], 'L0_gnn_att_src1': _L0_gnn_in['att_src1'], 'L0_gnn_att_dst1': _L0_gnn_in['att_dst1'], 'L0_gnn_b1': _L0_gnn_in['b1'], 'L0_gnn_W2': _L0_gnn_in['W2'], 'L0_gnn_att_src2': _L0_gnn_in['att_src2'], 'L0_gnn_att_dst2': _L0_gnn_in['att_dst2'], 'L0_gnn_b2': _L0_gnn_in['b2'], 'L0_mix_ln1_g': _L0_mix_in['ln1_g'], 'L0_mix_ln1_b': _L0_mix_in['ln1_b'], 'L0_mix_qkv_w': _L0_mix_in['qkv_w'], 'L0_mix_qkv_b': _L0_mix_in['qkv_b'], 'L0_mix_w_orf': _L0_mix_in['w_orf'], 'L0_mix_proj_w': _L0_mix_in['proj_w'], 'L0_mix_proj_b': _L0_mix_in['proj_b'], 'L0_mix_ln2_g': _L0_mix_in['ln2_g'], 'L0_mix_ln2_b': _L0_mix_in['ln2_b'], 'L0_mix_fc1_w': _L0_mix_in['fc1_w'], 'L0_mix_fc1_b': _L0_mix_in['fc1_b'], 'L0_mix_fc2_w': _L0_mix_in['fc2_w'], 'L0_mix_fc2_b': _L0_mix_in['fc2_b'], 'L0_ffn_P': _L0_ffn_in['P'], 'L0_ffn_C': _L0_ffn_in['C'], 'L0_ffn_W1': _L0_ffn_in['W1'], 'L0_ffn_b1': _L0_ffn_in['b1'], 'L0_ffn_W2': _L0_ffn_in['W2'], 'L0_ffn_b2': _L0_ffn_in['b2'], 'L0_ffn_G1': _L0_ffn_in['G1'], 'L0_ffn_g1b': _L0_ffn_in['g1b'], 'L0_ffn_G2': _L0_ffn_in['G2'], 'L0_ffn_g2b': _L0_ffn_in['g2b'], 'L1_gnn_W1': _L1_gnn_in['W1'], 'L1_gnn_a_src1': _L1_gnn_in['a_src1'], 'L1_gnn_a_dst1': _L1_gnn_in['a_dst1'], 'L1_gnn_b1': _L1_gnn_in['b1'], 'L1_gnn_W2': _L1_gnn_in['W2'], 'L1_gnn_a_src2': _L1_gnn_in['a_src2'], 'L1_gnn_a_dst2': _L1_gnn_in['a_dst2'], 'L1_gnn_b2': _L1_gnn_in['b2'], 'L1_mix_W_qkv': _L1_mix_in['W_qkv'], 'L1_mix_W_proj': _L1_mix_in['W_proj'], 'L1_mix_b_proj': _L1_mix_in['b_proj'], 'L1_mix_gamma': _L1_mix_in['gamma'], 'L1_mix_beta': _L1_mix_in['beta'], 'L1_mix_random_features': _L1_mix_in['random_features'], 'L1_ffn_w_in': _L1_ffn_in['w_in'], 'L1_ffn_g_in': _L1_ffn_in['g_in'], 'L1_ffn_w_out': _L1_ffn_in['w_out'], 'L1_ffn_g_out': _L1_ffn_in['g_out']}

def reference(x, src, dst, L0_gnn_W1, L0_gnn_att_src1, L0_gnn_att_dst1, L0_gnn_b1, L0_gnn_W2, L0_gnn_att_src2, L0_gnn_att_dst2, L0_gnn_b2, L0_mix_ln1_g, L0_mix_ln1_b, L0_mix_qkv_w, L0_mix_qkv_b, L0_mix_w_orf, L0_mix_proj_w, L0_mix_proj_b, L0_mix_ln2_g, L0_mix_ln2_b, L0_mix_fc1_w, L0_mix_fc1_b, L0_mix_fc2_w, L0_mix_fc2_b, L0_ffn_P, L0_ffn_C, L0_ffn_W1, L0_ffn_b1, L0_ffn_W2, L0_ffn_b2, L0_ffn_G1, L0_ffn_g1b, L0_ffn_G2, L0_ffn_g2b, L1_gnn_W1, L1_gnn_a_src1, L1_gnn_a_dst1, L1_gnn_b1, L1_gnn_W2, L1_gnn_a_src2, L1_gnn_a_dst2, L1_gnn_b2, L1_mix_W_qkv, L1_mix_W_proj, L1_mix_b_proj, L1_mix_gamma, L1_mix_beta, L1_mix_random_features, L1_ffn_w_in, L1_ffn_g_in, L1_ffn_w_out, L1_ffn_g_out):
    import jax
    import jax.numpy as jnp

    def _L0_gnn_ref(x, edge_index, W1, att_src1, att_dst1, b1, W2, att_src2, att_dst2, b2):
        import jax, jax.numpy as jnp
        import numpy as np
        N_NODES = 1250
        NEG_SLOPE = 0.2
        EPS = 1e-16

        def gat_layer(x, W, att_src, att_dst, bias, src, dst, heads, out_ch, concat):
            n = x.shape[0]
            h = (x @ W.T).reshape(n, heads, out_ch)
            a_src = jnp.einsum('nhc,hc->nh', h, att_src)
            a_dst = jnp.einsum('nhc,hc->nh', h, att_dst)
            e = a_src[src] + a_dst[dst]
            e = jax.nn.leaky_relu(e, NEG_SLOPE)
            m = jax.ops.segment_max(e, dst, num_segments=n)
            ex = jnp.exp(e - m[dst])
            denom = jax.ops.segment_sum(ex, dst, num_segments=n)
            alpha = ex / (denom[dst] + EPS)
            msg = alpha[:, :, None] * h[src]
            out = jax.ops.segment_sum(msg, dst, num_segments=n)
            if concat:
                out = out.reshape(n, heads * out_ch)
            else:
                out = out.mean(axis=1)
            return out + bias
        src, dst = (edge_index[0], edge_index[1])
        h = gat_layer(x, W1, att_src1, att_dst1, b1, src, dst, heads=8, out_ch=128, concat=True)
        h = jax.nn.relu(h)
        out = gat_layer(h, W2, att_src2, att_dst2, b2, src, dst, heads=1, out_ch=768, concat=True)
        return out

    def _L0_mix_ref(x, ln1_g, ln1_b, qkv_w, qkv_b, w_orf, proj_w, proj_b, ln2_g, ln2_b, fc1_w, fc1_b, fc2_w, fc2_b):
        import jax, jax.numpy as jnp
        import numpy as np
        DIM = 768
        HEADS = 12
        HEAD_DIM = DIM // HEADS
        M = int(DIM * 0.5)
        HIDDEN = int(DIM * 4.0)
        SCALE = HEAD_DIM ** (-0.25)
        EPSILON = 1e-08
        LN_EPS = 1e-05

        def _orf(key):

            def one(k):
                a = jax.random.normal(k, (M, HEAD_DIM))
                q, _ = jnp.linalg.qr(a)
                return q.T
            ks = jax.random.split(key, HEADS)
            return jax.vmap(one)(ks) * np.sqrt(M)

        def _layernorm(x, g, b):
            mu = jnp.mean(x, axis=-1, keepdims=True)
            var = jnp.mean(jnp.square(x - mu), axis=-1, keepdims=True)
            return (x - mu) * jax.lax.rsqrt(var + LN_EPS) * g + b

        def _feature_map(x, w):
            xs = x * SCALE
            proj = jnp.einsum('bhnc,hcm->bhnm', xs, w)
            sq = 0.5 * jnp.sum(xs * xs, axis=-1, keepdims=True)
            return jnp.exp(proj - sq) / np.sqrt(M)

        def _performer_attn(x, qkv_w, qkv_b, w_orf, proj_w, proj_b):
            B, N, _ = x.shape
            qkv = x @ qkv_w + qkv_b
            qkv = qkv.reshape(B, N, 3, HEADS, HEAD_DIM)
            qkv = jnp.transpose(qkv, (2, 0, 3, 1, 4))
            q = _feature_map(qkv[0], w_orf)
            k = _feature_map(qkv[1], w_orf)
            v = qkv[2]
            k_sum = jnp.sum(k, axis=2)
            D = jnp.einsum('bhnm,bhm->bhn', q, k_sum)[..., None] + EPSILON
            ktv = jnp.einsum('bhnm,bhnc->bhmc', k, v)
            out = jnp.einsum('bhnm,bhmc->bhnc', q, ktv) / D
            out = jnp.transpose(out, (0, 2, 1, 3)).reshape(B, N, DIM)
            return out @ proj_w + proj_b
        h = x + _performer_attn(_layernorm(x, ln1_g, ln1_b), qkv_w, qkv_b, w_orf, proj_w, proj_b)
        y = _layernorm(h, ln2_g, ln2_b)
        y = jax.nn.gelu(y @ fc1_w + fc1_b) @ fc2_w + fc2_b
        return h + y

    def _L0_ffn_ref(x, P, C, W1, b1, W2, b2, G1, g1b, G2, g2b):
        import jax, jax.numpy as jnp
        import numpy as np
        B, T, D = (2, 256, 768)
        S, R, M, K = (8, 16, 64, 4)
        H, G = (32, 256)

        def _ssinf3(x, P, C, W1, b1, W2, b2, G1, g1b, G2, g2b):
            shp = x.shape
            xf = x.reshape(-1, shp[-1])
            z = jnp.einsum('nd,sdr->nsr', xf, P)
            scores = jnp.einsum('nsr,smr->nsm', z, C)
            topv, topi = jax.lax.top_k(scores, K)
            w = jax.nn.softmax(topv, axis=-1)
            sidx = jnp.arange(S)[None, :, None]
            W1g = W1[sidx, topi]
            b1g = b1[sidx, topi]
            W2g = W2[sidx, topi]
            b2g = b2[sidx, topi]
            h = jax.nn.gelu(jnp.einsum('nsr,nskrh->nskh', z, W1g) + b1g)
            yl = jnp.einsum('nskh,nskhr->nskr', h, W2g) + b2g
            comb = jnp.einsum('nskr,nsk->nsr', yl, w)
            comb = comb.reshape(xf.shape[0], S * R)
            out = jax.nn.gelu(comb @ G1 + g1b) @ G2 + g2b
            return out.reshape(shp)
        return _ssinf3(x, P, C, W1, b1, W2, b2, G1, g1b, G2, g2b)

    def _L1_gnn_ref(x, edge_index, W1, a_src1, a_dst1, b1, W2, a_src2, a_dst2, b2):
        import jax, jax.numpy as jnp
        import numpy as np
        N = 2500
        E_RAND = 40000
        NEG_SLOPE = 0.2

        def gat_layer(x, W, a_src, a_dst, bias, src, dst, heads, out_c, concat):
            n = x.shape[0]
            h = (x @ W).reshape(n, heads, out_c)
            al_s = jnp.einsum('nhc,hc->nh', h, a_src)
            al_d = jnp.einsum('nhc,hc->nh', h, a_dst)
            e = jax.nn.leaky_relu(al_s[src] + al_d[dst], NEG_SLOPE)
            m = jax.ops.segment_max(e, dst, num_segments=n)
            ex = jnp.exp(e - m[dst])
            z = jax.ops.segment_sum(ex, dst, num_segments=n)
            alpha = ex / (z[dst] + 1e-16)
            msg = h[src] * alpha[:, :, None]
            out = jax.ops.segment_sum(msg, dst, num_segments=n)
            out = out.reshape(n, heads * out_c) if concat else out.mean(axis=1)
            return out + bias
        src, dst = (edge_index[0], edge_index[1])
        h = gat_layer(x, W1, a_src1, a_dst1, b1, src, dst, heads=8, out_c=96, concat=True)
        h = jax.nn.elu(h)
        out = gat_layer(h, W2, a_src2, a_dst2, b2, src, dst, heads=1, out_c=768, concat=False)
        return out

    def _L1_mix_ref(x, W_qkv, W_proj, b_proj, gamma, beta, random_features):
        import jax, jax.numpy as jnp
        import numpy as np
        import math
        B, N, C = (8, 512, 768)
        H = 12
        DH = C // H
        M = 256
        LN_EPS = 1e-05

        def _phi(t, random_features):
            norm_sq = 0.5 * jnp.sum(t * t, axis=-1, keepdims=True)
            proj = jnp.einsum('bhnd,md->bhnm', t, random_features)
            return jnp.exp(proj - norm_sq) * (1.0 / math.sqrt(M))
        b, n, c = x.shape
        qkv = (x @ W_qkv).reshape(b, n, 3, H, DH)
        qkv = jnp.transpose(qkv, (2, 0, 3, 1, 4))
        q, k, v = (qkv[0], qkv[1], qkv[2])
        q_p = _phi(q, random_features)
        k_p = _phi(k, random_features)
        kv = jnp.einsum('bhnm,bhnd->bhmd', k_p, v)
        out = jnp.einsum('bhnm,bhmd->bhnd', q_p, kv)
        k_sum = jnp.sum(k_p, axis=2)
        normalizer = jnp.einsum('bhnm,bhm->bhn', q_p, k_sum)[..., None]
        out = out / (normalizer + 1e-06)
        x_attn = jnp.transpose(out, (0, 2, 1, 3)).reshape(b, n, c)
        x_attn = x_attn @ W_proj + b_proj
        y = x + x_attn
        mu = jnp.mean(y, axis=-1, keepdims=True)
        var = jnp.mean(jnp.square(y - mu), axis=-1, keepdims=True)
        return (y - mu) * jax.lax.rsqrt(var + LN_EPS) * gamma + beta

    def _L1_ffn_ref(x, w_in, g_in, w_out, g_out):
        import jax, jax.numpy as jnp
        import numpy as np
        EPS_NORM = 1e-06
        EPS_Q = 1e-05

        def rmsnorm(x, g):
            return x * jax.lax.rsqrt(jnp.mean(x * x, axis=-1, keepdims=True) + EPS_NORM) * g

        def activation_quant(x):
            scale = 127.0 / jnp.maximum(jnp.max(jnp.abs(x), axis=-1, keepdims=True), EPS_Q)
            return jnp.clip(jnp.round(x * scale), -128, 127) / scale

        def weight_quant(w):
            scale = 1.0 / jnp.maximum(jnp.mean(jnp.abs(w)), EPS_Q)
            return jnp.clip(jnp.round(w * scale), -1, 1) / scale

        def bitlinear(x, w, g):
            x_norm = rmsnorm(x, g)
            x_q = x_norm + jax.lax.stop_gradient(activation_quant(x_norm) - x_norm)
            w_q = w + jax.lax.stop_gradient(weight_quant(w) - w)
            return jnp.einsum('bsd,od->bso', x_q, w_q)
        h = bitlinear(x, w_in, g_in)
        up, gate = jnp.split(h, 2, axis=-1)
        y = jax.nn.silu(gate) * up
        return bitlinear(y, w_out, g_out)
    edge_index = jnp.stack([src, dst])
    xn = _layernorm(x, axis=-1)
    x = x + _L0_gnn_ref(xn, edge_index, L0_gnn_W1, L0_gnn_att_src1, L0_gnn_att_dst1, L0_gnn_b1, L0_gnn_W2, L0_gnn_att_src2, L0_gnn_att_dst2, L0_gnn_b2) + _L0_mix_ref(xn[None], L0_mix_ln1_g, L0_mix_ln1_b, L0_mix_qkv_w, L0_mix_qkv_b, L0_mix_w_orf, L0_mix_proj_w, L0_mix_proj_b, L0_mix_ln2_g, L0_mix_ln2_b, L0_mix_fc1_w, L0_mix_fc1_b, L0_mix_fc2_w, L0_mix_fc2_b)[0]
    x = x + _L0_ffn_ref(_layernorm(x, axis=-1)[None], L0_ffn_P, L0_ffn_C, L0_ffn_W1, L0_ffn_b1, L0_ffn_W2, L0_ffn_b2, L0_ffn_G1, L0_ffn_g1b, L0_ffn_G2, L0_ffn_g2b)[0]
    xn = _layernorm(x, axis=-1)
    x = x + _L1_gnn_ref(xn, edge_index, L1_gnn_W1, L1_gnn_a_src1, L1_gnn_a_dst1, L1_gnn_b1, L1_gnn_W2, L1_gnn_a_src2, L1_gnn_a_dst2, L1_gnn_b2) + _L1_mix_ref(xn[None], L1_mix_W_qkv, L1_mix_W_proj, L1_mix_b_proj, L1_mix_gamma, L1_mix_beta, L1_mix_random_features)[0]
    x = x + _L1_ffn_ref(_layernorm(x, axis=-1)[None], L1_ffn_w_in, L1_ffn_g_in, L1_ffn_w_out, L1_ffn_g_out)[0]
    return x

_drawn_inputs = setup_inputs


def setup_inputs(seed=0):
    import zlib

    import numpy as np

    out = dict(_drawn_inputs(seed))
    spreads = {'L0_gnn_b1': (0.0, 0.1),
     'L0_gnn_b2': (0.0, 0.1),
     'L0_mix_ln1_g': (1.0, 0.2),
     'L0_mix_ln1_b': (0.0, 0.1),
     'L0_mix_qkv_b': (0.0, 0.1),
     'L0_mix_proj_b': (0.0, 0.1),
     'L0_mix_ln2_g': (1.0, 0.2),
     'L0_mix_ln2_b': (0.0, 0.1),
     'L0_mix_fc1_b': (0.0, 0.1),
     'L0_mix_fc2_b': (0.0, 0.1),
     'L0_ffn_b1': (0.0, 0.1),
     'L0_ffn_b2': (0.0, 0.1),
     'L0_ffn_g1b': (0.0, 0.1),
     'L0_ffn_g2b': (0.0, 0.1),
     'L1_gnn_b1': (0.0, 0.1),
     'L1_gnn_b2': (0.0, 0.1),
     'L1_mix_b_proj': (0.0, 0.1),
     'L1_mix_gamma': (1.0, 0.2),
     'L1_mix_beta': (0.0, 0.1),
     'L1_ffn_g_in': (1.0, 0.2),
     'L1_ffn_g_out': (1.0, 0.2)}
    factors = {}
    for name, (base, spread) in spreads.items():
        noise = np.random.default_rng([zlib.crc32(name.encode()), seed]).standard_normal(out[name].shape)
        drawn = base * np.exp(spread * noise) if base else spread * noise
        out[name] = jnp.asarray(drawn.astype(out[name].dtype))
    for name, factor in factors.items():
        out[name] = (out[name] * factor).astype(out[name].dtype)
    return out
```

```python
from contextlib import ExitStack, contextmanager

import numpy as np

import concourse.bass as bass
from concourse import mybir

F32 = mybir.dt.float32
BF16 = mybir.dt.bfloat16
F16 = mybir.dt.float16
I32 = mybir.dt.int32
ACT = mybir.ActivationFunctionType
ALU = mybir.AluOpType
AX = mybir.AxisListType

N = 1250
E = 20000
D = 768
NT = 10
TP = N // NT
KB = D // 128
HEADS = 12
HD = D // HEADS
HP = HEADS // 2
CHUNKS = [(0, 512), (512, 512), (1024, N - 1024)]
EC = E // TP
XS = 4
EB = 16
NEG = -3.0e38
ES, ER, EM, EH = 8, 16, 64, 32
EJ = EM * EH // 128
NPART = [(0, 0), (1, 0), (0, 1), (1, 1), (2, 0), (0, 2)]
ZK = len(NPART) * ER + 3
EXTRA = 128


class Stage:

    def __init__(self, nc, name):
        self.nc, self.name, self.sems = nc, name, []

    def __enter__(self):
        self.ctx = ExitStack()
        return self

    def sb(self, name, shape, dt=F32):
        return self.ctx.enter_context(self.nc.sbuf_tensor(f"{self.name}_{name}", shape, dt))

    def ps(self, name, shape, dt=F32):
        return self.ctx.enter_context(self.nc.psum_tensor(f"{self.name}_{name}", shape, dt))

    def sem(self, name):
        s = self.nc.alloc_semaphore(f"{self.name}_{name}")
        self.sems.append(s)
        return s

    def __exit__(self, kind, *rest):
        if kind is None:
            self.nc.clear_and_free_semaphores(self.sems)
            self.nc.all_engine_barrier()
        self.ctx.close()


class Chain:

    def __init__(self, eng, sem, base=0):
        self.eng, self.sem, self.base, self.n = eng, sem, base, 0

    def done(self, ins):
        self.n += 1
        return ins.then_inc(self.sem, 1)

    def wait(self):
        self.eng.wait_ge(self.sem, self.base + self.n)


def row_bcast(ap1d, parts):
    n = ap1d.shape[0]
    return bass.AP(ap1d.tensor, ap1d.offset, [[0, parts], [1, n]])


def tokens(ap2d):
    return ap2d.rearrange("(t p) d -> p t d", p=TP)


def kblocks(ap2d):
    return ap2d.rearrange("(kb p) n -> p kb n", p=128)


def edge_stage(nc, ident, src, dst, lower, key_off, key_val, adj_d):
    with Stage(nc, "edge") as S:
        ends = S.sb("ends", [TP, 2, EC], I32)
        endf = S.sb("endf", [TP, 2, EC])
        key = S.sb("key", [TP, EC])
        low = S.sb("low", [TP, TP])
        ones = S.sb("ones", [TP, TP])
        diag = S.sb("diag", [TP, 2, EB, TP])
        eq = S.sb("eq", [TP, EB, TP], BF16)
        below = S.sb("below", [TP, EB, TP], BF16)
        lowb = S.sb("lowb", [TP, TP], BF16)
        cnt = S.sb("cnt", [TP, EC])
        rank = S.sb("rank", [TP, EC])
        first = S.sb("first", [TP, EC])
        spare = S.sb("spare", [TP, 1])
        offf = S.sb("offf", [TP, EC])
        zero = S.sb("zero", [TP, 6250])
        keys = S.ps("keys", [TP, 2, 4, 512])
        loaded, low_ld, chain = S.sem("loaded"), S.sem("low_ld"), S.sem("chain")
        diag_done, bc_done, cmp_done = S.sem("diag_done"), S.sem("bc_done"), S.sem("cmp_done")
        zeroed, cleared, spare_set = S.sem("zeroed"), S.sem("cleared"), S.sem("spare_set")
        steps = EC // EB
        with nc.Block() as block:
            @block.sync
            def _(sp):
                sp.dma_start(ends[:, 0, :], src.rearrange("(p c) -> p c", c=EC)).then_inc(loaded, 16)
                sp.dma_start(ends[:, 1, :], dst.rearrange("(p c) -> p c", c=EC)).then_inc(loaded, 16)
                sp.dma_start(low[:], lower[0:TP, 0:TP]).then_inc(low_ld, 16)
                sp.wait_ge(zeroed, 1)
                for half in range(2):
                    sp.dma_start(adj_d[half * TP * 6250:(half + 1) * TP * 6250].rearrange("(p n) -> p n", p=TP),
                                 zero[:]).then_inc(cleared, 16)
                sp.dma_start(adj_d[N * N:N * N + EXTRA].rearrange("(a n) -> a n", a=1),
                             zero[0:1, 0:EXTRA]).then_inc(cleared, 16)
                sp.wait_ge(cleared, 48)

            @block.gpsimd
            def _(pool):
                nc.gpsimd.memset(zero[:], 0.0).then_inc(zeroed, 1)
                nc.gpsimd.iota(key_off[:, 0:1], [[0, 1]], base=N * N, channel_multiplier=1).then_inc(spare_set, 1)

            @block.tensor
            def _(pe):
                pe.wait_ge(low_ld, 16)
                for i in range(steps):
                    pe.wait_ge(diag_done, i + 1)
                    if i >= 2:
                        pe.wait_ge(cmp_done, i - 1)
                    for b in range(4):
                        ins = pe.matmul(keys[:, i % 2, b, 0:4 * TP], ones[:, :],
                                        diag[:, i % 2, 4 * b:4 * b + 4, :], start=True, stop=True)
                    ins.then_inc(bc_done, 1)

            @block.vector
            def _(dve):
                steps_done = Chain(dve, chain)
                steps_done.done(dve.memset(ones[:], 1.0))
                dve.wait_ge(loaded, 32)
                steps_done.done(dve.tensor_copy(endf[:], ends[:]))
                steps_done.wait()
                steps_done.done(dve.scalar_tensor_tensor(out=key[:], in0=endf[:, 0, :], scalar=float(N),
                                                         in1=endf[:, 1, :], op0=ALU.mult, op1=ALU.add))
                dve.wait_ge(low_ld, 16)
                steps_done.done(dve.tensor_copy(lowb[:], low[:]))
                steps_done.wait()

                def set_diag(i):
                    if i >= 2:
                        dve.wait_ge(bc_done, i - 1)
                    dve.tensor_tensor(diag[:, i % 2], ident[0:TP, 0:TP].unsqueeze(1).to_broadcast([TP, EB, TP]),
                                      key[:, i * EB:(i + 1) * EB].unsqueeze(2).to_broadcast([TP, EB, TP]),
                                      ALU.mult).then_inc(diag_done, 1)

                set_diag(0)
                for i in range(steps):
                    cols = slice(i * EB, (i + 1) * EB)
                    if i + 1 < steps:
                        set_diag(i + 1)
                    dve.wait_ge(bc_done, i + 1)
                    for b in range(4):
                        ins = steps_done.done(dve.tensor_tensor(
                            eq[:, 4 * b:4 * b + 4, :], keys[:, i % 2, b, 0:4 * TP].rearrange("p (c e) -> p c e", c=4),
                            key[:, i * EB + 4 * b:i * EB + 4 * b + 4].unsqueeze(2).to_broadcast([TP, 4, TP]),
                            ALU.is_equal))
                    steps_done.wait()
                    dve.tensor_tensor(below[:], eq[:], lowb[:].unsqueeze(1).to_broadcast([TP, EB, TP]),
                                      ALU.mult).then_inc(cmp_done, 1)
                    steps_done.done(dve.tensor_reduce(cnt[:, cols], eq[:], AX.X, ALU.add))
                    dve.wait_ge(cmp_done, i + 1)
                    steps_done.done(dve.tensor_reduce(rank[:, cols], below[:], AX.X, ALU.add))
                    steps_done.wait()
                dve.wait_ge(spare_set, 1)
                steps_done.done(dve.tensor_copy(spare[:], key_off[:, 0:1]))
                steps_done.done(dve.tensor_scalar(first[:], rank[:], 0.0, None, ALU.is_equal))
                steps_done.wait()
                steps_done.done(dve.tensor_scalar(offf[:], key[:], spare[:, 0:1], None, ALU.subtract))
                steps_done.done(dve.tensor_tensor(key_val[:], cnt[:], first[:], ALU.mult))
                steps_done.wait()
                steps_done.done(dve.tensor_tensor(offf[:], offf[:], first[:], ALU.mult))
                steps_done.wait()
                steps_done.done(dve.tensor_scalar(key_off[:], offf[:], spare[:, 0:1], None, ALU.add))


def add_edges(nc, pool, key_off, key_val, added, adj_flat):
    for c in range(EC):
        if c:
            pool.wait_ge(added, c * 16)
        nc.gpsimd.indirect_dma_start(
            out=adj_flat, out_offset=bass.IndirectOffsetOnAxis(ap=key_off[:, c:c + 1], axis=0),
            in_=key_val[:, c:c + 1], in_offset=None, compute_op=ALU.add).then_inc(added, 16)
    pool.wait_ge(added, EC * 16)


def norm_stage(nc, name, ident, eps, x_d, add_d, bias_d, sum_d, normed_d, gain_cols, shift_cols, yT):
    second = gain_cols is not None
    with Stage(nc, name) as S:
        x = S.sb("x", [TP, NT, D])
        add = S.sb("add", [TP, NT, D]) if add_d is not None else None
        bias = S.sb("bias", [TP, D])
        cols = S.sb("cols", [128, 2, KB])
        stats = S.sb("stats", [TP, NT, 2, 6])
        mv = S.sb("mv", [TP, 2, NT, 2])
        std = S.sb("std", [TP, 2, NT])
        rstd = S.sb("rstd", [TP, 2, NT])
        epst = S.sb("epst", [TP, 1])
        tps = S.ps("tps", [128, 2, 1024])
        x_ld, add_ld, cols_ld = [S.sem("x_ld0"), S.sem("x_ld1")], S.sem("add_ld"), S.sem("cols_ld")
        chain, var_ready, std_ready = S.sem("chain"), S.sem("var_ready"), S.sem("std_ready")
        sum_ready, normed, final = S.sem("sum_ready"), S.sem("normed"), S.sem("final")
        turned, kept, stored = S.sem("turned"), S.sem("kept"), S.sem("stored")
        half = NT // 2
        with nc.Block() as block:
            @block.sync
            def _(sp):
                n_stored = 0
                for h in range(2):
                    rows = slice(h * half, (h + 1) * half)
                    sp.dma_start(x[:, rows, :], tokens(x_d)[:, rows, :]).then_inc(x_ld[h], 16)
                if add_d is not None:
                    sp.dma_start(add[:], tokens(add_d)).then_inc(add_ld, 16)
                    sp.dma_start(bias[:], row_bcast(bias_d, TP)).then_inc(add_ld, 16)
                if second:
                    sp.dma_start(cols[:, 0, :], gain_cols).then_inc(cols_ld, 16)
                    sp.dma_start(cols[:, 1, :], shift_cols).then_inc(cols_ld, 16)
                if sum_d is not None:
                    sp.wait_ge(sum_ready, NT)
                    sp.dma_start(tokens(sum_d), add[:]).then_inc(stored, 16)
                    n_stored += 1
                if normed_d is not None:
                    sp.wait_ge(normed, NT)
                    sp.dma_start(tokens(normed_d), x[:]).then_inc(stored, 16)
                    n_stored += 1
                if n_stored:
                    sp.wait_ge(stored, 16 * n_stored)

            @block.vector
            def _(dve):
                steps_done = Chain(dve, chain)
                steps_done.done(dve.memset(epst[:], eps))
                if add_d is not None:
                    dve.wait_ge(add_ld, 32)
                for t in range(NT):
                    if t % half == 0:
                        dve.wait_ge(x_ld[t // half], 16)
                    if add_d is not None:
                        steps_done.done(dve.tensor_tensor(add[:, t, :], add[:, t, :], bias[:], ALU.add))
                        steps_done.wait()
                        steps_done.done(dve.tensor_tensor(add[:, t, :], add[:, t, :], x[:, t, :], ALU.add))
                        steps_done.wait()
                        dve.tensor_copy(x[:, t, :], add[:, t, :]).then_inc(sum_ready, 1)
                        dve.wait_ge(sum_ready, t + 1)
                    for k in range(2):
                        steps_done.done(dve.bn_stats(stats[:, t, k, :], x[:, t, k * 384:(k + 1) * 384]))
                    steps_done.wait()
                    dve.bn_aggr(mv[:, 0, t, :], stats[:, t, :, :]).then_inc(var_ready, 1)

                def normalise(r, signal):
                    dve.wait_ge(std_ready, r + 1)
                    steps_done.done(dve.reciprocal(rstd[:, r, :], std[:, r, :]))
                    steps_done.wait()
                    dve.wait_ge(var_ready, (r + 1) * NT)
                    for t in range(NT):
                        ins = dve.tensor_scalar(x[:, t, :], x[:, t, :], mv[:, r, t, 0:1], rstd[:, r, t:t + 1],
                                                ALU.subtract, ALU.mult)
                        ins.then_inc(signal, 1)

                if second:
                    normalise(0, normed)
                    for t in range(NT):
                        dve.wait_ge(normed, t + 1)
                        for k in range(2):
                            steps_done.done(dve.bn_stats(stats[:, t, k, :], x[:, t, k * 384:(k + 1) * 384]))
                        steps_done.wait()
                        dve.bn_aggr(mv[:, 1, t, :], stats[:, t, :, :]).then_inc(var_ready, 1)
                    if normed_d is not None:
                        dve.wait_ge(stored, 16)
                    normalise(1, final)
                else:
                    normalise(0, normed)

            @block.scalar
            def _(act):
                for r in range(2 if second else 1):
                    act.wait_ge(chain, 1)
                    act.wait_ge(var_ready, (r + 1) * NT)
                    act.activation(std[:, r, :], mv[:, r, :, 1], ACT.Sqrt, bias=epst[:, 0:1]).then_inc(std_ready, 1)
                if second:
                    act.wait_ge(cols_ld, 32)
                for t in range(NT):
                    act.wait_ge(turned, t + 1)
                    tile = yT[:, :, t * TP:(t + 1) * TP]
                    if second:
                        for kb in range(KB):
                            ins = act.activation(tile[:, kb, :], tps[:, t % 2, kb * 128:kb * 128 + TP], ACT.Identity,
                                                 scale=cols[:, 0, kb:kb + 1], bias=cols[:, 1, kb:kb + 1])
                    else:
                        ins = act.copy(tile, tps[:, t % 2, 0:KB * 128].rearrange("p (kb n) -> p kb n", kb=KB)[:, :, 0:TP])
                    ins.then_inc(kept, 1)

            @block.tensor
            def _(pe):
                for t in range(NT):
                    pe.wait_ge(final if second else normed, t + 1)
                    if t >= 2:
                        pe.wait_ge(kept, t - 1)
                    for kb in range(KB):
                        ins = pe.transpose(tps[:, t % 2, kb * 128:kb * 128 + TP], x[:, t, kb * 128:(kb + 1) * 128],
                                           ident[0:TP, 0:TP])
                    ins.then_inc(turned, 1)


def performer_stage(nc, name, yT, w_d, bias_cols, vbias_d, feat_d, per_head, m, scale, eps, out_d, edges=None):
    mb_n = m // 128
    n_phi = NT + 3 * mb_n
    vw = HD + 1
    with Stage(nc, name) as S:
        w = S.sb("w", [128, 2, 3, KB, 128])
        feat = S.sb("feat", [128, 2, 2, m])
        qs = S.sb("qs", [128, 2, N])
        ks = S.sb("ks", [128, 2, N])
        v = S.sb("v", [TP, NT, 2, vw])
        kphi = S.sb("kphi", [TP, 2, NT, m])
        qphi = S.sb("qphi", [128, 2, mb_n, N])
        ktv = S.sb("ktv", [128, 2, mb_n, vw])
        den = S.sb("den", [TP, NT])
        rden = S.sb("rden", [TP, NT])
        o = S.sb("o", [TP, 2, NT, 128])
        bcols = S.sb("bcols", [128, 12])
        vbias = S.sb("vbias", [TP, D])
        lnm = S.sb("lnm", [128, 1])
        proj = S.ps("proj", [128, 1536])
        phi = S.ps("phi", [128, 2, 512])
        ktv_ps = S.ps("ktv_ps", [128, 512])
        o_ps = S.ps("o_ps", [128, 2, 512])
        w_ld = [S.sem("w_ld0"), S.sem("w_ld1")]
        o_st = [S.sem("o_st0"), S.sem("o_st1")]
        bias_ld, const_set = S.sem("bias_ld"), S.sem("const_set")
        proj_done, plain_done, square_done, v_done = (S.sem(s) for s in (
            "proj_done", "plain_done", "square_done", "v_done"))
        phi_done, exp_done, ktv_done, ktv_kept, o_done, o_kept, chain = (S.sem(s) for s in (
            "phi_done", "exp_done", "ktv_done", "ktv_kept", "o_done", "o_kept", "chain"))
        added = S.sem("added")
        o_tiles = [(0, 0, 7), (1, 7, 3)]
        biased = bias_cols is not None

        with nc.Block() as block:
            if edges is not None:
                @block.gpsimd
                def _(pool):
                    add_edges(nc, pool, edges[0], edges[1], added, edges[2])

            @block.sync
            def _(sp):
                for u in range(2):
                    sp.nop().then_inc(o_st[u], 16)
                if biased:
                    sp.dma_start(bcols[:], bias_cols).then_inc(bias_ld, 16)
                    sp.dma_start(vbias[:], row_bcast(vbias_d, TP)).then_inc(bias_ld, 16)

                def load(g, u):
                    for k in range(3):
                        sp.dma_start(w[:, u, k], kblocks(w_d)[:, :, bass.ds(g * 128 + k * D, 128)]).then_inc(w_ld[u], 16)
                    for x in range(2):
                        f = feat_d[bass.ds(g * 2 + x, 1), :, :].rearrange("a c m -> (a c) m") if per_head else feat_d
                        sp.dma_start(feat[64 * x:64 * x + 64, u, x, :], f).then_inc(w_ld[u], 16)

                def store(g, u):
                    sp.dma_start(tokens(out_d)[:, :, bass.ds(g * 128, 128)], o[:, u]).then_inc(o_st[u], 16)

                load(0, 0)
                load(1, 1)
                with sp.Fori(0, HP // 2 - 1) as i:
                    for u in range(2):
                        sp.wait_ge(o_done, (i * 2 + u) * 2 + 1)
                        load(i * 2 + u + 2, u)
                        sp.wait_ge(o_kept, (i * 2 + u + 1) * 4 + 1)
                        store(i * 2 + u, u)
                for u in range(2):
                    sp.wait_ge(o_kept, (HP - 1 + u) * 4 + 1)
                    store(HP - 2 + u, u)
                for u in range(2):
                    sp.wait_ge(o_st[u], 16 * (HP // 2) + 16)

            @block.tensor
            def _(pe):
                pe.wait_ge(const_set, 6)
                with pe.Fori(0, HP // 2) as i:
                    for u in range(2):
                        g = i * 2 + u
                        pe.wait_ge(w_ld[u], i * 80 + 80)
                        for k in range(2):
                            for c, (c0, cn) in enumerate(CHUNKS):
                                if k == 0:
                                    pe.wait_ge(v_done, g * 6 + 1)
                                else:
                                    pe.wait_ge(plain_done, g * 12 + 2 * c + 2)
                                for kb in range(KB):
                                    ins = pe.matmul(proj[:, c0:c0 + cn], w[:, u, k, kb, :], yT[:, kb, c0:c0 + cn],
                                                    start=(kb == 0), stop=(kb == KB - 1))
                                ins.then_inc(proj_done, 1)
                        for t in range(NT):
                            if t % 4 == 0:
                                pe.wait_ge(plain_done, g * 12 + 8 + 2 * (t // 4))
                            for kb in range(KB):
                                ins = pe.matmul(proj[0:TP, t * 128:(t + 1) * 128], yT[:, kb, t * TP:(t + 1) * TP],
                                                w[:, u, 2, kb, :], start=(kb == 0), stop=(kb == KB - 1))
                            if t in (3, 7, 9):
                                ins.then_inc(proj_done, 1)

                        def features(j, out, lhsT, rhs):
                            pe.wait_ge(exp_done, g * (2 * n_phi) + max(j, 1))
                            pe.matmul(out, lhsT, rhs, start=True, stop=True).then_inc(phi_done, 1)

                        def k_features(x):
                            for t in range(NT):
                                j = x * n_phi + t
                                features(j, phi[0:TP, j % 2, 0:m], ks[:, x, t * TP:(t + 1) * TP], feat[:, u, x, :])

                        def q_features(x):
                            j = x * n_phi + NT
                            for mb in range(mb_n):
                                for c0, cn in CHUNKS:
                                    features(j, phi[:, j % 2, 0:cn], feat[:, u, x, mb * 128:(mb + 1) * 128],
                                             qs[:, x, c0:c0 + cn])
                                    j += 1

                        def k_t_v(x):
                            pe.wait_ge(exp_done, g * (2 * n_phi) + x * n_phi + NT + 1)
                            pe.wait_ge(v_done, g * 6 + 7)
                            pe.wait_ge(ktv_kept, g * 2 + x + 1)
                            for mb in range(mb_n):
                                for t in range(NT):
                                    ins = pe.matmul(ktv_ps[:, mb * vw:(mb + 1) * vw],
                                                    kphi[:, x, t, mb * 128:(mb + 1) * 128], v[:, t, x, :],
                                                    start=(t == 0), stop=(t == NT - 1))
                            ins.then_inc(ktv_done, 1)

                        def outputs(x):
                            pe.wait_ge(exp_done, g * (2 * n_phi) + (x + 1) * n_phi + 1)
                            pe.wait_ge(ktv_kept, g * 2 + x + 2)
                            pe.wait_ge(o_kept, g * 4 + 2 * x + 1)
                            for bank, t0, tn in o_tiles:
                                for t in range(t0, t0 + tn):
                                    for mb in range(mb_n):
                                        ins = pe.matmul(o_ps[0:TP, bank, (t - t0) * vw:(t - t0 + 1) * vw],
                                                        qphi[:, x, mb, t * TP:(t + 1) * TP], ktv[:, x, mb, :],
                                                        start=(mb == 0), stop=(mb == mb_n - 1))
                            return ins

                        pe.wait_ge(plain_done, g * 12 + 12)
                        pe.wait_ge(square_done, g * 4 + 4)
                        k_features(0)
                        q_features(0)
                        k_features(1)
                        k_t_v(0)
                        q_features(1)
                        outputs(0).then_inc(o_done, 1)
                        k_t_v(1)
                        outputs(1).then_inc(o_done, 1)

            @block.scalar
            def _(act):
                act.wait_ge(const_set, 6)
                act.nop().then_inc(exp_done, 1)
                with act.Fori(0, HP // 2) as i:
                    for u in range(2):
                        g = i * 2 + u
                        for k, dest in enumerate((qs, ks)):
                            for x in range(2):
                                rows, other = slice(64 * x, 64 * x + 64), slice(64 - 64 * x, 128 - 64 * x)
                                act.wait_ge(plain_done, g * 12 + k * 6 + 6)
                                act.activation(dest[other, x, :], dest[rows, x, :], ACT.Square).then_inc(square_done, 1)

                        def exps(j, out, in_, parts):
                            act.wait_ge(phi_done, g * (2 * n_phi) + j + 1)
                            act.activation(out, in_, ACT.Exp, bias=lnm[0:parts, 0:1], scale=scale).then_inc(exp_done, 1)

                        def k_exps(x):
                            for t in range(NT):
                                j = x * n_phi + t
                                exps(j, kphi[:, x, t, :], phi[0:TP, j % 2, 0:m], TP)

                        def q_exps(x):
                            j = x * n_phi + NT
                            for mb in range(mb_n):
                                for c0, cn in CHUNKS:
                                    exps(j, qphi[:, x, mb, c0:c0 + cn], phi[:, j % 2, 0:cn], 128)
                                    j += 1

                        k_exps(0)
                        q_exps(0)
                        k_exps(1)
                        q_exps(1)

            @block.vector
            def _(dve):
                for s in (v_done, ktv_kept, o_kept):
                    dve.nop().then_inc(s, 1)
                for u in range(2):
                    dve.memset(feat[64:128, u, 0, :], -0.5 * scale).then_inc(const_set, 1)
                    dve.memset(feat[0:64, u, 1, :], -0.5 * scale).then_inc(const_set, 1)
                dve.memset(lnm[:], -0.5 * float(np.log(m))).then_inc(const_set, 1)
                dve.memset(v[:, :, :, HD:vw], 1.0).then_inc(const_set, 1)
                if biased:
                    dve.wait_ge(bias_ld, 32)
                with dve.Fori(0, HP // 2) as i:
                    for u in range(2):
                        g = i * 2 + u
                        steps_done = Chain(dve, chain, g * 6)
                        for k, dest in enumerate((qs, ks)):
                            for c, (c0, cn) in enumerate(CHUNKS):
                                dve.wait_ge(proj_done, g * 9 + k * 3 + c + 1)
                                for x in range(2):
                                    rows = slice(64 * x, 64 * x + 64)
                                    if biased:
                                        ins = dve.tensor_scalar(dest[rows, x, c0:c0 + cn], proj[rows, c0:c0 + cn],
                                                                bcols[rows, bass.ds(g + k * KB, 1)], None, ALU.add)
                                    else:
                                        ins = dve.tensor_copy(dest[rows, x, c0:c0 + cn], proj[rows, c0:c0 + cn])
                                    ins.then_inc(plain_done, 1)
                        for c, (t0, tn) in enumerate(((0, 4), (4, 4), (8, 2))):
                            dve.wait_ge(proj_done, g * 9 + 7 + c)
                            got = proj[0:TP, t0 * 128:(t0 + tn) * 128].rearrange("p (t x c) -> p t x c", t=tn, x=2)
                            for x in range(2):
                                if biased:
                                    vb = vbias[:, bass.ds(g * 128 + x * HD, HD)]
                                    ins = dve.tensor_tensor(v[:, t0:t0 + tn, x, 0:HD], got[:, :, x, :],
                                                            vb.unsqueeze(1).to_broadcast([TP, tn, HD]), ALU.add)
                                else:
                                    ins = dve.tensor_copy(v[:, t0:t0 + tn, x, 0:HD], got[:, :, x, :])
                                ins.then_inc(v_done, 1)

                        def keep_ktv(x):
                            dve.wait_ge(ktv_done, g * 2 + x + 1)
                            dve.tensor_copy(ktv[:, x], ktv_ps[:, 0:mb_n * vw].rearrange("p (a b) -> p a b", a=mb_n)
                                            ).then_inc(ktv_kept, 1)

                        def keep_out(x):
                            dve.wait_ge(o_done, g * 2 + x + 1)
                            if x == 0:
                                dve.wait_ge(o_st[u], i * 16 + 16)
                            got = [o_ps[0:TP, b, 0:tn * vw].rearrange("p (t w) -> p t w", t=tn) for b, _, tn in o_tiles]
                            for (_, t0, tn), a in zip(o_tiles, got):
                                steps_done.done(dve.tensor_scalar(den[:, t0:t0 + tn], a[:, :, HD], eps, None, ALU.add))
                            steps_done.wait()
                            steps_done.done(dve.reciprocal(rden[:], den[:]))
                            steps_done.wait()
                            for (_, t0, tn), a in zip(o_tiles, got):
                                dve.tensor_tensor(o[:, u, t0:t0 + tn, x * HD:(x + 1) * HD], a[:, :, 0:HD],
                                                  rden[:, t0:t0 + tn].unsqueeze(2).to_broadcast([TP, tn, HD]),
                                                  ALU.mult).then_inc(o_kept, 1)

                        keep_ktv(0)
                        keep_out(0)
                        keep_ktv(1)
                        keep_out(1)


def proj_stage(nc, name, ident, attn_d, w_d, bias_d, xn_d, x_d, sum_d, eps, gain, shift, yT):
    turn = yT is not None
    with Stage(nc, name) as S:
        a = S.sb("a", [TP, NT, D])
        h = S.sb("h", [TP, NT, D])
        x = S.sb("x", [TP, NT, D])
        w = S.sb("w", [128, KB, D])
        aT = S.sb("aT", [128, 2, KB, TP])
        bias = S.sb("bias", [TP, D])
        rows = S.sb("rows", [128, 2, KB if turn else D])
        stats = S.sb("stats", [TP, NT, 2, 6])
        mv = S.sb("mv", [TP, NT, 2])
        std = S.sb("std", [TP, NT])
        rstd = S.sb("rstd", [TP, NT])
        epst = S.sb("epst", [TP, 1])
        tps = S.ps("tps", [128, 2, 1024])
        hps = S.ps("hps", [128, 2, 1024])
        a_ld, w_ld, xn_ld, x_ld = S.sem("a_ld"), S.sem("w_ld"), S.sem("xn_ld"), S.sem("x_ld")
        rows_ld, chain = S.sem("rows_ld"), S.sem("chain")
        turned, kept, h_done, h_read, var_ready, std_ready = (S.sem(s) for s in (
            "turned", "kept", "h_done", "h_read", "var_ready", "std_ready"))
        normed, sum_ready, stored = S.sem("normed"), S.sem("sum_ready"), S.sem("stored")
        with nc.Block() as block:
            @block.sync
            def _(sp):
                sp.dma_start(a[:], tokens(attn_d)).then_inc(a_ld, 16)
                sp.dma_start(w[:], kblocks(w_d)).then_inc(w_ld, 16)
                sp.dma_start(h[:], tokens(xn_d)).then_inc(xn_ld, 16)
                sp.dma_start(bias[:], row_bcast(bias_d, TP)).then_inc(xn_ld, 16)
                sp.dma_start(x[:], tokens(x_d)).then_inc(x_ld, 16)
                for k, r in enumerate((gain, shift)):
                    if turn:
                        sp.dma_start(rows[:, k, :], r).then_inc(rows_ld, 16)
                    else:
                        sp.dma_start(rows[0:TP, k, :], row_bcast(r, TP)).then_inc(rows_ld, 16)
                sp.wait_ge(sum_ready, NT)
                sp.dma_start(tokens(sum_d), x[:]).then_inc(stored, 16)
                sp.wait_ge(stored, 16)

            @block.tensor
            def _(pe):
                pe.wait_ge(a_ld, 16)

                def turn_tile(t):
                    if t >= 2:
                        pe.wait_ge(kept, t - 1)
                    for kb in range(KB):
                        ins = pe.transpose(tps[:, t % 2, kb * 128:kb * 128 + TP], a[:, t % NT, kb * 128:(kb + 1) * 128],
                                           ident[0:TP, 0:TP])
                    ins.then_inc(turned, 1)

                turn_tile(0)
                pe.wait_ge(w_ld, 16)
                for t in range(NT):
                    if t + 1 < NT:
                        turn_tile(t + 1)
                    pe.wait_ge(kept, t + 1)
                    if t >= 2:
                        pe.wait_ge(h_read, t - 1)
                    for c in range(2):
                        for kb in range(KB):
                            ins = pe.matmul(hps[0:TP, t % 2, c * 512:c * 512 + 384], aT[:, t % 2, kb, :],
                                            w[:, kb, c * 384:(c + 1) * 384], start=(kb == 0), stop=(kb == KB - 1))
                    ins.then_inc(h_done, 1)
                if turn:
                    for t in range(NT):
                        pe.wait_ge(normed, t + 1)
                        turn_tile(NT + t)

            @block.scalar
            def _(act):
                for t in range(NT):
                    act.wait_ge(turned, t + 1)
                    if t >= 2:
                        act.wait_ge(h_done, t - 1)
                    act.copy(aT[:, t % 2], tps[:, t % 2, 0:KB * 128].rearrange("p (kb n) -> p kb n", kb=KB)[:, :, 0:TP]
                             ).then_inc(kept, 1)
                act.wait_ge(chain, 1)
                act.wait_ge(var_ready, NT)
                act.activation(std[:], mv[:, :, 1], ACT.Sqrt, bias=epst[:, 0:1]).then_inc(std_ready, 1)
                if turn:
                    act.wait_ge(rows_ld, 32)
                    for t in range(NT):
                        act.wait_ge(turned, NT + t + 1)
                        for kb in range(KB):
                            ins = act.activation(yT[:, kb, t * TP:(t + 1) * TP],
                                                 tps[:, t % 2, kb * 128:kb * 128 + TP], ACT.Identity,
                                                 scale=rows[:, 0, kb:kb + 1], bias=rows[:, 1, kb:kb + 1])
                        ins.then_inc(kept, 1)

            @block.vector
            def _(dve):
                steps_done = Chain(dve, chain)
                steps_done.done(dve.memset(epst[:], eps))
                dve.wait_ge(xn_ld, 32)
                dve.wait_ge(x_ld, 16)
                for t in range(NT):
                    steps_done.done(dve.tensor_tensor(h[:, t, :], h[:, t, :], bias[:], ALU.add))
                    dve.wait_ge(h_done, t + 1)
                    steps_done.wait()
                    both = h[:, t, :].rearrange("p (c n) -> p c n", c=2)
                    got = hps[0:TP, t % 2, :].rearrange("p (c n) -> p c n", c=2)[:, :, 0:384]
                    dve.tensor_tensor(both, both, got, ALU.add).then_inc(h_read, 1)
                    dve.wait_ge(h_read, t + 1)
                    for k in range(2):
                        steps_done.done(dve.bn_stats(stats[:, t, k, :], h[:, t, k * 384:(k + 1) * 384]))
                    if turn:
                        dve.tensor_tensor(x[:, t, :], x[:, t, :], h[:, t, :], ALU.add).then_inc(sum_ready, 1)
                    steps_done.wait()
                    dve.bn_aggr(mv[:, t, :], stats[:, t, :, :]).then_inc(var_ready, 1)
                dve.wait_ge(std_ready, 1)
                steps_done.done(dve.reciprocal(rstd[:], std[:]))
                steps_done.wait()
                dve.wait_ge(var_ready, NT)
                if not turn:
                    dve.wait_ge(rows_ld, 32)
                for t in range(NT):
                    dst = a[:, t, :] if turn else h[:, t, :]
                    dve.tensor_scalar(dst, h[:, t, :], mv[:, t, 0:1], rstd[:, t:t + 1],
                                      ALU.subtract, ALU.mult).then_inc(normed, 1)
                    if not turn:
                        dve.wait_ge(normed, t + 1)
                        steps_done.done(dve.tensor_tensor(h[:, t, :], h[:, t, :], rows[0:TP, 0, :], ALU.mult))
                        steps_done.done(dve.tensor_tensor(x[:, t, :], x[:, t, :], rows[0:TP, 1, :], ALU.add))
                        steps_done.wait()
                        dve.tensor_tensor(x[:, t, :], x[:, t, :], h[:, t, :], ALU.add).then_inc(sum_ready, 1)


def dense_stage(nc, name, xT, kb_n, w_d, ob_n, bias_cols, func, outT):
    with Stage(nc, name) as S:
        w = S.sb("w", [128, 2, kb_n, 128])
        bias = S.sb("bias", [128, ob_n])
        ps = S.ps("ps", [128, 2, 1536])
        w_ld = [S.sem("w_ld0"), S.sem("w_ld1")]
        bias_ld, done, kept = S.sem("bias_ld"), S.sem("done"), S.sem("kept")
        with nc.Block() as block:
            @block.sync
            def _(sp):
                sp.dma_start(bias[:], bias_cols).then_inc(bias_ld, 16)

                def load(g, u):
                    sp.dma_start(w[:, u], kblocks(w_d)[:, :, bass.ds(g * 128, 128)]).then_inc(w_ld[u], 16)

                load(0, 0)
                load(1, 1)
                if ob_n > 2:
                    with sp.Fori(0, ob_n // 2 - 1) as i:
                        for u in range(2):
                            sp.wait_ge(done, i * 2 + u + 1)
                            load(i * 2 + u + 2, u)

            @block.tensor
            def _(pe):
                with pe.Fori(0, ob_n // 2) as i:
                    for u in range(2):
                        pe.wait_ge(w_ld[u], i * 16 + 16)
                        pe.wait_ge(kept, i * 2 + u + 1)
                        for c0, cn in CHUNKS:
                            for kb in range(kb_n):
                                ins = pe.matmul(ps[:, u, c0:c0 + cn], w[:, u, kb, :], xT[:, kb, c0:c0 + cn],
                                                start=(kb == 0), stop=(kb == kb_n - 1))
                        ins.then_inc(done, 1)

            @block.scalar
            def _(act):
                act.wait_ge(bias_ld, 16)
                act.nop().then_inc(kept, 2)
                with act.Fori(0, ob_n // 2) as i:
                    for u in range(2):
                        act.wait_ge(done, i * 2 + u + 1)
                        act.activation(outT[:, bass.ds(i * 2 + u, 1), :], ps[:, u:u + 1, 0:N], func,
                                       bias=bias[:, bass.ds(i * 2 + u, 1)]).then_inc(kept, 1)


def dense_add_stage(nc, name, ident, xT, kb_n, w_d, bias_cols, sum_d, out_d):
    ob_n = KB
    with Stage(nc, name) as S:
        w = S.sb("w", [128, 2, kb_n, 128])
        bias = S.sb("bias", [128, ob_n])
        y = S.sb("y", [128, 2, N])
        acc = S.sb("acc", [TP, 2, NT, 128])
        ps = S.ps("ps", [128, 1536])
        tps = S.ps("tps", [128, 1536])
        w_ld, acc_ld = [S.sem("w_ld0"), S.sem("w_ld1")], [S.sem("acc_ld0"), S.sem("acc_ld1")]
        stored = [S.sem("stored0"), S.sem("stored1")]
        bias_ld, done, kept, turned, summed = (S.sem(s) for s in ("bias_ld", "done", "kept", "turned", "summed"))
        with nc.Block() as block:
            @block.sync
            def _(sp):
                sp.dma_start(bias[:], bias_cols).then_inc(bias_ld, 16)
                for g in range(ob_n + 2):
                    u = g % 2
                    cols = slice(g * 128, (g + 1) * 128)
                    if g >= 2:
                        old = slice((g - 2) * 128, (g - 1) * 128)
                        sp.wait_ge(summed, g - 1)
                        sp.dma_start(tokens(out_d)[:, :, old], acc[:, u]).then_inc(stored[u], 16)
                    if g < ob_n:
                        sp.dma_start(w[:, u], kblocks(w_d)[:, :, cols]).then_inc(w_ld[u], 16)
                        if g >= 2:
                            sp.wait_ge(stored[u], 16 * (g // 2))
                        sp.dma_start(acc[:, u], tokens(sum_d)[:, :, cols]).then_inc(acc_ld[u], 16)
                for u in range(2):
                    sp.wait_ge(stored[u], 16 * (ob_n // 2))

            @block.tensor
            def _(pe):
                def turn_back(g):
                    pe.wait_ge(kept, 3 * (g + 1))
                    if g:
                        pe.wait_ge(summed, g)
                    for t in range(NT):
                        ins = pe.transpose(tps[0:TP, t * 128:(t + 1) * 128], y[:, g % 2, t * TP:(t + 1) * TP], ident[:])
                    ins.then_inc(turned, 1)

                for g in range(ob_n):
                    pe.wait_ge(w_ld[g % 2], 16 * (g // 2 + 1))
                    for c, (c0, cn) in enumerate(CHUNKS):
                        if g:
                            pe.wait_ge(kept, 3 * (g - 1) + c + 1)
                        for kb in range(kb_n):
                            ins = pe.matmul(ps[:, c0:c0 + cn], w[:, g % 2, kb, :], xT[:, kb, c0:c0 + cn],
                                            start=(kb == 0), stop=(kb == kb_n - 1))
                        ins.then_inc(done, 1)
                    if g:
                        turn_back(g - 1)
                turn_back(ob_n - 1)

            @block.scalar
            def _(act):
                act.wait_ge(bias_ld, 16)
                for g in range(ob_n):
                    for c, (c0, cn) in enumerate(CHUNKS):
                        act.wait_ge(done, 3 * g + c + 1)
                        if g >= 2:
                            act.wait_ge(turned, g - 1)
                        act.activation(y[:, g % 2, c0:c0 + cn], ps[:, c0:c0 + cn], ACT.Identity,
                                       bias=bias[:, g:g + 1]).then_inc(kept, 1)

            @block.vector
            def _(dve):
                for g in range(ob_n):
                    dve.wait_ge(turned, g + 1)
                    dve.wait_ge(acc_ld[g % 2], 16 * (g // 2 + 1))
                    dve.tensor_tensor(acc[:, g % 2], acc[:, g % 2],
                                      tps[0:TP, 0:NT * 128].rearrange("p (t n) -> p t n", t=NT), ALU.add).then_inc(summed, 1)


def mask_stage(nc, ident, adj_d, mask_d):
    with Stage(nc, "mask") as S:
        adj = S.sb("adj", [TP, NT, N])
        mask = S.sb("mask", [TP, NT, N], BF16)
        tps = S.ps("tps", [128, 2, 2048])
        adj_ld, turned, kept, stored = S.sem("adj_ld"), S.sem("turned"), S.sem("kept"), S.sem("stored")
        with nc.Block() as block:
            @block.sync
            def _(sp):
                sp.dma_start(adj[:], tokens(adj_d)).then_inc(adj_ld, 16)
                sp.wait_ge(kept, NT)
                sp.dma_start(tokens(mask_d), mask[:]).then_inc(stored, 16)
                sp.wait_ge(stored, 16)

            @block.tensor
            def _(pe):
                pe.wait_ge(adj_ld, 16)
                for d in range(NT):
                    if d >= 2:
                        pe.wait_ge(kept, d - 1)
                    for s in range(NT):
                        ins = pe.transpose(tps[0:TP, d % 2, s * 128:s * 128 + TP], adj[:, s, d * TP:(d + 1) * TP],
                                           ident[0:TP, 0:TP])
                    ins.then_inc(turned, 1)

            @block.vector
            def _(dve):
                for d in range(NT):
                    dve.wait_ge(turned, d + 1)
                    dve.tensor_scalar(mask[:, d, :].rearrange("p (s n) -> p s n", s=NT),
                                      tps[0:TP, d % 2, 0:NT * 128].rearrange("p (s n) -> p s n", s=NT)[:, :, 0:TP],
                                      0.0, NEG, ALU.is_equal, ALU.mult).then_inc(kept, 1)


def gat_project_stage(nc, name, ident, x_d, k, act_kind, bias_d, w_d, heads, width, asrc_d, adst_d, h, a_s, a_d, rows_d,
                      graph):
    kb_n = k // 128
    oc = heads * width
    half = oc // 2
    hh = max(heads // 2, 1)
    hw = half // hh
    with Stage(nc, name) as S:
        w = S.sb("w", [128, kb_n, oc])
        x = S.sb("x", [TP, XS, k])
        neg = S.sb("neg", [TP, 2, k])
        bias = S.sb("bias", [TP, k])
        xT = S.sb("xT", [128, 2, kb_n, TP])
        att = S.sb("att", [TP, 2, oc])
        prod = S.sb("prod", [TP, 2, oc])
        rows = S.sb("rows", [heads * NT, TP])
        tps = S.ps("tps", [128, 2, 1024])
        hps = S.ps("hps", [128, 2, 1024])
        x_ld = [S.sem(f"x_ld{u}") for u in range(XS)]
        graph_ld = S.sem("graph_ld")
        w_ld, att_ld, bias_ld = S.sem("w_ld"), S.sem("att_ld"), S.sem("bias_ld")
        x_ready, exp_ready, low_ready, chain = S.sem("x_ready"), S.sem("exp_ready"), S.sem("low_ready"), S.sem("chain")
        turned, kept, h_done, h_kept, reduced = (S.sem(s) for s in ("turned", "kept", "h_done", "h_kept", "reduced"))
        rows_turned, rows_kept, stored, ones_set = (S.sem(s) for s in ("rows_turned", "rows_kept", "stored", "ones_set"))
        plain = act_kind is None
        with nc.Block() as block:
            @block.sync
            def _(sp):
                if not plain:
                    sp.dma_start(bias[:], row_bcast(bias_d, TP)).then_inc(bias_ld, 16)
                for t in range(NT):
                    if t >= XS:
                        sp.wait_ge(turned, t - XS + 1)
                    sp.dma_start(x[:, t % XS, :], x_d[t * TP:(t + 1) * TP, :]).then_inc(x_ld[t % XS], 16)
                    if t == 0:
                        sp.dma_start(w[:], kblocks(w_d)).then_inc(w_ld, 16)
                        sp.dma_start(att[:, 0, :], row_bcast(asrc_d, TP)).then_inc(att_ld, 16)
                        sp.dma_start(att[:, 1, :], row_bcast(adst_d, TP)).then_inc(att_ld, 16)
                sp.wait_ge(rows_kept, 1)
                sp.dma_start(rows_d[0:heads * N].rearrange("(a n) -> a n", n=TP), rows[:]).then_inc(stored, 16)
                sp.wait_ge(stored, 16)
                sp.wait_ge(graph_ld, 16 * len(graph))

            @block.gpsimd
            def _(pool):
                nc.gpsimd.memset(h[:, :, :, width:width + 1], 1.0).then_inc(ones_set, 1)

            @block.tensor
            def _(pe):
                def turn_tile(t):
                    if plain:
                        pe.wait_ge(x_ld[t % XS], 16 * (t // XS + 1))
                    else:
                        pe.wait_ge(x_ready, t + 1)
                    if t >= 2:
                        pe.wait_ge(kept, t - 1)
                    for kb in range(kb_n):
                        ins = pe.transpose(tps[:, t % 2, kb * 128:kb * 128 + TP], x[:, t % XS, kb * 128:(kb + 1) * 128],
                                           ident[0:TP, 0:TP])
                    ins.then_inc(turned, 1)

                turn_tile(0)
                pe.wait_ge(w_ld, 16)
                for t in range(NT):
                    if t + 1 < NT:
                        turn_tile(t + 1)
                    pe.wait_ge(kept, t + 1)
                    if t >= 2:
                        pe.wait_ge(h_kept, t - 1)
                    for c in range(2):
                        for kb in range(kb_n):
                            ins = pe.matmul(hps[0:TP, t % 2, c * 512:c * 512 + half], xT[:, t % 2, kb, :],
                                            w[:, kb, c * half:(c + 1) * half], start=(kb == 0), stop=(kb == kb_n - 1))
                    ins.then_inc(h_done, 1)
                pe.wait_ge(reduced, NT * 2)
                pe.transpose(tps[0:heads * NT, 0, 0:TP], a_s[:].rearrange("p h t -> p (h t)"),
                             ident[0:TP, 0:TP]).then_inc(rows_turned, 1)

            @block.scalar
            def _(act):
                def keep_h(t):
                    act.wait_ge(h_done, t + 1)
                    for c in range(2):
                        got = hps[0:TP, t % 2, c * 512:c * 512 + half].rearrange("p (h c) -> p h c", h=hh)
                        to = h[:, t, c * hh:(c + 1) * hh, 0:width] if heads > 1 else h[:, t, :, c * half:(c + 1) * half]
                        ins = act.copy(to, got)
                    ins.then_inc(h_kept, 1)

                for t in range(NT):
                    if act_kind == "elu":
                        act.wait_ge(low_ready, t + 1)
                        act.activation(neg[:, t % 2, :], neg[:, t % 2, :], ACT.Exp).then_inc(exp_ready, 1)
                    act.wait_ge(turned, t + 1)
                    if t >= 2:
                        act.wait_ge(h_done, t - 1)
                    act.copy(xT[:, t % 2], tps[:, t % 2, 0:kb_n * 128].rearrange("p (kb n) -> p kb n", kb=kb_n)[:, :, 0:TP]
                             ).then_inc(kept, 1)
                    if t == 1:
                        for to, src_d in graph:
                            act.dma_start(to[:], tokens(src_d)).then_inc(graph_ld, 16)
                    if t:
                        keep_h(t - 1)
                keep_h(NT - 1)
                act.wait_ge(rows_turned, 1)
                act.copy(rows[:], tps[0:heads * NT, 0, 0:TP]).then_inc(rows_kept, 1)

            @block.vector
            def _(dve):
                steps_done = Chain(dve, chain)

                def terms(t):
                    dve.wait_ge(h_kept, t + 1)
                    for r, to in enumerate((a_s, a_d)):
                        steps_done.done(dve.tensor_tensor(
                            prod[:, r, :].rearrange("p (h c) -> p h c", h=heads), h[:, t, :, 0:width],
                            att[:, r, :].rearrange("p (h c) -> p h c", h=heads), ALU.mult))
                    steps_done.wait()
                    for r, to in enumerate((a_s, a_d)):
                        dve.tensor_reduce(to[:, :, t], prod[:, r, :].rearrange("p (h c) -> p h c", h=heads),
                                          AX.X, ALU.add).then_inc(reduced, 1)
                    dve.wait_ge(reduced, 2 * t + 2)

                dve.wait_ge(att_ld, 32)
                if not plain:
                    dve.wait_ge(bias_ld, 16)
                for t in range(NT):
                    if not plain:
                        dve.wait_ge(x_ld[t % XS], 16 * (t // XS + 1))
                        xt = x[:, t % XS, :]
                        steps_done.done(dve.tensor_tensor(xt, xt, bias[:], ALU.add))
                        steps_done.wait()
                        if act_kind == "relu":
                            dve.tensor_scalar(xt, xt, 0.0, None, ALU.max).then_inc(x_ready, 1)
                        else:
                            dve.tensor_scalar(neg[:, t % 2, :], xt, 0.0, None, ALU.min).then_inc(low_ready, 1)
                            dve.wait_ge(low_ready, t + 1)
                            steps_done.done(dve.tensor_scalar(xt, xt, 0.0, None, ALU.max))
                            steps_done.wait()
                            dve.wait_ge(exp_ready, t + 1)
                            steps_done.done(dve.tensor_scalar(neg[:, t % 2, :], neg[:, t % 2, :], -1.0, None, ALU.add))
                            steps_done.wait()
                            dve.tensor_tensor(xt, xt, neg[:, t % 2, :], ALU.add).then_inc(x_ready, 1)
                    if t >= 2:
                        terms(t - 2)
                terms(NT - 2)
                terms(NT - 1)


def gat_max_stage(nc, name, ident, mask, heads, a_s, a_d, rows_d, a_s02, shift_d):
    with Stage(nc, name) as S:
        row = S.sb("row", [TP, 2, N])
        junk = S.sb("junk", [TP, 2, N])
        top = S.sb("top", [TP, 2, NT])
        mx = S.sb("mx", [TP, heads, NT])
        m = S.sb("m", [TP, heads, NT])
        shift = S.sb("shift", [TP, 2, heads, NT])
        rows = S.sb("rows", [heads * NT, 2, TP])
        tps = S.ps("tps", [128, 2, 512])
        row_ld = [S.sem("row_ld0"), S.sem("row_ld1")]
        chain, top_done, scanned, shift_ready = S.sem("chain"), S.sem("top_done"), S.sem("scanned"), S.sem("shift_ready")
        turned, kept, stored = S.sem("turned"), S.sem("kept"), S.sem("stored")
        with nc.Block() as block:
            @block.sync
            def _(sp):
                sp.dma_start(row[:, 0, :], row_bcast(rows_d[0:N], TP)).then_inc(row_ld[0], 16)
                for hd in range(1, heads):
                    if hd >= 2:
                        sp.wait_ge(top_done, (hd - 1) * NT)
                    sp.dma_start(row[:, hd % 2, :], row_bcast(rows_d[hd * N:(hd + 1) * N], TP)).then_inc(row_ld[hd % 2], 16)
                sp.wait_ge(kept, 2)
                sp.dma_start(shift_d[:, 0:heads * N].rearrange("r (a n) -> a r n", n=TP), rows[:]).then_inc(stored, 16)
                sp.wait_ge(stored, 16)

            @block.vector
            def _(dve):
                steps_done = Chain(dve, chain)
                for hd in range(heads):
                    dve.wait_ge(row_ld[hd % 2], 16 * (hd // 2 + 1))
                    if hd >= 2:
                        dve.wait_ge(scanned, hd - 1)
                    for d in range(NT):
                        dve.tensor_tensor_reduce(junk[:, d % 2, :], mask[:, d, :], row[:, hd % 2, :], 1.0, NEG,
                                                 ALU.add, ALU.max, top[:, hd % 2, d:d + 1]).then_inc(top_done, 1)
                        if d % 2 == 1:
                            dve.wait_ge(top_done, hd * NT + d + 1)
                    dve.tensor_copy(mx[:, hd, :], top[:, hd % 2, :]).then_inc(scanned, 1)
                dve.wait_ge(scanned, heads)
                steps_done.done(dve.tensor_tensor(mx[:], mx[:], a_d[:], ALU.add))
                steps_done.done(dve.tensor_scalar(a_s02[:], a_s[:], 0.2, None, ALU.mult))
                steps_done.wait()
                steps_done.done(dve.scalar_tensor_tensor(out=m[:], in0=mx[:], scalar=0.2, in1=mx[:],
                                                         op0=ALU.mult, op1=ALU.max))
                steps_done.wait()
                dve.tensor_tensor(shift[:, 0], a_d[:], m[:], ALU.subtract).then_inc(shift_ready, 1)
                dve.scalar_tensor_tensor(out=shift[:, 1], in0=a_d[:], scalar=0.2, in1=m[:],
                                         op0=ALU.mult, op1=ALU.subtract).then_inc(shift_ready, 1)
                for r in range(2):
                    dve.wait_ge(turned, r + 1)
                    dve.tensor_copy(rows[:, r, :], tps[0:heads * NT, r, 0:TP]).then_inc(kept, 1)

            @block.tensor
            def _(pe):
                pe.wait_ge(shift_ready, 2)
                for r in range(2):
                    pe.transpose(tps[0:heads * NT, r, 0:TP], shift[:, r].rearrange("p h t -> p (h t)"),
                                 ident[0:TP, 0:TP]).then_inc(turned, 1)


def gat_attend_stage(nc, name, adj, heads, width, h, a_s, a_s02, shift_d, out_d):
    per = width if heads > 1 else 128
    starts = [0] if heads > 1 else list(range(width - per, -1, -per))
    banks = [(0, 3), (3, 3), (6, 3), (9, 1)]
    n_out = heads * len(starts)
    with Stage(nc, name) as S:
        sh = S.sb("sh", [TP, 2, 2, N])
        e1 = S.sb("e1", [TP, 2, N])
        e2 = S.sb("e2", [TP, 2, N])
        p = S.sb("p", [TP, NT, N])
        den = S.sb("den", [TP, NT])
        rden = S.sb("rden", [TP, NT])
        o = S.sb("o", [TP, 2, NT, per])
        ops = S.ps("ops", [128, 2, 4, 512])
        sh_ld, o_st = [S.sem("sh_ld0"), S.sem("sh_ld1")], [S.sem("o_st0"), S.sem("o_st1")]
        e_done, larger, p_done, p_used = S.sem("e_done"), S.sem("larger"), S.sem("p_done"), S.sem("p_used")
        chain, o_done, o_kept = S.sem("chain"), S.sem("o_done"), S.sem("o_kept")

        def span(k):
            return per + 1 if k == 0 else per

        def loop(eng, body):
            if heads == 1:
                body(0, 0)
            else:
                with eng.Fori(0, heads // 2) as i:
                    for u in range(2):
                        body(i * 2 + u, u)

        with nc.Block() as block:
            @block.sync
            def _(sp):
                for u in range(2):
                    sp.nop().then_inc(o_st[u], 16)

                def load(hd, u):
                    for r in range(2):
                        src = shift_d[r, bass.ds(hd * N, N)]
                        sp.dma_start(sh[:, u, r, :], row_bcast(src, TP)).then_inc(sh_ld[u], 16)

                load(0, 0)
                if heads > 1:
                    load(1, 1)

                def store(k, u, c0):
                    sp.dma_start(tokens(out_d)[:, :, bass.ds(c0, per)], o[:, u]).then_inc(o_st[u], 16)

                if heads == 1:
                    for k, c0 in enumerate(starts):
                        sp.wait_ge(o_kept, 4 * (k + 3))
                        store(k, k % 2, c0)
                else:
                    with sp.Fori(0, heads // 2 - 1) as i:
                        for u in range(2):
                            sp.wait_ge(e_done, (i * 2 + u + 1) * 2 * NT)
                            load(i * 2 + u + 2, u)
                            sp.wait_ge(o_kept, (i * 2 + u + 3) * 4)
                            store(i * 2 + u, u, (i * 2 + u) * per)
                    for u in range(2):
                        sp.wait_ge(o_kept, (heads + 1 + u) * 4)
                        store(heads - 2 + u, u, (heads - 2 + u) * per)
                for u in range(2):
                    sp.wait_ge(o_st[u], 16 * (n_out // 2) + 16)

            @block.scalar
            def _(act):
                def body(hd, u):
                    act.wait_ge(sh_ld[u], (hd - u) * 16 + 32)
                    for s in range(NT):
                        act.wait_ge(p_done, hd * NT + s + 1)
                        act.activation(e1[:, s % 2, :], sh[:, u, 0, :], ACT.Exp,
                                       bias=a_s[:, bass.ds(hd, 1), s]).then_inc(e_done, 1)
                        act.activation(e2[:, s % 2, :], sh[:, u, 1, :], ACT.Exp,
                                       bias=a_s02[:, bass.ds(hd, 1), s]).then_inc(e_done, 1)

                loop(act, body)

            @block.vector
            def _(dve):
                dve.nop().then_inc(p_done, 2)
                dve.nop().then_inc(o_kept, 8)

                def normalise(hd, k, u):
                    n = hd * len(starts) + k
                    w = span(k)
                    steps_done = Chain(dve, chain, hd * 5)
                    if heads > 1:
                        dve.wait_ge(p_used, (hd + 2) * NT)
                    else:
                        dve.wait_ge(o_done, n + 1)
                    dve.wait_ge(o_st[u], (n - u) * 8 + 16)
                    got = [ops[0:TP, u, b, 0:tn * w].rearrange("p (t w) -> p t w", t=tn) for b, (_, tn) in enumerate(banks)]
                    if k == 0:
                        for (t0, tn), a in zip(banks, got):
                            steps_done.done(dve.tensor_scalar(den[:, t0:t0 + tn], a[:, :, per], 1e-16, None, ALU.add))
                        steps_done.wait()
                        steps_done.done(dve.reciprocal(rden[:], den[:]))
                        steps_done.wait()
                    for (t0, tn), a in zip(banks, got):
                        dve.tensor_tensor(o[:, u, t0:t0 + tn, :], a[:, :, 0:per],
                                          rden[:, t0:t0 + tn].unsqueeze(2).to_broadcast([TP, tn, per]),
                                          ALU.mult).then_inc(o_kept, 1)

                def weights(hd, before=None):
                    for s in range(NT):
                        if s == 4 and before is not None:
                            normalise(*before)
                        dve.wait_ge(e_done, (hd * NT + s) * 2 + 2)
                        dve.tensor_tensor(e1[:, s % 2, :], e1[:, s % 2, :], e2[:, s % 2, :], ALU.max).then_inc(larger, 1)
                        dve.wait_ge(p_used, hd * NT + s + 1)
                        dve.wait_ge(larger, hd * NT + s + 1)
                        dve.scalar_tensor_tensor(out=p[:, s, :], in0=e1[:, s % 2, :], scalar=1.0, in1=adj[:, s, :],
                                                 op0=ALU.min, op1=ALU.mult).then_inc(p_done, 1)

                weights(0)
                if heads == 1:
                    for k in range(len(starts)):
                        normalise(0, k, k % 2)
                else:
                    with dve.Fori(0, heads // 2 - 1) as i:
                        for u in range(2):
                            weights(i * 2 + u + 1, (i * 2 + u, 0, u))
                    weights(heads - 1, (heads - 2, 0, 0))
                    normalise(heads - 1, 0, 1)

            @block.tensor
            def _(pe):
                def block_sums(hd, k, c0, u):
                    n = hd * len(starts) + k
                    w = span(k)
                    if heads > 1:
                        pe.wait_ge(o_kept, (n - u) * 4 + 4 * u + 4)
                    elif k >= 2:
                        pe.wait_ge(o_kept, (k + 1) * 4)
                    for s in range(NT):
                        pe.wait_ge(p_done, hd * NT + s + 3)
                        rhs = h[:, s, bass.ds(hd, 1), c0:c0 + w]
                        for b, (t0, tn) in enumerate(banks):
                            for t in range(tn):
                                ins = pe.matmul(ops[0:TP, u, b, t * w:(t + 1) * w],
                                                p[:, s, (t0 + t) * TP:(t0 + t + 1) * TP], rhs,
                                                start=(s == 0 and t == 0), stop=(s == NT - 1), skip_group_check=True)
                        if heads > 1:
                            ins.then_inc(p_used, 1)
                    if heads == 1:
                        ins.then_inc(o_done, 1)

                def body(hd, u):
                    for k, c0 in enumerate(starts):
                        block_sums(hd, k, c0, u if heads > 1 else k % 2)

                pe.nop().then_inc(p_used, NT)
                loop(pe, body)


def router_stage(nc, ident, xT, p_d, c_d, w1_d, b1_d, z_parts_d, w1_parts_d, b1_parts_d, w_parts_d, wT):
    sm = ES * EM
    with Stage(nc, "router") as S:
        pw = S.sb("pw", [128, KB, 128])
        cb = S.sb("cb", [128, sm])
        zT = S.sb("zT", [128, N])
        zp = S.sb("zp", [128, 3, N], BF16)
        raw = S.sb("raw", [TP, 2, 2, ES, EM])
        e = S.sb("e", [TP, 2, 2, ES, EM])
        top = S.sb("top", [TP, 2, ES, 8])
        tot = S.sb("tot", [TP, ES])
        rtot = S.sb("rtot", [TP, ES])
        wgt = S.sb("wgt", [TP, 2, sm])
        w16 = S.sb("w16", [128, 2, 4, N], F16)
        rest = S.sb("rest", [128, 4, N])
        w1 = S.sb("w1", [128, EM * EH])
        w1p = S.sb("w1p", [128, 3, EM * EH], BF16)
        b1 = S.sb("b1", [ES, EM * EH])
        b1p = S.sb("b1p", [ES, 3, EM * EH], BF16)
        zps = S.ps("zps", [128, 1536])
        sps = S.ps("sps", [128, 2, 512])
        wps = S.ps("wps", [128, 2, 512])
        p_ld, c_ld, w1_ld, b1_ld, cb_zero = (S.sem(s) for s in ("p_ld", "c_ld", "w1_ld", "b1_ld", "cb_zero"))
        z_done, z_kept, s_done, s_kept = (S.sem(s) for s in ("z_done", "z_kept", "s_done", "s_kept"))
        diff, exp_done, chosen, turned, w_kept = (S.sem(s) for s in ("diff", "exp_done", "chosen", "turned", "w_kept"))
        chain, z_split, w_split, w1_split, b1_split, stored, pchain = (S.sem(s) for s in (
            "chain", "z_split", "w_split", "w1_split", "b1_split", "stored", "pchain"))
        with nc.Block() as block:
            @block.sync
            def _(sp):
                sp.dma_start(pw[:], kblocks(p_d)).then_inc(p_ld, 16)
                sp.wait_ge(cb_zero, 1)
                for s in range(ES):
                    sp.dma_start(cb[s * ER:(s + 1) * ER, s * EM:(s + 1) * EM], c_d[s]).then_inc(c_ld, 16)
                sp.dma_start(w1[:], w1_d.rearrange("s r n -> (s r) n")).then_inc(w1_ld, 16)
                sp.dma_start(b1[:], b1_d).then_inc(b1_ld, 16)
                sp.wait_ge(z_split, 3)
                sp.dma_start(z_parts_d.rearrange("k p n -> p k n"), zp[:]).then_inc(stored, 16)
                sp.wait_ge(w1_split, 3)
                sp.dma_start(w1_parts_d.rearrange("k p n -> p k n"), w1p[:]).then_inc(stored, 16)
                sp.wait_ge(b1_split, 3)
                sp.dma_start(b1_parts_d.rearrange("k p n -> p k n"), b1p[:]).then_inc(stored, 16)
                sp.wait_ge(w_split, 2)
                to = w_parts_d.rearrange("(b two) (k m) n -> two k m b n", two=2, k=2)
                for two in range(2):
                    for k in range(2):
                        sp.dma_start(to[two, k], w16[two * EM:(two + 1) * EM, k]).then_inc(stored, 16)
                sp.wait_ge(stored, 16 * 7)

            @block.gpsimd
            def _(pool):
                steps_done = Chain(pool, pchain)
                for src, parts, ld, split in ((w1, w1p, w1_ld, w1_split), (b1, b1p, b1_ld, b1_split)):
                    pool.wait_ge(ld, 16)
                    for k in range(3):
                        nc.gpsimd.tensor_copy(parts[:, k, :], src[:]).then_inc(split, 1)
                        pool.wait_ge(split, k + 1)
                        if k < 2:
                            steps_done.done(nc.gpsimd.tensor_tensor(src[:], src[:], parts[:, k, :], ALU.subtract))
                            steps_done.wait()

            @block.tensor
            def _(pe):
                pe.wait_ge(p_ld, 16)
                for c0, cn in CHUNKS:
                    for kb in range(KB):
                        ins = pe.matmul(zps[:, c0:c0 + cn], pw[:, kb, :], xT[:, kb, c0:c0 + cn],
                                        start=(kb == 0), stop=(kb == KB - 1))
                ins.then_inc(z_done, 1)
                pe.wait_ge(z_kept, 1)
                pe.wait_ge(c_ld, 16 * ES)

                def scores(t):
                    if t >= 2:
                        pe.wait_ge(s_kept, t - 1)
                    pe.matmul(sps[0:TP, t % 2, :], zT[:, t * TP:(t + 1) * TP], cb[:], start=True, stop=True).then_inc(s_done, 1)

                scores(0)
                for t in range(NT):
                    if t + 1 < NT:
                        scores(t + 1)
                    pe.wait_ge(chosen, t + 1)
                    if t >= 2:
                        pe.wait_ge(w_kept, t - 1)
                    for b in range(4):
                        ins = pe.transpose(wps[:, t % 2, b * 128:b * 128 + TP], wgt[:, t % 2, b * 128:(b + 1) * 128],
                                           ident[0:TP, 0:TP])
                    ins.then_inc(turned, 1)

            @block.scalar
            def _(act):
                act.wait_ge(z_done, 1)
                act.copy(zT[:], zps[:, 0:N]).then_inc(z_kept, 1)

                def keep_scores(t):
                    act.wait_ge(s_done, t + 1)
                    if t >= 2:
                        act.wait_ge(exp_done, t - 1)
                    act.copy(raw[:, t % 2, 0].rearrange("p s m -> p (s m)"), sps[0:TP, t % 2, :]).then_inc(s_kept, 1)

                keep_scores(0)
                for t in range(NT):
                    if t + 1 < NT:
                        keep_scores(t + 1)
                    act.wait_ge(diff, 2 * t + 2)
                    if t >= 2:
                        act.wait_ge(chosen, t - 1)
                    act.activation(e[:, t % 2], raw[:, t % 2], ACT.Exp).then_inc(exp_done, 1)
                    act.wait_ge(turned, t + 1)
                    act.copy(wT[:, :, t * TP:(t + 1) * TP],
                             wps[:, t % 2, :].rearrange("p (b n) -> p b n", b=4)[:, :, 0:TP]).then_inc(w_kept, 1)

            @block.vector
            def _(dve):
                steps_done = Chain(dve, chain)
                dve.memset(cb[:], 0.0).then_inc(cb_zero, 1)
                dve.wait_ge(z_kept, 1)
                for t in range(NT):
                    u = t % 2
                    sc, less = raw[:, u, 0], raw[:, u, 1]
                    dve.wait_ge(s_kept, t + 1)
                    for s in range(ES):
                        steps_done.done(dve.max(top[:, u, s, :], sc[:, s, :]))
                    steps_done.wait()
                    steps_done.done(dve.memset(top[:, u, :, 4:8], -NEG))
                    steps_done.wait()
                    for s in range(ES):
                        steps_done.done(dve.match_replace(less[:, s, :], top[:, u, s, :], sc[:, s, :], NEG))
                    steps_done.wait()
                    best = top[:, u, :, 0:1].to_broadcast([TP, ES, EM])
                    for k in range(2):
                        dve.tensor_tensor(raw[:, u, k], raw[:, u, k], best, ALU.subtract).then_inc(diff, 1)
                    dve.wait_ge(exp_done, t + 1)
                    steps_done.done(dve.tensor_tensor(e[:, u, 0], e[:, u, 0], e[:, u, 1], ALU.subtract))
                    steps_done.wait()
                    steps_done.done(dve.tensor_reduce(tot[:], e[:, u, 0], AX.X, ALU.add))
                    steps_done.wait()
                    steps_done.done(dve.reciprocal(rtot[:], tot[:]))
                    steps_done.wait()
                    if t >= 2:
                        dve.wait_ge(turned, t - 1)
                    dve.tensor_tensor(wgt[:, u, :].rearrange("p (s m) -> p s m", s=ES), e[:, u, 0],
                                      rtot[:].unsqueeze(2).to_broadcast([TP, ES, EM]), ALU.mult).then_inc(chosen, 1)
                dve.wait_ge(s_done, NT)
                for k in range(3):
                    dve.tensor_copy(zp[:, k, :], zT[:]).then_inc(z_split, 1)
                    dve.wait_ge(z_split, k + 1)
                    if k < 2:
                        steps_done.done(dve.tensor_tensor(zT[:], zT[:], zp[:, k, :], ALU.subtract))
                        steps_done.wait()
                dve.wait_ge(w_kept, NT)
                dve.tensor_copy(w16[:, 0], wT[:]).then_inc(w_split, 1)
                dve.wait_ge(w_split, 1)
                steps_done.done(dve.tensor_tensor(rest[:], wT[:], w16[:, 0], ALU.subtract))
                steps_done.wait()
                dve.tensor_scalar(w16[:, 1], rest[:], 4096.0, None, ALU.mult).then_inc(w_split, 1)


def expert_stage(nc, z_parts_d, w1_parts_d, b1_parts_d, w_parts_d, spread_d, w2_d, b2_d, wT, comb_d):
    step = [(0, 417), (417, 417), (834, 416)]
    steps = EJ * 3
    with Stage(nc, "expert") as S:
        z = S.sb("z", [128, 2, N], BF16)
        w1 = S.sb("w1", [128, 2, EM * EH], BF16)
        wp = S.sb("wp", [128, 2, N], F16)
        spread = S.sb("spread", [128, EJ, 128], F16)
        w2 = S.sb("w2", [128, 2, EJ, ER])
        b2 = S.sb("b2", [128, 2, ER])
        gel = S.sb("gel", [128, 3, 512])
        wgel = S.sb("wgel", [128, 3, 512])
        comb = S.sb("comb", [ER, 2, N])
        hps = S.ps("hps", [128, 3, 512])
        wps = S.ps("wps", [128, 2, 512])
        cps = S.ps("cps", [128, 3, 512])
        in_ld, stored = [S.sem("in_ld0"), S.sem("in_ld1")], [S.sem("stored0"), S.sem("stored1")]
        spread_ld, const_set = S.sem("spread_ld"), S.sem("const_set")
        h_done, w_done, gel_done, wgel_done, w2_done, comb_kept = (S.sem(s) for s in (
            "h_done", "w_done", "gel_done", "wgel_done", "w2_done", "comb_kept"))
        n_in = len(NPART) * 2 + 3 + 3
        with nc.Block() as block:
            @block.sync
            def _(sp):
                for u in range(2):
                    sp.nop().then_inc(stored[u], 16)
                sp.dma_start(spread[:], spread_d.rearrange("p (j n) -> p j n", j=EJ)).then_inc(spread_ld, 16)
                sp.wait_ge(const_set, 4)

                def load(s, u):
                    rows = bass.ds(s * ER, ER)
                    for k, (a, b) in enumerate(NPART):
                        sp.dma_start(z[k * ER:(k + 1) * ER, u, :], z_parts_d[a, rows, :]).then_inc(in_ld[u], 16)
                        sp.dma_start(w1[k * ER:(k + 1) * ER, u, :], w1_parts_d[b, rows, :]).then_inc(in_ld[u], 16)
                    for k in range(3):
                        sp.dma_start(w1[len(NPART) * ER + k:len(NPART) * ER + k + 1, u, :],
                                     b1_parts_d[k, bass.ds(s, 1), :]).then_inc(in_ld[u], 16)
                    sp.dma_start(wp[:, u, :], w_parts_d[bass.ds(s, 1), :, :].rearrange("a p n -> (a p) n")).then_inc(in_ld[u], 16)
                    sp.dma_start(w2[:, u], w2_d[bass.ds(s, 1)].rearrange("a p j r -> (a p) j r")).then_inc(in_ld[u], 16)
                    sp.dma_start(b2[u * EM:(u + 1) * EM, u, :],
                                 b2_d[bass.ds(s, 1)].rearrange("a m r -> (a m) r")).then_inc(in_ld[u], 16)

                def store(s, u):
                    sp.dma_start(comb_d[bass.ds(s * ER, ER), :], comb[:, u, :]).then_inc(stored[u], 16)

                load(0, 0)
                load(1, 1)
                with sp.Fori(0, ES // 2 - 1) as i:
                    for u in range(2):
                        sp.wait_ge(w2_done, i * 2 * steps + (u + 1) * steps + 3)
                        load(i * 2 + u + 2, u)
                        sp.wait_ge(comb_kept, i * 6 + 3 * u + 6)
                        store(i * 2 + u, u)
                for u in range(2):
                    sp.wait_ge(comb_kept, 3 * (ES + u))
                    store(ES - 2 + u, u)
                for u in range(2):
                    sp.wait_ge(stored[u], 16 * (ES // 2) + 16)

            @block.tensor
            def _(pe):
                pe.wait_ge(spread_ld, 16)
                pe.wait_ge(const_set, 4)
                pe.nop().then_inc(w2_done, 3)
                with pe.Fori(0, ES // 2) as i:
                    base = i * (2 * steps)

                    def hidden(q):
                        u, j, c = q // steps, q % steps // 3, q % 3
                        c0, cn = step[c]
                        pe.wait_ge(gel_done, base + q + 1)
                        pe.matmul(hps[:, q % 3, 0:cn], w1[0:ZK, u, j * 128:(j + 1) * 128], z[0:ZK, u, c0:c0 + cn],
                                  start=True, stop=True).then_inc(h_done, 1)
                        pe.wait_ge(wgel_done, base + q + 2)
                        pe.matmul(wps[:, q % 2, 0:cn], spread[:, j, :], wp[:, u, c0:c0 + cn],
                                  start=True, stop=True).then_inc(w_done, 1)

                    for q in range(2 * steps):
                        u, j, c = q // steps, q % steps // 3, q % 3
                        c0, cn = step[c]
                        if q % steps == 0:
                            pe.wait_ge(in_ld[u], i * 16 * n_in + 16 * n_in)
                            pe.wait_ge(comb_kept, i * 6 + 3 * u + 3)
                            hidden(q)
                        if j == 0:
                            pe.matmul(cps[0:ER, c, 0:cn], b2[:, u, :], wT[:, bass.ds(i, 1), c0:c0 + cn], start=True, stop=False)
                        if q % steps < steps - 1:
                            hidden(q + 1)
                        pe.wait_ge(wgel_done, base + q + 4)
                        pe.matmul(cps[0:ER, c, 0:cn], w2[:, u, j, :], wgel[:, q % 3, 0:cn],
                                  start=False, stop=(j == EJ - 1)).then_inc(w2_done, 1)

            @block.scalar
            def _(act):
                act.nop().then_inc(gel_done, 3)
                with act.Fori(0, ES // 2) as i:
                    base = i * (2 * steps)
                    for q in range(2 * steps):
                        cn = step[q % 3][1]
                        act.wait_ge(h_done, base + q + 1)
                        act.wait_ge(wgel_done, base + q + 1)
                        act.activation(gel[:, q % 3, 0:cn], hps[:, q % 3, 0:cn], ACT.Gelu_apprx_tanh).then_inc(gel_done, 1)

            @block.vector
            def _(dve):
                dve.nop().then_inc(wgel_done, 3)
                dve.nop().then_inc(comb_kept, 3)
                for u in range(2):
                    dve.memset(z[len(NPART) * ER:ZK, u, :], 1.0).then_inc(const_set, 1)
                    dve.memset(b2[(1 - u) * EM:(2 - u) * EM, u, :], 0.0).then_inc(const_set, 1)
                with dve.Fori(0, ES // 2) as i:
                    base = i * (2 * steps)
                    for q in range(2 * steps):
                        u, cn = q // steps, step[q % 3][1]
                        dve.wait_ge(gel_done, base + q + 4)
                        dve.wait_ge(w_done, base + q + 1)
                        dve.wait_ge(w2_done, base + q + 1)
                        dve.tensor_tensor(wgel[:, q % 3, 0:cn], gel[:, q % 3, 0:cn], wps[:, q % 2, 0:cn],
                                          ALU.mult).then_inc(wgel_done, 1)
                        if q % steps == steps - 1:
                            dve.wait_ge(w2_done, base + q + 4)
                            dve.wait_ge(stored[u], i * 16 + 16)
                            for c, (c0, cn) in enumerate(step):
                                dve.tensor_copy(comb[:, u, c0:c0 + cn], cps[0:ER, c, 0:cn]).then_inc(comb_kept, 1)


def load_rows_stage(nc, name, src_d, to):
    with Stage(nc, name) as S:
        loaded = S.sem("loaded")
        with nc.Block() as block:
            @block.sync
            def _(sp):
                sp.dma_start(to, src_d).then_inc(loaded, 16)
                sp.wait_ge(loaded, 16)


def bitlinear_stage(nc, ident, x_d, add_d, bias_d, win_d, wout_d, gin_d, gout_d, out_d):
    H = wout_d.shape[0]
    ROUND = 1.5 * 2.0 ** 23
    layers = ((win_d, KB, 2 * H), (wout_d, H // 128, D))
    with Stage(nc, "bit") as S:
        x = S.sb("x", [TP, NT, D])
        xn = S.sb("xn", [TP, NT, D])
        y = S.sb("y", [TP, NT, H])
        bias = S.sb("bias", [TP, D])
        gin = S.sb("gin", [TP, D])
        gout = S.sb("gout", [TP, H])
        win = S.sb("win", [128, KB, 2 * H])
        wout = S.sb("wout", [128, H // 128, D])
        winq = S.sb("winq", [128, KB, 2 * H], BF16)
        woutq = S.sb("woutq", [128, H // 128, D], BF16)
        stats = S.sb("stats", [TP, NT, 2, 6])
        mv = S.sb("mv", [TP, NT, 2])
        ssq = S.sb("ssq", [TP, 2, NT])
        std = S.sb("std", [TP, 3, NT])
        rstd = S.sb("rstd", [TP, 3, NT])
        epst = S.sb("epst", [128, 2])
        junk = S.sb("junk", [TP, 2, D])
        big = S.sb("big", [TP, 2, 2, NT])
        amax = S.sb("amax", [TP, 2, NT])
        ascale = S.sb("ascale", [TP, 2, NT])
        back = S.sb("back", [TP, 2, NT])
        wabs = S.sb("wabs", [128, 2])
        wmean = S.sb("wmean", [128, 2])
        wscale = S.sb("wscale", [128, 2])
        ones = S.sb("ones", [128, 128])
        identb = S.sb("identb", [128, 128], BF16)
        q = S.sb("q", [TP, 2, D], BF16)
        qT = S.sb("qT", [128, 2, KB, TP], BF16)
        sig = S.sb("sig", [TP, 2, H])
        tps = S.ps("tps", [128, 2, 1024], BF16)
        ups = S.ps("ups", [128, 2, 1024])
        mps = S.ps("mps", [128, 2])
        x_ld, add_ld, g_ld, w_ld, const_set = (S.sem(s) for s in ("x_ld", "add_ld", "g_ld", "w_ld", "const_set"))
        chain, x_ready, var_ready, std_ready, wsum_done, wmean_done, w_ready = (S.sem(s) for s in (
            "chain", "x_ready", "var_ready", "std_ready", "wsum_done", "wmean_done", "w_ready"))
        normed, sq_done, q_ready, turned, kept, up_done = (S.sem(s) for s in (
            "normed", "sq_done", "q_ready", "turned", "kept", "up_done"))
        sig_done, out_ready, stored, y_ready = (S.sem(s) for s in ("sig_done", "out_ready", "stored", "y_ready"))
        with nc.Block() as block:
            @block.sync
            def _(sp):
                sp.dma_start(win[:], kblocks(win_d)).then_inc(w_ld, 16)
                sp.dma_start(wout[:], kblocks(wout_d)).then_inc(w_ld, 16)
                sp.dma_start(x[:], tokens(x_d)).then_inc(x_ld, 16)
                sp.dma_start(xn[:], tokens(add_d)).then_inc(add_ld, 16)
                sp.dma_start(bias[:], row_bcast(bias_d, TP)).then_inc(add_ld, 16)
                sp.dma_start(gin[:], row_bcast(gin_d, TP)).then_inc(g_ld, 16)
                sp.dma_start(gout[:], row_bcast(gout_d, TP)).then_inc(g_ld, 16)
                for t in range(NT):
                    sp.wait_ge(out_ready, t + 1)
                    sp.dma_start(out_d[t * TP:(t + 1) * TP, :], x[:, t, :]).then_inc(stored, 16)
                sp.wait_ge(stored, 16 * NT)

            @block.tensor
            def _(pe):
                pe.wait_ge(const_set, 4)
                pe.wait_ge(wsum_done, 2)
                pe.matmul(mps[:, 0:2], ones[:], wabs[:], start=True, stop=True).then_inc(wmean_done, 1)
                pe.wait_ge(w_ready, 2)
                for r, wq in enumerate((winq, woutq)):
                    kb_n, cols = layers[r][1], layers[r][2]
                    cs = cols // 2
                    for t in range(NT):
                        n = r * NT + t
                        pe.wait_ge(q_ready, n + 1)
                        if n >= 2:
                            pe.wait_ge(kept, n - 1)
                        for kb in range(kb_n):
                            ins = pe.transpose(tps[:, n % 2, kb * 128:kb * 128 + TP], q[:, n % 2, kb * 128:(kb + 1) * 128],
                                               identb[0:TP, 0:TP])
                        ins.then_inc(turned, 1)
                        pe.wait_ge(kept, n + 1)
                        if n >= 2 and n - 2 < NT:
                            pe.wait_ge(y_ready, n - 1)
                        elif n >= 2:
                            pe.wait_ge(out_ready, n - 1 - NT)
                        for c in range(2):
                            for kb in range(kb_n):
                                ins = pe.matmul(ups[0:TP, n % 2, c * 512:c * 512 + cs], qT[:, n % 2, kb, :],
                                                wq[:, kb, c * cs:(c + 1) * cs], start=(kb == 0), stop=(kb == kb_n - 1))
                        ins.then_inc(up_done, 1)

            @block.scalar
            def _(act):
                act.wait_ge(const_set, 4)
                act.wait_ge(var_ready, NT)
                act.activation(std[:, 0, :], mv[:, :, 1], ACT.Sqrt, bias=epst[0:TP, 0:1]).then_inc(std_ready, 1)
                for r in range(2):
                    width = (D, H)[r]
                    for t in range(NT):
                        act.wait_ge(normed if r == 0 else y_ready, t + 1)
                        act.activation(junk[:, r, 0:width], xn[:, t, :] if r == 0 else y[:, t, :], ACT.Square,
                                       accum_out=ssq[:, r, t:t + 1]).then_inc(sq_done, 1)
                        act.wait_ge(sq_done, r * NT + t + 1)
                    act.activation(std[:, 1 + r, :], ssq[:, r, :], ACT.Sqrt, bias=epst[0:TP, 1:2],
                                   scale=1.0 / width).then_inc(std_ready, 1)
                    kb_n = layers[r][1]
                    for t in range(NT):
                        n = r * NT + t
                        act.wait_ge(turned, n + 1)
                        if n >= 2:
                            act.wait_ge(up_done, n - 1)
                        act.copy(qT[:, n % 2, 0:kb_n, :],
                                 tps[:, n % 2, 0:kb_n * 128].rearrange("p (kb n) -> p kb n", kb=kb_n)[:, :, 0:TP]).then_inc(kept, 1)
                        if r == 0:
                            act.wait_ge(up_done, n + 1)
                            if t >= 2:
                                act.wait_ge(y_ready, t - 1)
                            act.activation(sig[:, t % 2, :], ups[0:TP, n % 2, 512:512 + H], ACT.Silu,
                                           scale=back[:, 0, t:t + 1]).then_inc(sig_done, 1)

            @block.vector
            def _(dve):
                steps_done = Chain(dve, chain)
                dve.memset(epst[:, 0:1], 1e-5).then_inc(const_set, 1)
                dve.memset(epst[:, 1:2], 1e-6).then_inc(const_set, 1)
                dve.memset(ones[:], 1.0).then_inc(const_set, 1)
                dve.tensor_copy(identb[:], ident[:]).then_inc(const_set, 1)
                dve.wait_ge(w_ld, 32)
                for k, wt in enumerate((win, wout)):
                    dve.tensor_reduce(wabs[:, k:k + 1], wt[:], AX.XY, ALU.add, apply_absolute_value=True).then_inc(wsum_done, 1)
                dve.wait_ge(wmean_done, 1)
                for k, (_, kb_n, cols) in enumerate(layers):
                    steps_done.done(dve.tensor_scalar(wmean[:, k:k + 1], mps[:, k:k + 1], 1.0 / (kb_n * 128 * cols), 1e-5,
                                                      ALU.mult, ALU.max))
                steps_done.wait()
                steps_done.done(dve.reciprocal(wscale[:], wmean[:]))
                steps_done.wait()
                for k, (wt, wq) in enumerate(((win, winq), (wout, woutq))):
                    steps_done.done(dve.tensor_scalar(wt[:], wt[:], wscale[:, k:k + 1], ROUND, ALU.mult, ALU.add))
                    steps_done.wait()
                    steps_done.done(dve.tensor_scalar(wt[:], wt[:], ROUND, 1.0, ALU.subtract, ALU.min))
                    steps_done.wait()
                    dve.tensor_scalar(wq[:], wt[:], -1.0, None, ALU.max).then_inc(w_ready, 1)
                dve.wait_ge(x_ld, 16)
                dve.wait_ge(add_ld, 32)
                for t in range(NT):
                    steps_done.done(dve.tensor_tensor(xn[:, t, :], xn[:, t, :], bias[:], ALU.add))
                    steps_done.wait()
                    dve.tensor_tensor(x[:, t, :], x[:, t, :], xn[:, t, :], ALU.add).then_inc(x_ready, 1)
                    dve.wait_ge(x_ready, t + 1)
                    for k in range(2):
                        steps_done.done(dve.bn_stats(stats[:, t, k, :], x[:, t, k * 384:(k + 1) * 384]))
                    steps_done.wait()
                    dve.bn_aggr(mv[:, t, :], stats[:, t, :, :]).then_inc(var_ready, 1)
                dve.wait_ge(std_ready, 1)
                steps_done.done(dve.reciprocal(rstd[:, 0, :], std[:, 0, :]))
                steps_done.wait()
                dve.wait_ge(var_ready, NT)
                for t in range(NT):
                    dve.tensor_scalar(xn[:, t, :], x[:, t, :], mv[:, t, 0:1], rstd[:, 0, t:t + 1],
                                      ALU.subtract, ALU.mult).then_inc(normed, 1)
                dve.wait_ge(normed, NT)
                dve.wait_ge(g_ld, 32)
                for r in range(2):
                    rows, gain = ((xn, gin), (y, gout))[r]
                    width = (D, H)[r]
                    dve.wait_ge(std_ready, 2 + r)
                    steps_done.done(dve.reciprocal(rstd[:, 1 + r, :], std[:, 1 + r, :]))
                    steps_done.wait()
                    for t in range(NT):
                        steps_done.done(dve.scalar_tensor_tensor(out=rows[:, t, :], in0=rows[:, t, :],
                                                                 scalar=rstd[:, 1 + r, t:t + 1], in1=gain[:],
                                                                 op0=ALU.mult, op1=ALU.mult))
                    steps_done.wait()
                    steps_done.done(dve.tensor_reduce(amax[:, r, :], rows[:], AX.X, ALU.max, apply_absolute_value=True))
                    steps_done.wait()
                    steps_done.done(dve.tensor_scalar(amax[:, r, :], amax[:, r, :], 1e-5, None, ALU.max))
                    steps_done.wait()
                    steps_done.done(dve.reciprocal(ascale[:, r, :], amax[:, r, :]))
                    steps_done.done(dve.tensor_scalar(back[:, r, :], amax[:, r, :], wmean[0:TP, r:r + 1], 1.0 / 127.0,
                                                      ALU.mult, ALU.mult))
                    steps_done.wait()
                    steps_done.done(dve.tensor_scalar(ascale[:, r, :], ascale[:, r, :], 127.0, None, ALU.mult))
                    steps_done.wait()

                    def read_product(t):
                        n = r * NT + t
                        if r == 0:
                            dve.wait_ge(sig_done, t + 1)
                            ins = dve.scalar_tensor_tensor(out=y[:, t, :], in0=ups[0:TP, n % 2, 0:H],
                                                           scalar=back[:, 0, t:t + 1], in1=sig[:, t % 2, :],
                                                           op0=ALU.mult, op1=ALU.mult)
                            ins.then_inc(y_ready, 1)
                        else:
                            dve.wait_ge(up_done, n + 1)
                            got = ups[0:TP, n % 2, :].rearrange("p (c n) -> p c n", c=2)[:, :, 0:D // 2]
                            both = x[:, t, :].rearrange("p (c n) -> p c n", c=2)
                            dve.scalar_tensor_tensor(out=both, in0=got, scalar=back[:, 1, t:t + 1], in1=both,
                                                     op0=ALU.mult, op1=ALU.add).then_inc(out_ready, 1)

                    for t in range(NT):
                        n = r * NT + t
                        steps_done.done(dve.tensor_scalar(rows[:, t, :], rows[:, t, :], ascale[:, r, t:t + 1], ROUND,
                                                          ALU.mult, ALU.add))
                        steps_done.wait()
                        steps_done.done(dve.tensor_scalar(rows[:, t, :], rows[:, t, :], ROUND, 127.0, ALU.subtract, ALU.min))
                        steps_done.wait()
                        if n >= 2:
                            dve.wait_ge(turned, n - 1)
                        dve.tensor_scalar(q[:, n % 2, 0:width], rows[:, t, :], -128.0, None, ALU.max).then_inc(q_ready, 1)
                        if t:
                            read_product(t - 1)
                    read_product(NT - 1)


def gat_stages(nc, name, ident, x_d, adj_d, mask_d, rows_d, shift_d, layers):
    with ExitStack() as ctx:
        adj = ctx.enter_context(nc.sbuf_tensor(f"{name}_adj", [TP, NT, N], F32))
        for n, (k, act_kind, bias_d, w_d, heads, width, asrc_d, adst_d, out_d) in enumerate(layers):
            with ExitStack() as layer:
                def sb(what, shape):
                    return layer.enter_context(nc.sbuf_tensor(f"{name}{n}_{what}", shape, F32))

                h = sb("h", [TP, NT, heads, width + 1])
                a_s, a_d, a_s02 = (sb(s, [TP, heads, NT]) for s in ("a_s", "a_d", "a_s02"))
                with nc.sbuf_tensor(f"{name}{n}_mask", [TP, NT, N], BF16) as mask:
                    graph = [(mask, mask_d), (adj, adj_d)] if n == 0 else [(mask, mask_d)]
                    gat_project_stage(nc, f"{name}{n}proj", ident, x_d, k, act_kind, bias_d, w_d, heads, width,
                                      asrc_d, adst_d, h, a_s, a_d, rows_d, graph)
                    gat_max_stage(nc, f"{name}{n}max", ident, mask, heads, a_s, a_d, rows_d, a_s02, shift_d)
                gat_attend_stage(nc, f"{name}{n}att", adj, heads, width, h, a_s, a_s02, shift_d, out_d)
            x_d = out_d


def gps_two_layers(nc, inp, out_d):
    def dram(name, shape, dt=F32):
        return nc.dram_tensor(name, shape, dt).ap()

    xn_d, attn_d, sum_d, x1_d, x2_d = (dram(s, [N, D]) for s in ("xn_d", "attn_d", "sum_d", "x1_d", "x2_d"))
    adj_flat = dram("adj_d", [N * N + EXTRA])
    adj_d = adj_flat[0:N * N].rearrange("(s d) -> s d", d=N)
    mask_d = dram("mask_d", [N, N], BF16)
    g1a_d, g1b_d, g2_d = dram("g1a_d", [N, 1024]), dram("g1b_d", [N, D]), dram("g2_d", [N, D])
    rows_d, shift_d = dram("rows_d", [8 * N]), dram("shift_d", [2, 8 * N])
    z_parts_d = dram("z_parts_d", [3, 128, N], BF16)
    w1_parts_d = dram("w1_parts_d", [3, 128, EM * EH], BF16)
    b1_parts_d = dram("b1_parts_d", [3, ES, EM * EH], BF16)
    w_parts_d = dram("w_parts_d", [ES, 2 * EM, N], F16)
    comb_d = dram("comb_d", [128, N])

    with ExitStack() as top:
        def sb(ctx, name, shape, dt=F32):
            return ctx.enter_context(nc.sbuf_tensor(name, shape, dt))

        ident = sb(top, "ident", [128, 128])
        key_off = sb(top, "key_off", [TP, EC], I32)
        key_val = sb(top, "key_val", [TP, EC])
        load_rows_stage(nc, "ident", inp["ident"], ident[:])
        edge_stage(nc, ident, inp["src"], inp["dst"], inp["lower"], key_off, key_val, adj_flat)

        with ExitStack() as ctx:
            yT = sb(ctx, "yT0", [128, KB, N])
            norm_stage(nc, "ln0", ident, 1e-5, inp["x"], None, None, None, xn_d,
                       inp["L0_mix_ln1_g"], inp["L0_mix_ln1_b"], yT)
            performer_stage(nc, "perf0", yT, inp["L0_mix_qkv_w"], inp["L0_mix_qkv_b"], inp["L0_mix_v_b"],
                            inp["L0_mix_w_orf"], True, 384, HD ** -0.25, 1e-8, attn_d,
                            edges=(key_off, key_val, adj_flat.rearrange("(n a) -> n a", a=1)))
            proj_stage(nc, "proj0", ident, attn_d, inp["L0_mix_proj_w"], inp["L0_mix_proj_b"], xn_d, inp["x"], sum_d,
                       1e-5, inp["L0_mix_ln2_g"], inp["L0_mix_ln2_b"], yT)
            hidden = sb(ctx, "hidden", [128, 4 * KB, N])
            dense_stage(nc, "fc1", yT, KB, inp["L0_mix_fc1_w"], 4 * KB, inp["L0_mix_fc1_b"], ACT.Gelu_apprx_tanh, hidden)
            dense_add_stage(nc, "fc2", ident, hidden, 4 * KB, inp["L0_mix_fc2_w"], inp["L0_mix_fc2_b"], sum_d, sum_d)
        mask_stage(nc, ident, adj_d, mask_d)
        gat_stages(nc, "gat0", ident, xn_d, adj_d, mask_d, rows_d, shift_d, [
            (D, None, None, inp["L0_gnn_W1"], 8, 128, inp["L0_gnn_att_src1"], inp["L0_gnn_att_dst1"], g1a_d),
            (1024, "relu", inp["L0_gnn_b1"], inp["L0_gnn_W2"], 1, D, inp["L0_gnn_att_src2"], inp["L0_gnn_att_dst2"], g2_d)])
        with ExitStack() as ctx:
            xT = sb(ctx, "xT0", [128, KB, N])
            norm_stage(nc, "ln1", ident, 1e-5, sum_d, g2_d, inp["L0_gnn_b2"], x1_d, None, None, None, xT)
            wT = sb(ctx, "wT", [128, 4, N])
            router_stage(nc, ident, xT, inp["L0_ffn_P"], inp["L0_ffn_C"], inp["L0_ffn_W1"], inp["L0_ffn_b1"],
                         z_parts_d, w1_parts_d, b1_parts_d, w_parts_d, wT)
            expert_stage(nc, z_parts_d, w1_parts_d, b1_parts_d, w_parts_d, inp["spread"], inp["L0_ffn_W2"],
                         inp["L0_ffn_b2"], wT, comb_d)
            combT = sb(ctx, "combT", [128, 1, N])
            gT = sb(ctx, "gT", [128, 2, N])
            load_rows_stage(nc, "comb", comb_d, combT[:, 0, :])
            dense_stage(nc, "mixup", combT, 1, inp["L0_ffn_G1"], 2, inp["L0_ffn_g1b"], ACT.Gelu_apprx_tanh, gT)
            dense_add_stage(nc, "mixdown", ident, gT, 2, inp["L0_ffn_G2"], inp["L0_ffn_g2b"], x1_d, x2_d)
        with ExitStack() as ctx:
            yT = sb(ctx, "yT1", [128, KB, N])
            norm_stage(nc, "ln2", ident, 1e-5, x2_d, None, None, None, xn_d, None, None, yT)
            performer_stage(nc, "perf1", yT, inp["L1_mix_W_qkv"], None, None, inp["L1_mix_random_features"], False, 256,
                            1.0, 1e-6, attn_d)
            proj_stage(nc, "proj1", ident, attn_d, inp["L1_mix_W_proj"], inp["L1_mix_b_proj"], xn_d, x2_d, sum_d,
                       1e-5, inp["L1_mix_gamma"], inp["L1_mix_beta"], None)
        gat_stages(nc, "gat1", ident, xn_d, adj_d, mask_d, rows_d, shift_d, [
            (D, None, None, inp["L1_gnn_W1"], 8, 96, inp["L1_gnn_a_src1"], inp["L1_gnn_a_dst1"], g1b_d),
            (D, "elu", inp["L1_gnn_b1"], inp["L1_gnn_W2"], 1, D, inp["L1_gnn_a_src2"], inp["L1_gnn_a_dst2"], g2_d)])
        bitlinear_stage(nc, ident, sum_d, g2_d, inp["L1_gnn_b2"], inp["L1_ffn_w_in"], inp["L1_ffn_w_out"],
                        inp["L1_ffn_g_in"], inp["L1_ffn_g_out"], out_d)



def columns(a):
    return a.reshape(-1, 128).T


def layout(inputs):
    a = {k: np.asarray(v) for k, v in inputs.items()}
    a["L0_gnn_W1"] = a["L0_gnn_W1"].T
    a["L0_gnn_W2"] = a["L0_gnn_W2"].T
    for k in ("L0_gnn_att_src1", "L0_gnn_att_dst1", "L0_gnn_att_src2", "L0_gnn_att_dst2",
              "L1_gnn_a_src1", "L1_gnn_a_dst1", "L1_gnn_a_src2", "L1_gnn_a_dst2"):
        a[k] = a[k].reshape(-1)
    for k in ("L0_mix_ln1_g", "L0_mix_ln1_b", "L0_mix_ln2_g", "L0_mix_ln2_b", "L0_mix_fc1_b", "L0_mix_fc2_b",
              "L0_ffn_g1b", "L0_ffn_g2b"):
        a[k] = columns(a[k])
    a["L0_mix_v_b"] = a["L0_mix_qkv_b"][2 * D:]
    a["L0_mix_qkv_b"] = columns(a["L0_mix_qkv_b"][:2 * D])
    a["L0_ffn_P"] = a["L0_ffn_P"].transpose(1, 0, 2).reshape(D, ES * ER)
    a["L0_ffn_C"] = a["L0_ffn_C"].transpose(0, 2, 1)
    a["L0_ffn_W1"] = a["L0_ffn_W1"].transpose(0, 2, 1, 3).reshape(ES, ER, EM * EH)
    a["L0_ffn_b1"] = a["L0_ffn_b1"].reshape(ES, EM * EH)
    a["L0_ffn_W2"] = a["L0_ffn_W2"].reshape(ES, EJ, 128, ER).transpose(0, 2, 1, 3)
    a["L1_mix_random_features"] = a["L1_mix_random_features"].T
    a["L1_ffn_w_in"] = a["L1_ffn_w_in"].T
    a["L1_ffn_w_out"] = a["L1_ffn_w_out"].T
    a["ident"] = np.eye(128, dtype=np.float32)
    a["lower"] = np.tril(np.ones((128, 128), np.float32), -1)
    spread = np.zeros((2, EM, EJ, 4, EH), np.float16)
    for j in range(EJ):
        for m in range(4):
            spread[0, 4 * j + m, j, m, :] = 1.0
            spread[1, 4 * j + m, j, m, :] = 2.0 ** -12
    a["spread"] = spread.reshape(2 * EM, EJ * 128)
    return {k: np.ascontiguousarray(v) for k, v in a.items()}


def kernel(**inputs):
    import concourse.bacc as _bacc
    from concourse.bass_utils import run_bass_kernel_spmd as _run

    nc = _bacc.Bacc("TRN2", target_bir_lowering=False, num_devices=1)
    arrays, args = {}, {}
    for name, a in layout(inputs).items():
        arrays[f"in_{name}"] = a
        args[name] = nc.dram_tensor(f"in_{name}", a.shape, mybir.dt.from_np(a.dtype), kind="ExternalInput").ap()
    out = nc.dram_tensor("out", (N, D), F32, kind="ExternalOutput").ap()
    gps_two_layers(nc, args, out)
    r = _run(nc, [arrays], core_ids=[0])
    return r.results[0]["out"]
```

```python
from contextlib import ExitStack, contextmanager

import numpy as np

import concourse.bass as bass
from concourse import mybir

F32 = mybir.dt.float32
BF16 = mybir.dt.bfloat16
F32R = mybir.dt.float32r

F16 = mybir.dt.float16
I32 = mybir.dt.int32
I16 = mybir.dt.int16
ACT = mybir.ActivationFunctionType
ALU = mybir.AluOpType
AX = mybir.AxisListType

N = 1250
E = 20000
D = 768
NT = 10
TP = N // NT
KB = D // 128
HEADS = 12
HD = D // HEADS
HP = HEADS // 2
CHUNKS = [(0, 512), (512, 512), (1024, N - 1024)]
EC = E // TP
XS = 4
WS = 3
EB = 16
NEG = -3.0e38
ES, ER, EM, EH = 8, 16, 64, 32
EJ = EM * EH // 128
NPART = [(0, 0), (1, 0), (0, 1), (1, 1), (2, 0), (0, 2)]
ZK = len(NPART) * ER + 3
EG = 4
EXTRA = 128


class Stage:

    def __init__(self, nc, name):
        self.nc, self.name, self.sems = nc, name, []

    def __enter__(self):
        self.ctx = ExitStack()
        return self

    def sb(self, name, shape, dt=F32):
        return self.ctx.enter_context(self.nc.sbuf_tensor(f"{self.name}_{name}", shape, dt))

    def ps(self, name, shape, dt=F32):
        return self.ctx.enter_context(self.nc.psum_tensor(f"{self.name}_{name}", shape, dt))

    def sem(self, name):
        s = self.nc.alloc_semaphore(f"{self.name}_{name}")
        self.sems.append(s)
        return s

    def __exit__(self, kind, *rest):
        if kind is None:
            self.nc.clear_and_free_semaphores(self.sems)
            self.nc.all_engine_barrier()
        self.ctx.close()


class Chain:

    def __init__(self, eng, sem, base=0):
        self.eng, self.sem, self.base, self.n = eng, sem, base, 0

    def done(self, ins):
        self.n += 1
        return ins.then_inc(self.sem, 1)

    def wait(self):
        self.eng.wait_ge(self.sem, self.base + self.n)


def row_bcast(ap1d, parts):
    n = ap1d.shape[0]
    return bass.AP(ap1d.tensor, ap1d.offset, [[0, parts], [1, n]])


def tokens(ap2d):
    return ap2d.rearrange("(t p) d -> p t d", p=TP)


def kblocks(ap2d):
    return ap2d.rearrange("(kb p) n -> p kb n", p=128)


def split_tile(dve, full, parts, t, split):
    cols = slice(t * TP, (t + 1) * TP)
    dve.tensor_copy(parts[0][:, :, cols], full).then_inc(split, 1)
    dve.wait_ge(split, 2 * t + 1)
    dve.tensor_tensor(parts[1][:, :, cols], full, parts[0][:, :, cols].bitcast(F32), ALU.subtract).then_inc(split, 1)


def edge_stage(nc, ident, src, dst, lower, key_off, key_val, adj_d):
    with Stage(nc, "edge") as S:
        ends = S.sb("ends", [TP, 2, EC], I32)
        endf = S.sb("endf", [TP, 2, EC])
        key = S.sb("key", [TP, EC])
        low = S.sb("low", [TP, TP])
        ones = S.sb("ones", [TP, TP])
        diag = S.sb("diag", [TP, 2, EB, TP])
        eq = S.sb("eq", [TP, EB, TP], BF16)
        below = S.sb("below", [TP, EB, TP], BF16)
        lowb = S.sb("lowb", [TP, TP], BF16)
        cnt = S.sb("cnt", [TP, EC])
        rank = S.sb("rank", [TP, EC])
        first = S.sb("first", [TP, EC])
        spare = S.sb("spare", [TP, 1])
        offf = S.sb("offf", [TP, EC])
        zero = S.sb("zero", [TP, 6250])
        keys = S.ps("keys", [TP, 2, 4, 512])
        loaded, low_ld, chain = S.sem("loaded"), S.sem("low_ld"), S.sem("chain")
        diag_done, bc_done, cmp_done = S.sem("diag_done"), S.sem("bc_done"), S.sem("cmp_done")
        zeroed, cleared, spare_set = S.sem("zeroed"), S.sem("cleared"), S.sem("spare_set")
        steps = EC // EB
        with nc.Block() as block:
            @block.sync
            def _(sp):
                sp.dma_start(ends[:, 0, :], src.rearrange("(p c) -> p c", c=EC)).then_inc(loaded, 16)
                sp.dma_start(ends[:, 1, :], dst.rearrange("(p c) -> p c", c=EC)).then_inc(loaded, 16)
                sp.dma_start(low[:], lower[0:TP, 0:TP]).then_inc(low_ld, 16)
                sp.wait_ge(zeroed, 1)
                for half in range(2):
                    sp.dma_start(adj_d[half * TP * 6250:(half + 1) * TP * 6250].rearrange("(p n) -> p n", p=TP),
                                 zero[:]).then_inc(cleared, 16)
                sp.dma_start(adj_d[N * N:N * N + EXTRA].rearrange("(a n) -> a n", a=1),
                             zero[0:1, 0:EXTRA]).then_inc(cleared, 16)
                sp.wait_ge(cleared, 48)

            @block.gpsimd
            def _(pool):
                nc.gpsimd.memset(zero[:], 0.0).then_inc(zeroed, 1)
                nc.gpsimd.iota(key_off[:, 0:1], [[0, 1]], base=N * N, channel_multiplier=1).then_inc(spare_set, 1)

            @block.tensor
            def _(pe):
                pe.wait_ge(low_ld, 16)
                for i in range(steps):
                    pe.wait_ge(diag_done, i + 1)
                    if i >= 2:
                        pe.wait_ge(cmp_done, i - 1)
                    for b in range(4):
                        ins = pe.matmul(keys[:, i % 2, b, 0:4 * TP], ones[:, :],
                                        diag[:, i % 2, 4 * b:4 * b + 4, :], start=True, stop=True)
                    ins.then_inc(bc_done, 1)

            @block.vector
            def _(dve):
                steps_done = Chain(dve, chain)
                steps_done.done(dve.memset(ones[:], 1.0))
                dve.wait_ge(loaded, 32)
                steps_done.done(dve.tensor_copy(endf[:], ends[:]))
                steps_done.wait()
                steps_done.done(dve.scalar_tensor_tensor(out=key[:], in0=endf[:, 0, :], scalar=float(N),
                                                         in1=endf[:, 1, :], op0=ALU.mult, op1=ALU.add))
                dve.wait_ge(low_ld, 16)
                steps_done.done(dve.tensor_copy(lowb[:], low[:]))
                steps_done.wait()

                def set_diag(i):
                    if i >= 2:
                        dve.wait_ge(bc_done, i - 1)
                    dve.tensor_tensor(diag[:, i % 2], ident[0:TP, 0:TP].unsqueeze(1).to_broadcast([TP, EB, TP]),
                                      key[:, i * EB:(i + 1) * EB].unsqueeze(2).to_broadcast([TP, EB, TP]),
                                      ALU.mult).then_inc(diag_done, 1)

                set_diag(0)
                for i in range(steps):
                    cols = slice(i * EB, (i + 1) * EB)
                    if i + 1 < steps:
                        set_diag(i + 1)
                    dve.wait_ge(bc_done, i + 1)
                    for b in range(4):
                        ins = steps_done.done(dve.tensor_tensor(
                            eq[:, 4 * b:4 * b + 4, :], keys[:, i % 2, b, 0:4 * TP].rearrange("p (c e) -> p c e", c=4),
                            key[:, i * EB + 4 * b:i * EB + 4 * b + 4].unsqueeze(2).to_broadcast([TP, 4, TP]),
                            ALU.is_equal))
                    steps_done.wait()
                    dve.tensor_tensor(below[:], eq[:], lowb[:].unsqueeze(1).to_broadcast([TP, EB, TP]),
                                      ALU.mult).then_inc(cmp_done, 1)
                    steps_done.done(dve.tensor_reduce(cnt[:, cols], eq[:], AX.X, ALU.add))
                    dve.wait_ge(cmp_done, i + 1)
                    steps_done.done(dve.tensor_reduce(rank[:, cols], below[:], AX.X, ALU.add))
                    steps_done.wait()
                dve.wait_ge(spare_set, 1)
                steps_done.done(dve.tensor_copy(spare[:], key_off[:, 0:1]))
                steps_done.done(dve.tensor_scalar(first[:], rank[:], 0.0, None, ALU.is_equal))
                steps_done.wait()
                steps_done.done(dve.tensor_scalar(offf[:], key[:], spare[:, 0:1], None, ALU.subtract))
                steps_done.done(dve.tensor_tensor(key_val[:], cnt[:], first[:], ALU.mult))
                steps_done.wait()
                steps_done.done(dve.tensor_tensor(offf[:], offf[:], first[:], ALU.mult))
                steps_done.wait()
                steps_done.done(dve.tensor_scalar(key_off[:], offf[:], spare[:, 0:1], None, ALU.add))


def add_edges(nc, pool, key_off, key_val, added, adj_flat):
    for c in range(EC):
        if c:
            pool.wait_ge(added, c * 16)
        nc.gpsimd.indirect_dma_start(
            out=adj_flat, out_offset=bass.IndirectOffsetOnAxis(ap=key_off[:, c:c + 1], axis=0),
            in_=key_val[:, c:c + 1], in_offset=None, compute_op=ALU.add).then_inc(added, 16)
    pool.wait_ge(added, EC * 16)


def norm_stage(nc, name, ident, eps, x_d, add_d, bias_d, sum_d, normed_d, gain_cols, shift_cols, yT):
    second = gain_cols is not None
    with Stage(nc, name) as S:
        x = S.sb("x", [TP, NT, D])
        add = S.sb("add", [TP, NT, D]) if add_d is not None else None
        bias = S.sb("bias", [TP, D])
        cols = S.sb("cols", [128, 2, KB])
        stats = S.sb("stats", [TP, NT, 2, 6])
        mv = S.sb("mv", [TP, 2, NT, 2])
        std = S.sb("std", [TP, 2, NT])
        rstd = S.sb("rstd", [TP, 2, NT])
        epst = S.sb("epst", [TP, 1])
        tps = S.ps("tps", [128, 2, 1024])
        x_ld, add_ld, cols_ld = [S.sem("x_ld0"), S.sem("x_ld1")], S.sem("add_ld"), S.sem("cols_ld")
        chain, var_ready, std_ready = S.sem("chain"), S.sem("var_ready"), S.sem("std_ready")
        sum_ready, normed, final = S.sem("sum_ready"), S.sem("normed"), S.sem("final")
        turned, kept, stored = S.sem("turned"), S.sem("kept"), S.sem("stored")
        half = NT // 2
        with nc.Block() as block:
            @block.sync
            def _(sp):
                n_stored = 0
                for h in range(2):
                    rows = slice(h * half, (h + 1) * half)
                    sp.dma_start(x[:, rows, :], tokens(x_d)[:, rows, :]).then_inc(x_ld[h], 16)
                if add_d is not None:
                    sp.dma_start(add[:], tokens(add_d)).then_inc(add_ld, 16)
                    sp.dma_start(bias[:], row_bcast(bias_d, TP)).then_inc(add_ld, 16)
                if second:
                    sp.dma_start(cols[:, 0, :], gain_cols).then_inc(cols_ld, 16)
                    sp.dma_start(cols[:, 1, :], shift_cols).then_inc(cols_ld, 16)
                if sum_d is not None:
                    sp.wait_ge(sum_ready, NT)
                    sp.dma_start(tokens(sum_d), add[:]).then_inc(stored, 16)
                    n_stored += 1
                if normed_d is not None:
                    sp.wait_ge(normed, NT)
                    sp.dma_start(tokens(normed_d), x[:]).then_inc(stored, 16)
                    n_stored += 1
                if n_stored:
                    sp.wait_ge(stored, 16 * n_stored)

            @block.vector
            def _(dve):
                steps_done = Chain(dve, chain)
                steps_done.done(dve.memset(epst[:], eps))
                if add_d is not None:
                    dve.wait_ge(add_ld, 32)
                for t in range(NT):
                    if t % half == 0:
                        dve.wait_ge(x_ld[t // half], 16)
                    if add_d is not None:
                        steps_done.done(dve.tensor_tensor(add[:, t, :], add[:, t, :], bias[:], ALU.add))
                        steps_done.wait()
                        steps_done.done(dve.tensor_tensor(add[:, t, :], add[:, t, :], x[:, t, :], ALU.add))
                        steps_done.wait()
                        dve.tensor_copy(x[:, t, :], add[:, t, :]).then_inc(sum_ready, 1)
                        dve.wait_ge(sum_ready, t + 1)
                    for k in range(2):
                        steps_done.done(dve.bn_stats(stats[:, t, k, :], x[:, t, k * 384:(k + 1) * 384]))
                    steps_done.wait()
                    dve.bn_aggr(mv[:, 0, t, :], stats[:, t, :, :]).then_inc(var_ready, 1)

                def normalise(r, signal):
                    dve.wait_ge(std_ready, r + 1)
                    steps_done.done(dve.reciprocal(rstd[:, r, :], std[:, r, :]))
                    steps_done.wait()
                    dve.wait_ge(var_ready, (r + 1) * NT)
                    for t in range(NT):
                        ins = dve.tensor_scalar(x[:, t, :], x[:, t, :], mv[:, r, t, 0:1], rstd[:, r, t:t + 1],
                                                ALU.subtract, ALU.mult)
                        ins.then_inc(signal, 1)

                if second:
                    normalise(0, normed)
                    for t in range(NT):
                        dve.wait_ge(normed, t + 1)
                        for k in range(2):
                            steps_done.done(dve.bn_stats(stats[:, t, k, :], x[:, t, k * 384:(k + 1) * 384]))
                        steps_done.wait()
                        dve.bn_aggr(mv[:, 1, t, :], stats[:, t, :, :]).then_inc(var_ready, 1)
                    if normed_d is not None:
                        dve.wait_ge(stored, 16)
                    normalise(1, final)
                else:
                    normalise(0, normed)

            @block.scalar
            def _(act):
                for r in range(2 if second else 1):
                    act.wait_ge(chain, 1)
                    act.wait_ge(var_ready, (r + 1) * NT)
                    act.activation(std[:, r, :], mv[:, r, :, 1], ACT.Sqrt, bias=epst[:, 0:1]).then_inc(std_ready, 1)
                if second:
                    act.wait_ge(cols_ld, 32)
                for t in range(NT):
                    act.wait_ge(turned, t + 1)
                    tile = yT[:, :, t * TP:(t + 1) * TP]
                    if second:
                        for kb in range(KB):
                            ins = act.activation(tile[:, kb, :], tps[:, t % 2, kb * 128:kb * 128 + TP], ACT.Identity,
                                                 scale=cols[:, 0, kb:kb + 1], bias=cols[:, 1, kb:kb + 1])
                    else:
                        ins = act.copy(tile, tps[:, t % 2, 0:KB * 128].rearrange("p (kb n) -> p kb n", kb=KB)[:, :, 0:TP])
                    ins.then_inc(kept, 1)

            @block.tensor
            def _(pe):
                for t in range(NT):
                    pe.wait_ge(final if second else normed, t + 1)
                    if t >= 2:
                        pe.wait_ge(kept, t - 1)
                    for kb in range(KB):
                        ins = pe.transpose(tps[:, t % 2, kb * 128:kb * 128 + TP], x[:, t, kb * 128:(kb + 1) * 128],
                                           ident[0:TP, 0:TP])
                    ins.then_inc(turned, 1)


def performer_stage(nc, name, yT, w_d, bias_cols, vbias_d, feat_d, per_head, m, scale, eps, out_d, edges=None, scan=None):
    mb_n = m // 128
    per = 512 // m
    n_k = NT // per
    n_phi = n_k + 3 * mb_n
    phi_banks = [3, 4, 0, 1, 2]
    ring = len(phi_banks)
    vw = HD + 1
    with Stage(nc, name) as S:
        w = S.sb("w", [128, 2, 3, KB, 128])
        feat = S.sb("feat", [128, 2, 2, m])
        qs = S.sb("qs", [128, 2, N])
        ks = S.sb("ks", [128, 2, N])
        v = S.sb("v", [TP, NT, 2, vw])
        kphi = S.sb("kphi", [TP, 2, NT, m])
        qphi = S.sb("qphi", [128, 2, mb_n, N])
        ktv = S.sb("ktv", [128, 2, mb_n, vw])
        den = S.sb("den", [TP, NT])
        rden = S.sb("rden", [TP, NT])
        o = S.sb("o", [TP, 2, NT, 128])
        bcols = S.sb("bcols", [128, 12])
        vbias = S.sb("vbias", [TP, D])
        lnm = S.sb("lnm", [128, 1])
        wide = S.ps("wide", [128, 5, 512])
        proj = wide[:, 0:3, :].rearrange("p b n -> p (b n)")
        ktv_ps = S.ps("ktv_ps", [128, 512])
        o_ps = S.ps("o_ps", [128, 2, 512])
        w_ld = [S.sem("w_ld0"), S.sem("w_ld1")]
        o_st = [S.sem("o_st0"), S.sem("o_st1")]
        bias_ld, const_set = S.sem("bias_ld"), S.sem("const_set")
        proj_done, plain_done, square_done, v_done = (S.sem(s) for s in (
            "proj_done", "plain_done", "square_done", "v_done"))
        phi_done, exp_done, ktv_done, ktv_kept, o_done, o_kept, chain = (S.sem(s) for s in (
            "phi_done", "exp_done", "ktv_done", "ktv_kept", "o_done", "o_kept", "chain"))
        added = S.sem("added")
        o_tiles = [(0, 0, 7), (1, 7, 3)]
        biased = bias_cols is not None
        scan = MaxScan(S, *scan) if scan is not None else None

        with nc.Block() as block:
            if scan is not None:
                @block.gpsimd
                def _(pool):
                    scan.load(pool)

            if edges is not None:
                @block.gpsimd
                def _(pool):
                    add_edges(nc, pool, edges[0], edges[1], added, edges[2])

            @block.sync
            def _(sp):
                for u in range(2):
                    sp.nop().then_inc(o_st[u], 16)
                if biased:
                    sp.dma_start(bcols[:], bias_cols).then_inc(bias_ld, 16)
                    sp.dma_start(vbias[:], row_bcast(vbias_d, TP)).then_inc(bias_ld, 16)

                def load(g, u):
                    for k in range(3):
                        sp.dma_start(w[:, u, k], kblocks(w_d)[:, :, bass.ds(g * 128 + k * D, 128)]).then_inc(w_ld[u], 16)
                    for x in range(2):
                        f = feat_d[bass.ds(g * 2 + x, 1), :, :].rearrange("a c m -> (a c) m") if per_head else feat_d
                        sp.dma_start(feat[64 * x:64 * x + 64, u, x, :], f).then_inc(w_ld[u], 16)

                def store(g, u):
                    sp.dma_start(tokens(out_d)[:, :, bass.ds(g * 128, 128)], o[:, u]).then_inc(o_st[u], 16)

                load(0, 0)
                load(1, 1)
                with sp.Fori(0, HP // 2 - 1) as i:
                    for u in range(2):
                        sp.wait_ge(o_done, (i * 2 + u) * 2 + 1)
                        load(i * 2 + u + 2, u)
                        sp.wait_ge(o_kept, (i * 2 + u + 1) * 4 + 1)
                        store(i * 2 + u, u)
                for u in range(2):
                    sp.wait_ge(o_kept, (HP - 1 + u) * 4 + 1)
                    store(HP - 2 + u, u)
                for u in range(2):
                    sp.wait_ge(o_st[u], 16 * (HP // 2) + 16)

            @block.tensor
            def _(pe):
                pe.wait_ge(const_set, 6)
                with pe.Fori(0, HP // 2) as i:
                    for u in range(2):
                        g = i * 2 + u
                        pe.wait_ge(w_ld[u], i * 80 + 80)
                        for k in range(2):
                            for c, (c0, cn) in enumerate(CHUNKS):
                                if k == 0:
                                    pe.wait_ge(v_done, g * 6 + 1)
                                else:
                                    pe.wait_ge(plain_done, g * 12 + 2 * c + 2)
                                for kb in range(KB):
                                    ins = pe.matmul(proj[:, c0:c0 + cn], w[:, u, k, kb, :], yT[:, kb, c0:c0 + cn],
                                                    start=(kb == 0), stop=(kb == KB - 1))
                                ins.then_inc(proj_done, 1)
                        for t in range(NT):
                            if t % 4 == 0:
                                pe.wait_ge(plain_done, g * 12 + 8 + 2 * (t // 4))
                            for kb in range(KB):
                                ins = pe.matmul(proj[0:TP, t * 128:(t + 1) * 128], yT[:, kb, t * TP:(t + 1) * TP],
                                                w[:, u, 2, kb, :], start=(kb == 0), stop=(kb == KB - 1))
                            if t in (3, 7, 9):
                                ins.then_inc(proj_done, 1)

                        def features(j, products):
                            if j == 0:
                                pe.wait_ge(exp_done, g * (2 * n_phi) + 1)
                            elif j == 2:
                                pe.wait_ge(v_done, g * 6 + 7)
                            elif j >= ring:
                                pe.wait_ge(exp_done, g * (2 * n_phi) + j - ring + 2)
                            for out, lhsT, rhs in products:
                                ins = pe.matmul(out, lhsT, rhs, start=True, stop=True)
                            ins.then_inc(phi_done, 1)

                        def k_features(x):
                            for n in range(n_k):
                                j = x * n_phi + n
                                features(j, [(wide[0:TP, phi_banks[j % ring], y * m:(y + 1) * m],
                                              ks[:, x, (n * per + y) * TP:(n * per + y + 1) * TP], feat[:, u, x, :])
                                             for y in range(per)])

                        def q_features(x):
                            j = x * n_phi + n_k
                            for mb in range(mb_n):
                                for c0, cn in CHUNKS:
                                    features(j, [(wide[:, phi_banks[j % ring], 0:cn],
                                                  feat[:, u, x, mb * 128:(mb + 1) * 128], qs[:, x, c0:c0 + cn])])
                                    j += 1

                        def k_t_v(x):
                            pe.wait_ge(exp_done, g * (2 * n_phi) + x * n_phi + n_k + 1)
                            pe.wait_ge(v_done, g * 6 + 7)
                            pe.wait_ge(ktv_kept, g * 2 + x + 1)
                            for mb in range(mb_n):
                                for t in range(NT):
                                    ins = pe.matmul(ktv_ps[:, mb * vw:(mb + 1) * vw],
                                                    kphi[:, x, t, mb * 128:(mb + 1) * 128], v[:, t, x, :],
                                                    start=(t == 0), stop=(t == NT - 1))
                            ins.then_inc(ktv_done, 1)

                        def outputs(x):
                            pe.wait_ge(exp_done, g * (2 * n_phi) + (x + 1) * n_phi + 1)
                            pe.wait_ge(ktv_kept, g * 2 + x + 2)
                            pe.wait_ge(o_kept, g * 4 + 2 * x + 1)
                            for bank, t0, tn in o_tiles:
                                for t in range(t0, t0 + tn):
                                    for mb in range(mb_n):
                                        ins = pe.matmul(o_ps[0:TP, bank, (t - t0) * vw:(t - t0 + 1) * vw],
                                                        qphi[:, x, mb, t * TP:(t + 1) * TP], ktv[:, x, mb, :],
                                                        start=(mb == 0), stop=(mb == mb_n - 1))
                            return ins

                        pe.wait_ge(plain_done, g * 12 + 12)
                        pe.wait_ge(square_done, g * 4 + 4)
                        k_features(0)
                        q_features(0)
                        k_features(1)
                        k_t_v(0)
                        q_features(1)
                        outputs(0).then_inc(o_done, 1)
                        k_t_v(1)
                        outputs(1).then_inc(o_done, 1)

            @block.scalar
            def _(act):
                act.wait_ge(const_set, 6)
                act.nop().then_inc(exp_done, 1)
                with act.Fori(0, HP // 2) as i:
                    for u in range(2):
                        g = i * 2 + u
                        for k, dest in enumerate((qs, ks)):
                            for x in range(2):
                                rows, other = slice(64 * x, 64 * x + 64), slice(64 - 64 * x, 128 - 64 * x)
                                act.wait_ge(plain_done, g * 12 + k * 6 + 6)
                                act.activation(dest[other, x, :], dest[rows, x, :], ACT.Square).then_inc(square_done, 1)

                        def exps(j, out, in_, parts):
                            act.wait_ge(phi_done, g * (2 * n_phi) + j + 1)
                            act.activation(out, in_, ACT.Exp, bias=lnm[0:parts, 0:1], scale=scale).then_inc(exp_done, 1)

                        def k_exps(x):
                            for n in range(n_k):
                                j = x * n_phi + n
                                got = wide[0:TP, phi_banks[j % ring], 0:per * m].rearrange("p (y m) -> p y m", y=per)
                                exps(j, kphi[:, x, n * per:(n + 1) * per, :], got, TP)

                        def q_exps(x):
                            j = x * n_phi + n_k
                            for mb in range(mb_n):
                                for c0, cn in CHUNKS:
                                    exps(j, qphi[:, x, mb, c0:c0 + cn], wide[:, phi_banks[j % ring], 0:cn], 128)
                                    j += 1

                        k_exps(0)
                        q_exps(0)
                        k_exps(1)
                        q_exps(1)

            @block.vector
            def _(dve):
                for s in (v_done, ktv_kept, o_kept):
                    dve.nop().then_inc(s, 1)
                for u in range(2):
                    dve.memset(feat[64:128, u, 0, :], -0.5 * scale).then_inc(const_set, 1)
                    dve.memset(feat[0:64, u, 1, :], -0.5 * scale).then_inc(const_set, 1)
                dve.memset(lnm[:], -0.5 * float(np.log(m))).then_inc(const_set, 1)
                dve.memset(v[:, :, :, HD:vw], 1.0).then_inc(const_set, 1)
                if biased:
                    dve.wait_ge(bias_ld, 32)
                if scan is not None:
                    dve.wait_ge(scan.mask_ld, 16)
                    scan.head(dve, 0, 0, 0)
                with dve.Fori(0, HP // 2) as i:
                    for u in range(2):
                        g = i * 2 + u
                        steps_done = Chain(dve, chain, g * 6)
                        for k, dest in enumerate((qs, ks)):
                            for c, (c0, cn) in enumerate(CHUNKS):
                                dve.wait_ge(proj_done, g * 9 + k * 3 + c + 1)
                                for x in range(2):
                                    rows = slice(64 * x, 64 * x + 64)
                                    if biased:
                                        ins = dve.tensor_scalar(dest[rows, x, c0:c0 + cn], proj[rows, c0:c0 + cn],
                                                                bcols[rows, bass.ds(g + k * KB, 1)], None, ALU.add)
                                    else:
                                        ins = dve.tensor_copy(dest[rows, x, c0:c0 + cn], proj[rows, c0:c0 + cn])
                                    ins.then_inc(plain_done, 1)
                        for c, (t0, tn) in enumerate(((0, 4), (4, 4), (8, 2))):
                            dve.wait_ge(proj_done, g * 9 + 7 + c)
                            got = proj[0:TP, t0 * 128:(t0 + tn) * 128].rearrange("p (t x c) -> p t x c", t=tn, x=2)
                            for x in range(2):
                                if biased:
                                    vb = vbias[:, bass.ds(g * 128 + x * HD, HD)]
                                    ins = dve.tensor_tensor(v[:, t0:t0 + tn, x, 0:HD], got[:, :, x, :],
                                                            vb.unsqueeze(1).to_broadcast([TP, tn, HD]), ALU.add)
                                else:
                                    ins = dve.tensor_copy(v[:, t0:t0 + tn, x, 0:HD], got[:, :, x, :])
                                ins.then_inc(v_done, 1)

                        if scan is not None:
                            scan.head(dve, g + 1, 1 - u, i + u)

                        def keep_ktv(x):
                            dve.wait_ge(ktv_done, g * 2 + x + 1)
                            dve.tensor_copy(ktv[:, x], ktv_ps[:, 0:mb_n * vw].rearrange("p (a b) -> p a b", a=mb_n)
                                            ).then_inc(ktv_kept, 1)

                        def keep_out(x):
                            dve.wait_ge(o_done, g * 2 + x + 1)
                            if x == 0:
                                dve.wait_ge(o_st[u], i * 16 + 16)
                            got = [o_ps[0:TP, b, 0:tn * vw].rearrange("p (t w) -> p t w", t=tn) for b, _, tn in o_tiles]
                            for (_, t0, tn), a in zip(o_tiles, got):
                                steps_done.done(dve.tensor_scalar(den[:, t0:t0 + tn], a[:, :, HD], eps, None, ALU.add))
                            steps_done.wait()
                            steps_done.done(dve.reciprocal(rden[:], den[:]))
                            steps_done.wait()
                            for (_, t0, tn), a in zip(o_tiles, got):
                                dve.tensor_tensor(o[:, u, t0:t0 + tn, x * HD:(x + 1) * HD], a[:, :, 0:HD],
                                                  rden[:, t0:t0 + tn].unsqueeze(2).to_broadcast([TP, tn, HD]),
                                                  ALU.mult).then_inc(o_kept, 1)

                        keep_ktv(0)
                        keep_out(0)
                        keep_ktv(1)
                        keep_out(1)
                if scan is not None:
                    scan.head(dve, HP + 1, 1, HP // 2)


def proj_stage(nc, name, ident, attn_d, w_d, bias_d, xn_d, x_d, sum_d, eps, gain, shift, yT, ahead=()):
    turn = yT is not None
    with Stage(nc, name) as S:
        a = S.sb("a", [TP, NT, D])
        h = S.sb("h", [TP, NT, D])
        x = S.sb("x", [TP, NT, D])
        w = S.sb("w", [128, KB, D])
        aT = S.sb("aT", [128, 2, KB, TP])
        bias = S.sb("bias", [TP, D])
        rows = S.sb("rows", [128, 2, KB if turn else D])
        stats = S.sb("stats", [TP, NT, 2, 6])
        mv = S.sb("mv", [TP, NT, 2])
        std = S.sb("std", [TP, NT])
        rstd = S.sb("rstd", [TP, NT])
        epst = S.sb("epst", [TP, 1])
        full = S.sb("full", [128, 2, KB, TP]) if turn else None
        tps = S.ps("tps", [128, 2, 1024])
        hps = S.ps("hps", [128, 2, 1024])
        split, full_ready = S.sem("split"), S.sem("full_ready")
        a_ld, w_ld, xn_ld, x_ld = S.sem("a_ld"), S.sem("w_ld"), S.sem("xn_ld"), S.sem("x_ld")
        rows_ld, chain = S.sem("rows_ld"), S.sem("chain")
        turned, kept, h_done, h_read, var_ready, std_ready = (S.sem(s) for s in (
            "turned", "kept", "h_done", "h_read", "var_ready", "std_ready"))
        normed, sum_ready, stored = S.sem("normed"), S.sem("sum_ready"), S.sem("stored")
        ahead_ld = S.sem("ahead_ld")
        with nc.Block() as block:
            @block.sync
            def _(sp):
                sp.dma_start(a[:], tokens(attn_d)).then_inc(a_ld, 16)
                sp.dma_start(w[:], kblocks(w_d)).then_inc(w_ld, 16)
                sp.dma_start(h[:], tokens(xn_d)).then_inc(xn_ld, 16)
                sp.dma_start(bias[:], row_bcast(bias_d, TP)).then_inc(xn_ld, 16)
                sp.dma_start(x[:], tokens(x_d)).then_inc(x_ld, 16)
                for k, r in enumerate((gain, shift)):
                    if turn:
                        sp.dma_start(rows[:, k, :], r).then_inc(rows_ld, 16)
                    else:
                        sp.dma_start(rows[0:TP, k, :], row_bcast(r, TP)).then_inc(rows_ld, 16)
                for to, src_d in ahead:
                    sp.dma_start(to, src_d).then_inc(ahead_ld, 16)
                sp.wait_ge(sum_ready, NT)
                sp.dma_start(tokens(sum_d), x[:]).then_inc(stored, 16)
                sp.wait_ge(stored, 16)
                if ahead:
                    sp.wait_ge(ahead_ld, 16 * len(ahead))

            @block.tensor
            def _(pe):
                pe.wait_ge(a_ld, 16)

                def turn_tile(t):
                    if t >= 2:
                        pe.wait_ge(kept, t - 1)
                    for kb in range(KB):
                        ins = pe.transpose(tps[:, t % 2, kb * 128:kb * 128 + TP], a[:, t % NT, kb * 128:(kb + 1) * 128],
                                           ident[0:TP, 0:TP])
                    ins.then_inc(turned, 1)

                turn_tile(0)
                pe.wait_ge(w_ld, 16)
                for t in range(NT):
                    if t + 1 < NT:
                        turn_tile(t + 1)
                    pe.wait_ge(kept, t + 1)
                    if t >= 2:
                        pe.wait_ge(h_read, t - 1)
                    for c in range(2):
                        for kb in range(KB):
                            ins = pe.matmul(hps[0:TP, t % 2, c * 512:c * 512 + 384], aT[:, t % 2, kb, :],
                                            w[:, kb, c * 384:(c + 1) * 384], start=(kb == 0), stop=(kb == KB - 1))
                    ins.then_inc(h_done, 1)
                if turn:
                    for t in range(NT):
                        pe.wait_ge(normed, t + 1)
                        turn_tile(NT + t)

            @block.scalar
            def _(act):
                for t in range(NT):
                    act.wait_ge(turned, t + 1)
                    if t >= 2:
                        act.wait_ge(h_done, t - 1)
                    act.copy(aT[:, t % 2], tps[:, t % 2, 0:KB * 128].rearrange("p (kb n) -> p kb n", kb=KB)[:, :, 0:TP]
                             ).then_inc(kept, 1)
                act.wait_ge(chain, 1)
                act.wait_ge(var_ready, NT)
                act.activation(std[:], mv[:, :, 1], ACT.Sqrt, bias=epst[:, 0:1]).then_inc(std_ready, 1)
                if turn:
                    act.wait_ge(rows_ld, 32)
                    for t in range(NT):
                        act.wait_ge(turned, NT + t + 1)
                        if t >= 2:
                            act.wait_ge(split, 2 * t - 2)
                        for kb in range(KB):
                            ins = act.activation(full[:, t % 2, kb, :],
                                                 tps[:, t % 2, kb * 128:kb * 128 + TP], ACT.Identity,
                                                 scale=rows[:, 0, kb:kb + 1], bias=rows[:, 1, kb:kb + 1])
                        ins.then_inc(kept, 1)

            @block.vector
            def _(dve):
                steps_done = Chain(dve, chain)
                steps_done.done(dve.memset(epst[:], eps))
                dve.wait_ge(xn_ld, 32)
                dve.wait_ge(x_ld, 16)
                for t in range(NT):
                    steps_done.done(dve.tensor_tensor(h[:, t, :], h[:, t, :], bias[:], ALU.add))
                    dve.wait_ge(h_done, t + 1)
                    steps_done.wait()
                    both = h[:, t, :].rearrange("p (c n) -> p c n", c=2)
                    got = hps[0:TP, t % 2, :].rearrange("p (c n) -> p c n", c=2)[:, :, 0:384]
                    dve.tensor_tensor(both, both, got, ALU.add).then_inc(h_read, 1)
                    dve.wait_ge(h_read, t + 1)
                    for k in range(2):
                        steps_done.done(dve.bn_stats(stats[:, t, k, :], h[:, t, k * 384:(k + 1) * 384]))
                    if turn:
                        dve.tensor_tensor(x[:, t, :], x[:, t, :], h[:, t, :], ALU.add).then_inc(sum_ready, 1)
                    steps_done.wait()
                    dve.bn_aggr(mv[:, t, :], stats[:, t, :, :]).then_inc(var_ready, 1)
                dve.wait_ge(std_ready, 1)
                steps_done.done(dve.reciprocal(rstd[:], std[:]))
                steps_done.wait()
                dve.wait_ge(var_ready, NT)
                if not turn:
                    dve.wait_ge(rows_ld, 32)
                for t in range(NT):
                    dst = a[:, t, :] if turn else h[:, t, :]
                    dve.tensor_scalar(dst, h[:, t, :], mv[:, t, 0:1], rstd[:, t:t + 1],
                                      ALU.subtract, ALU.mult).then_inc(normed, 1)
                    if not turn:
                        dve.wait_ge(normed, t + 1)
                        steps_done.done(dve.tensor_tensor(h[:, t, :], h[:, t, :], rows[0:TP, 0, :], ALU.mult))
                        steps_done.done(dve.tensor_tensor(x[:, t, :], x[:, t, :], rows[0:TP, 1, :], ALU.add))
                        steps_done.wait()
                        dve.tensor_tensor(x[:, t, :], x[:, t, :], h[:, t, :], ALU.add).then_inc(sum_ready, 1)
                if turn:
                    for t in range(NT):
                        dve.wait_ge(kept, NT + t + 1)
                        split_tile(dve, full[:, t % 2], yT, t, split)


def dense_stage(nc, name, xT, w_d, ob_n, bias_cols, func, outT):
    with Stage(nc, name) as S:
        w = S.sb("w", [128, ob_n, 128])
        bias = S.sb("bias", [128, ob_n])
        ps = S.ps("ps", [128, 2, 1536])
        in_ld, done, kept = S.sem("in_ld"), S.sem("done"), S.sem("kept")
        with nc.Block() as block:
            @block.sync
            def _(sp):
                sp.dma_start(w[:], w_d.rearrange("p (g n) -> p g n", g=ob_n)).then_inc(in_ld, 16)
                sp.dma_start(bias[:], bias_cols).then_inc(in_ld, 16)

            @block.tensor
            def _(pe):
                pe.wait_ge(in_ld, 32)
                for g in range(ob_n):
                    if g >= 2:
                        pe.wait_ge(kept, g - 1)
                    for c0, cn in CHUNKS:
                        ins = pe.matmul(ps[:, g % 2, c0:c0 + cn], w[:, g, :], xT[:, c0:c0 + cn], start=True, stop=True)
                    ins.then_inc(done, 1)

            @block.scalar
            def _(act):
                act.wait_ge(in_ld, 32)
                for g in range(ob_n):
                    act.wait_ge(done, g + 1)
                    act.activation(outT[:, g, :], ps[:, g % 2, 0:N], func, bias=bias[:, g:g + 1]).then_inc(kept, 1)


def fc1_stage(nc, yT, w_d, bias_cols, hidden, mask_d, rows_d, mx):
    ob_n, SB = 4 * KB, 16
    over = [hidden[0:TP, k0:k1].rearrange("p b n -> p (b n)") for k0, k1 in ((16, 21), (21, 23), (23, 24))]
    room = (over[0].bitcast(BF16).rearrange("p (t n) -> p t n", t=NT), over[1].rearrange("p (u n) -> p u n", u=2),
            over[2].bitcast(BF16).rearrange("p (u n) -> p u n", u=2))
    with Stage(nc, "fc1") as S:
        w = S.sb("w", [128, 2, KB, 128])
        w_hi, w_lo = S.sb("w_hi", [128, 2, KB, 128], F32R), S.sb("w_lo", [128, 2, KB, 128], F32R)
        bias = S.sb("bias", [128, ob_n])
        ps = S.ps("ps", [128, 2, 1536])
        w_ld = [S.sem("w_ld0"), S.sem("w_ld1")]
        bias_ld, w_high, w_split, done, kept = (S.sem(s) for s in ("bias_ld", "w_high", "w_split", "done", "kept"))
        scan = MaxScan(S, mask_d, rows_d, 8, mx, room)
        with nc.Block() as block:
            @block.sync
            def _(sp):
                sp.dma_start(bias[:], bias_cols).then_inc(bias_ld, 16)

                def load(g, u):
                    sp.dma_start(w[:, u], kblocks(w_d)[:, :, bass.ds(g * 128, 128)]).then_inc(w_ld[u], 16)

                load(0, 0)
                load(1, 1)
                with sp.Fori(0, ob_n // 2 - 1) as i:
                    for u in range(2):
                        sp.wait_ge(w_split, i * 2 + u + 1)
                        load(i * 2 + u + 2, u)

            @block.gpsimd
            def _(pool):
                scan.load(pool)

            @block.tensor
            def _(pe):
                with pe.Fori(0, ob_n // 2) as i:
                    for u in range(2):
                        pe.wait_ge(w_split, i * 2 + u + 1)
                        pe.wait_ge(kept, i * 2 + u + 1)
                        for c0, cn in CHUNKS:
                            for kb in range(KB):
                                for n, (wp, yp) in enumerate(((w_hi, 1), (w_lo, 0), (w_hi, 0))):
                                    ins = pe.matmul(ps[:, u, c0:c0 + cn], wp[:, u, kb, :], yT[yp][:, kb, c0:c0 + cn],
                                                    start=(kb == 0 and n == 0), stop=(kb == KB - 1 and n == 2))
                        ins.then_inc(done, 1)

            @block.scalar
            def _(act):
                def high(g, u, n):
                    act.wait_ge(w_ld[u], n * 16 + 16)
                    if not (isinstance(g, int) and g < 2):
                        act.wait_ge(done, g - 1)
                    act.copy(w_hi[:, u], w[:, u]).then_inc(w_high, 1)

                def gelu(g, u):
                    act.wait_ge(done, g + 1)
                    act.activation(hidden[:, bass.ds(g, 1), :], ps[:, u:u + 1, 0:N], ACT.Gelu_apprx_tanh,
                                   bias=bias[:, bass.ds(g, 1)]).then_inc(kept, 1)

                act.wait_ge(bias_ld, 16)
                act.nop().then_inc(kept, 2)
                high(0, 0, 0)
                high(1, 1, 0)
                gelu(0, 0)
                with act.Fori(0, SB // 2 - 1) as i:
                    for u in range(2):
                        high(i * 2 + u + 2, u, i + 1)
                        gelu(i * 2 + u + 1, 1 - u)
                act.wait_ge(scan.scanned, 8)
                with act.Fori(SB // 2 - 1, ob_n // 2 - 1) as i:
                    for u in range(2):
                        high(i * 2 + u + 2, u, i + 1)
                        gelu(i * 2 + u + 1, 1 - u)
                gelu(ob_n - 1, 1)

            @block.vector
            def _(dve):
                def low(g, u):
                    dve.wait_ge(w_high, g + 1)
                    dve.tensor_tensor(w_lo[:, u], w[:, u], w_hi[:, u].bitcast(F32), ALU.subtract).then_inc(w_split, 1)

                low(0, 0)
                low(1, 1)
                dve.wait_ge(scan.mask_ld, 16)
                scan.start(dve, 0, 0, 0)
                scan.tiles(dve, 0, 0, 0, NT // 2)
                low(2, 0)
                scan.tiles(dve, 0, 0, NT // 2, NT)
                scan.finish(dve, 0, 0)
                low(3, 1)
                scan.head(dve, 1, 1, 0)
                with dve.Fori(1, 4) as i:
                    for x in range(2):
                        hd = i * 2 + x
                        scan.start(dve, hd, x, i)
                        for half in range(2):
                            low(i * 4 + 2 * x + half, half)
                            scan.tiles(dve, hd, x, half * NT // 2, (half + 1) * NT // 2)
                        scan.finish(dve, hd, x)
                with dve.Fori(SB // 2, ob_n // 2) as i:
                    for u in range(2):
                        low(i * 2 + u, u)


def dense_add_stage(nc, name, ident, xT, kb_n, w_d, bias_cols, sum_d, out_d, ahead=()):
    ob_n = KB
    with Stage(nc, name) as S:
        w = S.sb("w", [128, 2, kb_n, 128])
        bias = S.sb("bias", [128, ob_n])
        y = S.sb("y", [128, 2, N])
        acc = S.sb("acc", [TP, 2, NT, 128])
        ps = S.ps("ps", [128, 1536])
        tps = S.ps("tps", [128, 1536])
        w_ld, acc_ld = [S.sem("w_ld0"), S.sem("w_ld1")], [S.sem("acc_ld0"), S.sem("acc_ld1")]
        stored = [S.sem("stored0"), S.sem("stored1")]
        bias_ld, done, kept, turned, summed = (S.sem(s) for s in ("bias_ld", "done", "kept", "turned", "summed"))
        ahead_ld = S.sem("ahead_ld")
        with nc.Block() as block:
            @block.sync
            def _(sp):
                sp.dma_start(bias[:], bias_cols).then_inc(bias_ld, 16)
                for g in range(ob_n + 2):
                    u = g % 2
                    cols = slice(g * 128, (g + 1) * 128)
                    if g >= 2:
                        old = slice((g - 2) * 128, (g - 1) * 128)
                        sp.wait_ge(summed, g - 1)
                        sp.dma_start(tokens(out_d)[:, :, old], acc[:, u]).then_inc(stored[u], 16)
                    if g < ob_n:
                        sp.dma_start(w[:, u], kblocks(w_d)[:, :, cols]).then_inc(w_ld[u], 16)
                        if g >= 2:
                            sp.wait_ge(stored[u], 16 * (g // 2))
                        sp.dma_start(acc[:, u], tokens(sum_d)[:, :, cols]).then_inc(acc_ld[u], 16)
                    if g == 1:
                        for to, src_d in ahead:
                            sp.dma_start(to, src_d).then_inc(ahead_ld, 16)
                for u in range(2):
                    sp.wait_ge(stored[u], 16 * (ob_n // 2))
                if ahead:
                    sp.wait_ge(ahead_ld, 16 * len(ahead))

            @block.tensor
            def _(pe):
                def turn_back(g):
                    pe.wait_ge(kept, 3 * (g + 1))
                    if g:
                        pe.wait_ge(summed, g)
                    for t in range(NT):
                        ins = pe.transpose(tps[0:TP, t * 128:(t + 1) * 128], y[:, g % 2, t * TP:(t + 1) * TP], ident[:])
                    ins.then_inc(turned, 1)

                for g in range(ob_n):
                    pe.wait_ge(w_ld[g % 2], 16 * (g // 2 + 1))
                    for c, (c0, cn) in enumerate(CHUNKS):
                        if g:
                            pe.wait_ge(kept, 3 * (g - 1) + c + 1)
                        for kb in range(kb_n):
                            ins = pe.matmul(ps[:, c0:c0 + cn], w[:, g % 2, kb, :], xT[:, kb, c0:c0 + cn],
                                            start=(kb == 0), stop=(kb == kb_n - 1))
                        ins.then_inc(done, 1)
                    if g:
                        turn_back(g - 1)
                turn_back(ob_n - 1)

            @block.scalar
            def _(act):
                act.wait_ge(bias_ld, 16)
                for g in range(ob_n):
                    for c, (c0, cn) in enumerate(CHUNKS):
                        act.wait_ge(done, 3 * g + c + 1)
                        if g >= 2:
                            act.wait_ge(turned, g - 1)
                        act.activation(y[:, g % 2, c0:c0 + cn], ps[:, c0:c0 + cn], ACT.Identity,
                                       bias=bias[:, g:g + 1]).then_inc(kept, 1)

            @block.vector
            def _(dve):
                for g in range(ob_n):
                    dve.wait_ge(turned, g + 1)
                    dve.wait_ge(acc_ld[g % 2], 16 * (g // 2 + 1))
                    dve.tensor_tensor(acc[:, g % 2], acc[:, g % 2],
                                      tps[0:TP, 0:NT * 128].rearrange("p (t n) -> p t n", t=NT), ALU.add).then_inc(summed, 1)


def mask_stage(nc, ident, adj_d, mask_d, counts_d):
    with Stage(nc, "mask") as S:
        adj = S.sb("adj", [TP, NT, N])
        mask = S.sb("mask", [TP, NT, N], BF16)
        counts = S.sb("counts", [TP, NT, N], I16)
        tps = S.ps("tps", [128, 2, 2048])
        adj_ld, turned, kept, stored = S.sem("adj_ld"), S.sem("turned"), S.sem("kept"), S.sem("stored")
        counted = S.sem("counted")
        with nc.Block() as block:
            @block.sync
            def _(sp):
                sp.dma_start(adj[:], tokens(adj_d)).then_inc(adj_ld, 16)
                sp.wait_ge(counted, NT)
                sp.dma_start(tokens(counts_d), counts[:]).then_inc(stored, 16)
                sp.wait_ge(kept, NT)
                sp.dma_start(tokens(mask_d), mask[:]).then_inc(stored, 16)
                sp.wait_ge(stored, 32)

            @block.scalar
            def _(act):
                act.wait_ge(adj_ld, 16)
                for s in range(NT):
                    act.copy(counts[:, s, :], adj[:, s, :]).then_inc(counted, 1)

            @block.tensor
            def _(pe):
                pe.wait_ge(adj_ld, 16)
                for d in range(NT):
                    if d >= 2:
                        pe.wait_ge(kept, d - 1)
                    for s in range(NT):
                        ins = pe.transpose(tps[0:TP, d % 2, s * 128:s * 128 + TP], adj[:, s, d * TP:(d + 1) * TP],
                                           ident[0:TP, 0:TP])
                    ins.then_inc(turned, 1)

            @block.vector
            def _(dve):
                for d in range(NT):
                    dve.wait_ge(turned, d + 1)
                    dve.tensor_scalar(mask[:, d, :].rearrange("p (s n) -> p s n", s=NT),
                                      tps[0:TP, d % 2, 0:NT * 128].rearrange("p (s n) -> p s n", s=NT)[:, :, 0:TP],
                                      0.0, NEG, ALU.is_equal, ALU.mult).then_inc(kept, 1)


def gat_project_stage(nc, name, ident, x_d, k, act_kind, bias_d, w_d, heads, width, asrc_d, adst_d, h, a_s, a_d, rows_d,
                      ahead=(), h_d=None):
    kb_n = k // 128
    oc = heads * width
    half = oc // 2
    hh = max(heads // 2, 1)
    hw = half // hh
    with Stage(nc, name) as S:
        w = S.sb("w", [128, WS, oc])
        w_hi, w_lo = S.sb("w_hi", [128, kb_n, oc], F32R), S.sb("w_lo", [128, kb_n, oc], F32R)
        x = S.sb("x", [TP, XS, k])
        neg = S.sb("neg", [TP, 2, k])
        bias = S.sb("bias", [TP, k])
        xT_hi, xT_lo = S.sb("xT_hi", [128, 2, kb_n, TP], F32R), S.sb("xT_lo", [128, 2, kb_n, TP], F32R)
        att = S.sb("att", [TP, 2, oc])
        prod = S.sb("prod", [TP, 2, oc])
        rows = S.sb("rows", [heads * NT, TP])
        tps = S.ps("tps", [128, 2, 1024])
        hps = S.ps("hps", [128, 2, 1024])
        x_ld = [S.sem(f"x_ld{u}") for u in range(XS)]
        ahead_ld, h_st = S.sem("ahead_ld"), S.sem("h_st")
        if h is None:
            h = S.sb("h", [TP, NT, heads, width + 1])
        w_ld, att_ld, bias_ld = [S.sem(f"w_ld{u}") for u in range(WS)], S.sem("att_ld"), S.sem("bias_ld")
        w_high, w_split, x_high = S.sem("w_high"), S.sem("w_split"), S.sem("x_high")
        x_ready, exp_ready, low_ready, chain = S.sem("x_ready"), S.sem("exp_ready"), S.sem("low_ready"), S.sem("chain")
        turned, kept, h_done, h_kept, reduced = (S.sem(s) for s in ("turned", "kept", "h_done", "h_kept", "reduced"))
        rows_turned, rows_kept, stored, ones_set = (S.sem(s) for s in ("rows_turned", "rows_kept", "stored", "ones_set"))
        plain = act_kind is None

        def turned_tile(t):
            return tps[:, t % 2, 0:kb_n * 128].rearrange("p (kb n) -> p kb n", kb=kb_n)[:, :, 0:TP]

        with nc.Block() as block:
            @block.sync
            def _(sp):
                if not plain:
                    sp.dma_start(bias[:], row_bcast(bias_d, TP)).then_inc(bias_ld, 16)
                for t in range(NT):
                    if t >= XS:
                        sp.wait_ge(turned, t - XS + 1)
                    sp.dma_start(x[:, t % XS, :], x_d[t * TP:(t + 1) * TP, :]).then_inc(x_ld[t % XS], 16)
                    if t == 0:
                        for kb in range(kb_n):
                            if kb >= WS:
                                sp.wait_ge(w_split, kb - WS + 1)
                            sp.dma_start(w[:, kb % WS, :], w_d[kb * 128:(kb + 1) * 128, :]).then_inc(w_ld[kb % WS], 16)
                        sp.dma_start(att[:, 0, :], row_bcast(asrc_d, TP)).then_inc(att_ld, 16)
                        sp.dma_start(att[:, 1, :], row_bcast(adst_d, TP)).then_inc(att_ld, 16)
                if h_d is not None:
                    sp.wait_ge(ones_set, 1)
                    for t in range(NT):
                        sp.wait_ge(h_kept, t + 1)
                        sp.dma_start(h_d[t * TP:(t + 1) * TP, :], h[:, t].rearrange("p h w -> p (h w)")).then_inc(h_st, 16)
                sp.wait_ge(rows_kept, 1)
                sp.dma_start(rows_d[0:heads * N].rearrange("(a n) -> a n", n=TP), rows[:]).then_inc(stored, 16)
                sp.wait_ge(stored, 16)
                if ahead:
                    sp.wait_ge(ahead_ld, 16 * len(ahead))
                if h_d is not None:
                    sp.wait_ge(h_st, 16 * NT)

            @block.gpsimd
            def _(pool):
                nc.gpsimd.memset(h[:, :, :, width:width + 1], 1.0).then_inc(ones_set, 1)

            @block.tensor
            def _(pe):
                def turn_tile(t):
                    if plain:
                        pe.wait_ge(x_ld[t % XS], 16 * (t // XS + 1))
                    else:
                        pe.wait_ge(x_ready, t + 1)
                    if t >= 2:
                        pe.wait_ge(kept, t - 1)
                    for kb in range(kb_n):
                        ins = pe.transpose(tps[:, t % 2, kb * 128:kb * 128 + TP], x[:, t % XS, kb * 128:(kb + 1) * 128],
                                           ident[0:TP, 0:TP])
                    ins.then_inc(turned, 1)

                turn_tile(0)
                for t in range(NT):
                    if t + 1 < NT:
                        turn_tile(t + 1)
                    pe.wait_ge(kept, t + 1)
                    if t >= 2:
                        pe.wait_ge(h_kept, t - 1)
                    for c in range(2):
                        cols = slice(c * half, (c + 1) * half)
                        for kb in range(kb_n):
                            if t == 0 and c == 0:
                                pe.wait_ge(w_split, kb + 1)
                            for n, (xp, wp) in enumerate(((xT_hi, w_lo), (xT_lo, w_hi), (xT_hi, w_hi))):
                                ins = pe.matmul(hps[0:TP, t % 2, c * 512:c * 512 + half], xp[:, t % 2, kb, :],
                                                wp[:, kb, cols], start=(kb == 0 and n == 0),
                                                stop=(kb == kb_n - 1 and n == 2))
                    ins.then_inc(h_done, 1)
                pe.wait_ge(reduced, NT * 2)
                pe.transpose(tps[0:heads * NT, 0, 0:TP], a_s[:].rearrange("p h t -> p (h t)"),
                             ident[0:TP, 0:TP]).then_inc(rows_turned, 1)

            @block.scalar
            def _(act):
                def keep_h(t):
                    act.wait_ge(h_done, t + 1)
                    for c in range(2):
                        got = hps[0:TP, t % 2, c * 512:c * 512 + half].rearrange("p (h c) -> p h c", h=hh)
                        to = h[:, t, c * hh:(c + 1) * hh, 0:width] if heads > 1 else h[:, t, :, c * half:(c + 1) * half]
                        ins = act.copy(to, got)
                    ins.then_inc(h_kept, 1)

                def exp_low(t):
                    act.wait_ge(low_ready, t + 1)
                    act.activation(neg[:, t % 2, :], neg[:, t % 2, :], ACT.Exp).then_inc(exp_ready, 1)

                if act_kind == "elu":
                    exp_low(0)
                for kb in range(kb_n):
                    act.wait_ge(w_ld[kb % WS], 16 * (kb // WS + 1))
                    act.copy(w_hi[:, kb, :], w[:, kb % WS, :]).then_inc(w_high, 1)
                for t in range(NT):
                    if act_kind == "elu" and t + 1 < NT:
                        exp_low(t + 1)
                    act.wait_ge(turned, t + 1)
                    if t >= 2:
                        act.wait_ge(h_done, t - 1)
                    act.copy(xT_hi[:, t % 2], turned_tile(t)).then_inc(x_high, 1)
                    if t == 1:
                        for to, src_d in ahead:
                            act.dma_start(to, src_d).then_inc(ahead_ld, 16)
                    if t:
                        keep_h(t - 1)
                keep_h(NT - 1)
                act.wait_ge(rows_turned, 1)
                act.copy(rows[:], tps[0:heads * NT, 0, 0:TP]).then_inc(rows_kept, 1)

            @block.vector
            def _(dve):
                steps_done = Chain(dve, chain)

                def terms(t):
                    dve.wait_ge(h_kept, t + 1)
                    for r, to in enumerate((a_s, a_d)):
                        steps_done.done(dve.tensor_tensor(
                            prod[:, r, :].rearrange("p (h c) -> p h c", h=heads), h[:, t, :, 0:width],
                            att[:, r, :].rearrange("p (h c) -> p h c", h=heads), ALU.mult))
                    steps_done.wait()
                    for r, to in enumerate((a_s, a_d)):
                        dve.tensor_reduce(to[:, :, t], prod[:, r, :].rearrange("p (h c) -> p h c", h=heads),
                                          AX.X, ALU.add).then_inc(reduced, 1)
                    dve.wait_ge(reduced, 2 * t + 2)

                def prepare(t):
                    dve.wait_ge(x_ld[t % XS], 16 * (t // XS + 1))
                    xt = x[:, t % XS, :]
                    steps_done.done(dve.tensor_tensor(xt, xt, bias[:], ALU.add))
                    steps_done.wait()
                    if act_kind == "relu":
                        dve.tensor_scalar(xt, xt, 0.0, None, ALU.max).then_inc(x_ready, 1)
                    else:
                        dve.tensor_scalar(neg[:, t % 2, :], xt, 0.0, None, ALU.min).then_inc(low_ready, 1)
                        dve.wait_ge(low_ready, t + 1)
                        steps_done.done(dve.tensor_scalar(xt, xt, 0.0, None, ALU.max))
                        steps_done.wait()
                        dve.wait_ge(exp_ready, t + 1)
                        steps_done.done(dve.tensor_scalar(neg[:, t % 2, :], neg[:, t % 2, :], -1.0, None, ALU.add))
                        steps_done.wait()
                        dve.tensor_tensor(xt, xt, neg[:, t % 2, :], ALU.add).then_inc(x_ready, 1)

                if not plain:
                    dve.wait_ge(bias_ld, 16)
                    prepare(0)
                for kb in range(kb_n):
                    dve.wait_ge(w_high, kb + 1)
                    dve.tensor_tensor(w_lo[:, kb, :], w[:, kb % WS, :], w_hi[:, kb, :].bitcast(F32),
                                      ALU.subtract).then_inc(w_split, 1)
                dve.wait_ge(att_ld, 32)
                for t in range(NT):
                    if not plain and t + 1 < NT:
                        prepare(t + 1)
                    dve.wait_ge(x_high, t + 1)
                    dve.tensor_tensor(xT_lo[:, t % 2], turned_tile(t), xT_hi[:, t % 2].bitcast(F32),
                                      ALU.subtract).then_inc(kept, 1)
                    if t >= 2:
                        terms(t - 2)
                terms(NT - 2)
                terms(NT - 1)


class MaxScan:

    def __init__(self, S, mask, rows_d, heads, mx, room=None):
        self.rows_d, self.heads, self.mx = rows_d, heads, mx
        self.mask_d = None if len(mask.shape) == 3 else mask
        if room is not None:
            self.mask, self.row, self.sums = room
        else:
            self.mask = mask if self.mask_d is None else S.sb("mask", [TP, NT, N], BF16)
            self.row = S.sb("row", [TP, 2, N])
            self.sums = S.sb("sums", [TP, 2, N], BF16)
        self.top = S.sb("top", [TP, 2, NT])
        self.mask_ld, self.row_ld = S.sem("mask_ld"), [S.sem("row_ld0"), S.sem("row_ld1")]
        self.top_done, self.scanned, self.paced = S.sem("top_done"), S.sem("scanned"), S.sem("paced")

    def load(self, eng):
        for hd in range(self.heads):
            if hd >= 2:
                eng.wait_ge(self.top_done, (hd - 1) * NT)
            eng.dma_start(self.row[:, hd % 2, :], row_bcast(self.rows_d[hd * N:(hd + 1) * N], TP)
                          ).then_inc(self.row_ld[hd % 2], 16)
            if hd == 0 and self.mask_d is not None:
                eng.dma_start(self.mask[:], tokens(self.mask_d)).then_inc(self.mask_ld, 16)

    def start(self, dve, hd, u, n):
        dve.wait_ge(self.row_ld[u], n * 16 + 16)
        if not (isinstance(hd, int) and hd == 0):
            dve.wait_ge(self.scanned, hd)
        dve.nop().then_inc(self.paced, 1)

    def tiles(self, dve, hd, u, d0, d1):
        for d in range(d0, d1):
            dve.tensor_tensor_reduce(self.sums[:, d % 2, :], self.mask[:, d, :], self.row[:, u, :], 1.0, NEG,
                                     ALU.add, ALU.max, self.top[:, u, d:d + 1]).then_inc(self.top_done, 1)
            if d % 2 == 1:
                dve.wait_ge(self.top_done, hd * NT + d + 1)
                dve.nop().then_inc(self.paced, 1)

    def finish(self, dve, hd, u):
        dve.tensor_copy(self.mx[:, bass.ds(hd, 1), :], self.top[:, u:u + 1, :]).then_inc(self.scanned, 1)

    def head(self, dve, hd, u, n):
        self.start(dve, hd, u, n)
        self.tiles(dve, hd, u, 0, NT)
        self.finish(dve, hd, u)


def gat_shift_stage(nc, name, ident, heads, a_s, a_d, mx, a_s02, shift_d, scan=None):
    with Stage(nc, name) as S:
        m = S.sb("m", [TP, heads, NT])
        shift = S.sb("shift", [TP, 2, heads, NT])
        rows = S.sb("rows", [heads * NT, 2, TP])
        tps = S.ps("tps", [128, 2, 512])
        chain, shift_ready = S.sem("chain"), S.sem("shift_ready")
        turned, kept, stored = S.sem("turned"), S.sem("kept"), S.sem("stored")
        scan = MaxScan(S, *scan) if scan is not None else None
        with nc.Block() as block:
            @block.sync
            def _(sp):
                if scan is not None:
                    scan.load(sp)
                sp.wait_ge(kept, 2)
                sp.dma_start(shift_d[:, 0:heads * N].rearrange("r (a n) -> a r n", n=TP), rows[:]).then_inc(stored, 16)
                sp.wait_ge(stored, 16)

            @block.vector
            def _(dve):
                steps_done = Chain(dve, chain)
                if scan is not None:
                    for hd in range(heads):
                        scan.head(dve, hd, hd % 2, hd // 2)
                    dve.wait_ge(scan.scanned, heads)
                steps_done.done(dve.tensor_tensor(mx[:], mx[:], a_d[:], ALU.add))
                steps_done.done(dve.tensor_scalar(a_s02[:], a_s[:], 0.2, None, ALU.mult))
                steps_done.wait()
                steps_done.done(dve.scalar_tensor_tensor(out=m[:], in0=mx[:], scalar=0.2, in1=mx[:],
                                                         op0=ALU.mult, op1=ALU.max))
                steps_done.wait()
                dve.tensor_tensor(shift[:, 0], a_d[:], m[:], ALU.subtract).then_inc(shift_ready, 1)
                dve.scalar_tensor_tensor(out=shift[:, 1], in0=a_d[:], scalar=0.2, in1=m[:],
                                         op0=ALU.mult, op1=ALU.subtract).then_inc(shift_ready, 1)
                for r in range(2):
                    dve.wait_ge(turned, r + 1)
                    dve.tensor_copy(rows[:, r, :], tps[0:heads * NT, r, 0:TP]).then_inc(kept, 1)

            @block.tensor
            def _(pe):
                pe.wait_ge(shift_ready, 2)
                for r in range(2):
                    pe.transpose(tps[0:heads * NT, r, 0:TP], shift[:, r].rearrange("p h t -> p (h t)"),
                                 ident[0:TP, 0:TP]).then_inc(turned, 1)


def gat_attend_stage(nc, name, adj, heads, width, h, a_s, a_s02, shift_d, out_d, h_d=None):
    per = width if heads > 1 else 128
    starts = [0] if heads > 1 else list(range(width - per, -1, -per))
    banks = [(0, 3), (3, 3), (6, 3), (9, 1)]
    n_out = heads * len(starts)
    with Stage(nc, name) as S:
        if h is None:
            h = S.sb("h", [TP, NT, heads, width + 1])
        h_ld = [S.sem(f"h_ld{t}") for t in range(NT)] if h_d is not None else None
        sh = S.sb("sh", [TP, min(heads, 2), 2, N])
        e1 = S.sb("e1", [TP, 2, N])
        e2 = S.sb("e2", [TP, 2, N])
        p = S.sb("p", [TP, NT, N])
        den = S.sb("den", [TP, NT])
        rden = S.sb("rden", [TP, NT])
        o = S.sb("o", [TP, 2, NT, per])
        ops = S.ps("ops", [128, 2, 4, 512])
        sh_ld, o_st = [S.sem("sh_ld0"), S.sem("sh_ld1")], [S.sem("o_st0"), S.sem("o_st1")]
        e_done, larger, p_done, p_used = S.sem("e_done"), S.sem("larger"), S.sem("p_done"), S.sem("p_used")
        chain, o_done, o_kept = S.sem("chain"), S.sem("o_done"), S.sem("o_kept")

        def span(k):
            return per + 1 if k == 0 else per

        def loop(eng, body):
            if heads == 1:
                body(0, 0)
            else:
                with eng.Fori(0, heads // 2) as i:
                    for u in range(2):
                        body(i * 2 + u, u)

        with nc.Block() as block:
            @block.sync
            def _(sp):
                for u in range(2):
                    sp.nop().then_inc(o_st[u], 16)

                def load(hd, u):
                    for r in range(2):
                        src = shift_d[r, bass.ds(hd * N, N)]
                        sp.dma_start(sh[:, u, r, :], row_bcast(src, TP)).then_inc(sh_ld[u], 16)

                load(0, 0)
                if h_d is not None:
                    for t in range(NT):
                        sp.dma_start(h[:, t].rearrange("p h w -> p (h w)"), h_d[t * TP:(t + 1) * TP, :]).then_inc(h_ld[t], 16)
                if heads > 1:
                    load(1, 1)

                def store(k, u, c0):
                    sp.dma_start(tokens(out_d)[:, :, bass.ds(c0, per)], o[:, u]).then_inc(o_st[u], 16)

                if heads == 1:
                    for k, c0 in enumerate(starts):
                        sp.wait_ge(o_kept, 4 * (k + 3))
                        store(k, k % 2, c0)
                else:
                    with sp.Fori(0, heads // 2 - 1) as i:
                        for u in range(2):
                            sp.wait_ge(e_done, (i * 2 + u + 1) * 2 * NT)
                            load(i * 2 + u + 2, u)
                            sp.wait_ge(o_kept, (i * 2 + u + 3) * 4)
                            store(i * 2 + u, u, (i * 2 + u) * per)
                    for u in range(2):
                        sp.wait_ge(o_kept, (heads + 1 + u) * 4)
                        store(heads - 2 + u, u, (heads - 2 + u) * per)
                for u in range(2):
                    sp.wait_ge(o_st[u], 16 * (n_out // 2) + 16)

            @block.scalar
            def _(act):
                def body(hd, u):
                    act.wait_ge(sh_ld[u], (hd - u) * 16 + 32)
                    for s in range(NT):
                        act.wait_ge(p_done, hd * NT + s + 1)
                        act.activation(e1[:, s % 2, :], sh[:, u, 0, :], ACT.Exp,
                                       bias=a_s[:, bass.ds(hd, 1), s]).then_inc(e_done, 1)
                        act.activation(e2[:, s % 2, :], sh[:, u, 1, :], ACT.Exp,
                                       bias=a_s02[:, bass.ds(hd, 1), s]).then_inc(e_done, 1)

                loop(act, body)

            @block.vector
            def _(dve):
                dve.nop().then_inc(p_done, 2)
                dve.nop().then_inc(o_kept, 8)

                def normalise(hd, k, u):
                    n = hd * len(starts) + k
                    w = span(k)
                    steps_done = Chain(dve, chain, hd * 5)
                    if heads > 1:
                        dve.wait_ge(p_used, (hd + 2) * NT)
                    else:
                        dve.wait_ge(o_done, n + 1)
                    dve.wait_ge(o_st[u], (n - u) * 8 + 16)
                    got = [ops[0:TP, u, b, 0:tn * w].rearrange("p (t w) -> p t w", t=tn) for b, (_, tn) in enumerate(banks)]
                    if k == 0:
                        for (t0, tn), a in zip(banks, got):
                            steps_done.done(dve.tensor_scalar(den[:, t0:t0 + tn], a[:, :, per], 1e-16, None, ALU.add))
                        steps_done.wait()
                        steps_done.done(dve.reciprocal(rden[:], den[:]))
                        steps_done.wait()
                    for (t0, tn), a in zip(banks, got):
                        dve.tensor_tensor(o[:, u, t0:t0 + tn, :], a[:, :, 0:per],
                                          rden[:, t0:t0 + tn].unsqueeze(2).to_broadcast([TP, tn, per]),
                                          ALU.mult).then_inc(o_kept, 1)

                def weights(hd, before=None):
                    for s in range(NT):
                        if s == 4 and before is not None:
                            normalise(*before)
                        dve.wait_ge(e_done, (hd * NT + s) * 2 + 2)
                        dve.tensor_tensor(e1[:, s % 2, :], e1[:, s % 2, :], e2[:, s % 2, :], ALU.max).then_inc(larger, 1)
                        dve.wait_ge(p_used, hd * NT + s + 1)
                        dve.wait_ge(larger, hd * NT + s + 1)
                        dve.scalar_tensor_tensor(out=p[:, s, :], in0=e1[:, s % 2, :], scalar=1.0, in1=adj[:, s, :],
                                                 op0=ALU.min, op1=ALU.mult).then_inc(p_done, 1)

                weights(0)
                if heads == 1:
                    for k in range(len(starts)):
                        normalise(0, k, k % 2)
                else:
                    with dve.Fori(0, heads // 2 - 1) as i:
                        for u in range(2):
                            weights(i * 2 + u + 1, (i * 2 + u, 0, u))
                    weights(heads - 1, (heads - 2, 0, 0))
                    normalise(heads - 1, 0, 1)

            @block.tensor
            def _(pe):
                def block_sums(hd, k, c0, u):
                    n = hd * len(starts) + k
                    w = span(k)
                    if heads > 1:
                        pe.wait_ge(o_kept, (n - u) * 4 + 4 * u + 4)
                    elif k >= 2:
                        pe.wait_ge(o_kept, (k + 1) * 4)
                    for s in range(NT):
                        pe.wait_ge(p_done, hd * NT + s + 3)
                        if h_d is not None:
                            pe.wait_ge(h_ld[s], 16)
                        rhs = h[:, s, bass.ds(hd, 1), c0:c0 + w]
                        for b, (t0, tn) in enumerate(banks):
                            for t in range(tn):
                                ins = pe.matmul(ops[0:TP, u, b, t * w:(t + 1) * w],
                                                p[:, s, (t0 + t) * TP:(t0 + t + 1) * TP], rhs,
                                                start=(s == 0 and t == 0), stop=(s == NT - 1), skip_group_check=True)
                        if heads > 1:
                            ins.then_inc(p_used, 1)
                    if heads == 1:
                        ins.then_inc(o_done, 1)

                def body(hd, u):
                    for k, c0 in enumerate(starts):
                        block_sums(hd, k, c0, u if heads > 1 else k % 2)

                pe.nop().then_inc(p_used, NT)
                loop(pe, body)


def router_stage(nc, ident, xT, p_d, c_d, w1_d, b1_d, z_parts_d, w1_parts_d, b1_parts_d, w_parts_d, wT):
    sm = ES * EM
    with Stage(nc, "router") as S:
        pw = S.sb("pw", [128, KB, 128])
        cb = S.sb("cb", [128, sm])
        zT = S.sb("zT", [128, N])
        zp = S.sb("zp", [128, 3, N], BF16)
        raw = S.sb("raw", [TP, 2, 2, ES, EM])
        e = S.sb("e", [TP, 2, 2, ES, EM])
        top = S.sb("top", [TP, 2, ES, 8])
        tot = S.sb("tot", [TP, ES])
        rtot = S.sb("rtot", [TP, ES])
        wgt = S.sb("wgt", [TP, 2, sm])
        w16 = S.sb("w16", [128, 2, 4, N], F16)
        rest = S.sb("rest", [128, 4, N])
        w1 = S.sb("w1", [128, EM * EH])
        w1p = S.sb("w1p", [128, 3, EM * EH], BF16)
        b1 = S.sb("b1", [ES, EM * EH])
        b1p = S.sb("b1p", [ES, 3, EM * EH], BF16)
        zps = S.ps("zps", [128, 1536])
        sps = S.ps("sps", [128, 2, 512])
        wps = S.ps("wps", [128, 2, 512])
        p_ld, c_ld, w1_ld, b1_ld, cb_zero = (S.sem(s) for s in ("p_ld", "c_ld", "w1_ld", "b1_ld", "cb_zero"))
        z_done, z_kept, s_done, s_kept = (S.sem(s) for s in ("z_done", "z_kept", "s_done", "s_kept"))
        diff, exp_done, chosen, turned, w_kept = (S.sem(s) for s in ("diff", "exp_done", "chosen", "turned", "w_kept"))
        chain, z_split, w_split, w1_split, b1_split, stored, pchain = (S.sem(s) for s in (
            "chain", "z_split", "w_split", "w1_split", "b1_split", "stored", "pchain"))
        with nc.Block() as block:
            @block.sync
            def _(sp):
                sp.dma_start(pw[:], kblocks(p_d)).then_inc(p_ld, 16)
                sp.wait_ge(cb_zero, 1)
                for s in range(ES):
                    sp.dma_start(cb[s * ER:(s + 1) * ER, s * EM:(s + 1) * EM], c_d[s]).then_inc(c_ld, 16)
                sp.dma_start(w1[:], w1_d.rearrange("s r n -> (s r) n")).then_inc(w1_ld, 16)
                sp.dma_start(b1[:], b1_d).then_inc(b1_ld, 16)
                sp.wait_ge(z_split, 3)
                sp.dma_start(z_parts_d.rearrange("k p n -> p k n"), zp[:]).then_inc(stored, 16)
                sp.wait_ge(w1_split, 3)
                sp.dma_start(w1_parts_d.rearrange("k p n -> p k n"), w1p[:]).then_inc(stored, 16)
                sp.wait_ge(b1_split, 3)
                sp.dma_start(b1_parts_d.rearrange("k p n -> p k n"), b1p[:]).then_inc(stored, 16)
                sp.wait_ge(w_split, 2)
                to = w_parts_d.rearrange("(b two) (k m) n -> two k m b n", two=2, k=2)
                for two in range(2):
                    for k in range(2):
                        sp.dma_start(to[two, k], w16[two * EM:(two + 1) * EM, k]).then_inc(stored, 16)
                sp.wait_ge(stored, 16 * 7)

            @block.gpsimd
            def _(pool):
                steps_done = Chain(pool, pchain)
                for src, parts, ld, split in ((w1, w1p, w1_ld, w1_split), (b1, b1p, b1_ld, b1_split)):
                    pool.wait_ge(ld, 16)
                    for k in range(3):
                        nc.gpsimd.tensor_copy(parts[:, k, :], src[:]).then_inc(split, 1)
                        pool.wait_ge(split, k + 1)
                        if k < 2:
                            steps_done.done(nc.gpsimd.tensor_tensor(src[:], src[:], parts[:, k, :], ALU.subtract))
                            steps_done.wait()

            @block.tensor
            def _(pe):
                pe.wait_ge(p_ld, 16)
                for c0, cn in CHUNKS:
                    for kb in range(KB):
                        ins = pe.matmul(zps[:, c0:c0 + cn], pw[:, kb, :], xT[:, kb, c0:c0 + cn],
                                        start=(kb == 0), stop=(kb == KB - 1))
                ins.then_inc(z_done, 1)
                pe.wait_ge(z_kept, 1)
                pe.wait_ge(c_ld, 16 * ES)

                def scores(t):
                    if t >= 2:
                        pe.wait_ge(s_kept, t - 1)
                    pe.matmul(sps[0:TP, t % 2, :], zT[:, t * TP:(t + 1) * TP], cb[:], start=True, stop=True).then_inc(s_done, 1)

                scores(0)
                for t in range(NT):
                    if t + 1 < NT:
                        scores(t + 1)
                    pe.wait_ge(chosen, t + 1)
                    if t >= 2:
                        pe.wait_ge(w_kept, t - 1)
                    for b in range(4):
                        ins = pe.transpose(wps[:, t % 2, b * 128:b * 128 + TP], wgt[:, t % 2, b * 128:(b + 1) * 128],
                                           ident[0:TP, 0:TP])
                    ins.then_inc(turned, 1)

            @block.scalar
            def _(act):
                act.wait_ge(z_done, 1)
                act.copy(zT[:], zps[:, 0:N]).then_inc(z_kept, 1)

                def keep_scores(t):
                    act.wait_ge(s_done, t + 1)
                    if t >= 2:
                        act.wait_ge(exp_done, t - 1)
                    act.copy(raw[:, t % 2, 0].rearrange("p s m -> p (s m)"), sps[0:TP, t % 2, :]).then_inc(s_kept, 1)

                keep_scores(0)
                for t in range(NT):
                    if t + 1 < NT:
                        keep_scores(t + 1)
                    act.wait_ge(diff, 2 * t + 2)
                    if t >= 2:
                        act.wait_ge(chosen, t - 1)
                    act.activation(e[:, t % 2], raw[:, t % 2], ACT.Exp).then_inc(exp_done, 1)
                    act.wait_ge(turned, t + 1)
                    act.copy(wT[:, :, t * TP:(t + 1) * TP],
                             wps[:, t % 2, :].rearrange("p (b n) -> p b n", b=4)[:, :, 0:TP]).then_inc(w_kept, 1)

            @block.vector
            def _(dve):
                steps_done = Chain(dve, chain)
                dve.memset(cb[:], 0.0).then_inc(cb_zero, 1)
                dve.wait_ge(z_kept, 1)
                for t in range(NT):
                    u = t % 2
                    sc, less = raw[:, u, 0], raw[:, u, 1]
                    dve.wait_ge(s_kept, t + 1)
                    for s in range(ES):
                        steps_done.done(dve.max(top[:, u, s, :], sc[:, s, :]))
                    steps_done.wait()
                    steps_done.done(dve.memset(top[:, u, :, 4:8], -NEG))
                    steps_done.wait()
                    for s in range(ES):
                        steps_done.done(dve.match_replace(less[:, s, :], top[:, u, s, :], sc[:, s, :], NEG))
                    steps_done.wait()
                    best = top[:, u, :, 0:1].to_broadcast([TP, ES, EM])
                    for k in range(2):
                        dve.tensor_tensor(raw[:, u, k], raw[:, u, k], best, ALU.subtract).then_inc(diff, 1)
                    dve.wait_ge(exp_done, t + 1)
                    steps_done.done(dve.tensor_tensor(e[:, u, 0], e[:, u, 0], e[:, u, 1], ALU.subtract))
                    steps_done.wait()
                    steps_done.done(dve.tensor_reduce(tot[:], e[:, u, 0], AX.X, ALU.add))
                    steps_done.wait()
                    steps_done.done(dve.reciprocal(rtot[:], tot[:]))
                    steps_done.wait()
                    if t >= 2:
                        dve.wait_ge(turned, t - 1)
                    dve.tensor_tensor(wgt[:, u, :].rearrange("p (s m) -> p s m", s=ES), e[:, u, 0],
                                      rtot[:].unsqueeze(2).to_broadcast([TP, ES, EM]), ALU.mult).then_inc(chosen, 1)
                dve.wait_ge(s_done, NT)
                for k in range(3):
                    dve.tensor_copy(zp[:, k, :], zT[:]).then_inc(z_split, 1)
                    dve.wait_ge(z_split, k + 1)
                    if k < 2:
                        steps_done.done(dve.tensor_tensor(zT[:], zT[:], zp[:, k, :], ALU.subtract))
                        steps_done.wait()
                dve.wait_ge(w_kept, NT)
                dve.tensor_copy(w16[:, 0], wT[:]).then_inc(w_split, 1)
                dve.wait_ge(w_split, 1)
                steps_done.done(dve.tensor_tensor(rest[:], wT[:], w16[:, 0], ALU.subtract))
                steps_done.wait()
                dve.tensor_scalar(w16[:, 1], rest[:], 4096.0, None, ALU.mult).then_inc(w_split, 1)


def expert_stage(nc, z_parts_d, w1_parts_d, b1_parts_d, w_parts_d, spread_d, w2_d, b2_d, wT, comb_d):
    chunk = [(0, 417), (417, 417), (834, 416)]
    per_chunk = EJ
    steps = 3 * per_chunk
    W = 2 * EG
    with Stage(nc, "expert") as S:
        z = S.sb("z", [128, 2, N], BF16)
        w1 = S.sb("w1", [128, 2, EM * EH], BF16)
        wp = S.sb("wp", [128, 2, N], F16)
        spread = S.sb("spread", [128, EJ, 128], F16)
        w2 = S.sb("w2", [128, 2, EJ + 1, ER])
        b2 = S.sb("b2", [128, 2, 32])
        gel = S.sb("gel", [128, 3, 512])
        wgel = S.sb("wgel", [128, W, 512])
        comb = S.sb("comb", [128, 2, N])
        hps = S.ps("hps", [128, 3, 512])
        wps = S.ps("wps", [128, 3, 512])
        cps = S.ps("cps", [128, 2, 512])
        in_ld, stored = [S.sem("in_ld0"), S.sem("in_ld1")], [S.sem("stored0"), S.sem("stored1")]
        spread_ld, const_set = S.sem("spread_ld"), S.sem("const_set")
        h_done, w_done, gel_done, wgel_done, w2_done, comb_kept = (S.sem(s) for s in (
            "h_done", "w_done", "gel_done", "wgel_done", "w2_done", "comb_kept"))
        n_in = len(NPART) * 2 + 3 + 3

        def at(q):
            u, c, j = q // steps, q % steps // per_chunk, q % per_chunk
            return u, c, 3 * u + c, j, chunk[c][0], chunk[c][1]

        with nc.Block() as block:
            @block.sync
            def _(sp):
                for u in range(2):
                    sp.nop().then_inc(stored[u], 16 * EG)
                sp.dma_start(spread[:], spread_d.rearrange("p (j n) -> p j n", j=EJ)).then_inc(spread_ld, 16)
                sp.wait_ge(const_set, 7)

                def load(s, u):
                    rows = bass.ds(s * ER, ER)
                    for k, (a, b) in enumerate(NPART):
                        sp.dma_start(z[k * ER:(k + 1) * ER, u, :], z_parts_d[a, rows, :]).then_inc(in_ld[u], 16)
                        sp.dma_start(w1[k * ER:(k + 1) * ER, u, :], w1_parts_d[b, rows, :]).then_inc(in_ld[u], 16)
                    for k in range(3):
                        sp.dma_start(w1[len(NPART) * ER + k:len(NPART) * ER + k + 1, u, :],
                                     b1_parts_d[k, bass.ds(s, 1), :]).then_inc(in_ld[u], 16)
                    sp.dma_start(wp[:, u, :], w_parts_d[bass.ds(s, 1), :, :].rearrange("a p n -> (a p) n")).then_inc(in_ld[u], 16)
                    sp.dma_start(w2[:, u, 0:EJ, :], w2_d[bass.ds(s, 1)].rearrange("a p j r -> (a p) j r")).then_inc(in_ld[u], 16)
                    sp.dma_start(b2[u * EM:(u + 1) * EM, u, 0:ER],
                                 b2_d[bass.ds(s, 1)].rearrange("a m r -> (a m) r")).then_inc(in_ld[u], 16)

                def store(s, u):
                    for e in range(EG):
                        sp.dma_start(comb_d[e, bass.ds(s * ER, ER), :], comb[32 * e:32 * e + ER, u, :]).then_inc(stored[u], 16)

                load(0, 0)
                load(1, 1)
                with sp.Fori(0, ES // 2 - 1) as i:
                    for u in range(2):
                        sp.wait_ge(w2_done, i * 2 * steps + (u + 1) * steps + W)
                        load(i * 2 + u + 2, u)
                        sp.wait_ge(comb_kept, i * 6 + 3 * u + 5)
                        store(i * 2 + u, u)
                for u in range(2):
                    sp.wait_ge(comb_kept, 3 * (ES - 1 + u) + 2)
                    store(ES - 2 + u, u)
                for u in range(2):
                    sp.wait_ge(stored[u], 16 * EG * (ES // 2) + 16 * EG)

            @block.tensor
            def _(pe):
                pe.wait_ge(spread_ld, 16)
                pe.wait_ge(const_set, 7)
                pe.nop().then_inc(w2_done, W)
                with pe.Fori(0, ES // 2) as i:
                    base = i * (2 * steps)

                    def hidden(q):
                        u, c, ch, j, c0, cn = at(q)
                        if q % steps == 0:
                            pe.wait_ge(in_ld[u], i * 16 * n_in + 16 * n_in)
                        pe.wait_ge(gel_done, base + q + 1)
                        pe.matmul(hps[:, q % 3, 0:cn], w1[0:ZK, u, j * 128:(j + 1) * 128], z[0:ZK, u, c0:c0 + cn],
                                  start=True, stop=True).then_inc(h_done, 1)
                        pe.wait_ge(wgel_done, base + q + 1)
                        pe.matmul(wps[:, q % 3, 0:cn], spread[:, j, :], wp[:, u, c0:c0 + cn],
                                  start=True, stop=True).then_inc(w_done, 1)

                    for q in range(EG):
                        hidden(q)
                    for q0 in range(0, 2 * steps, EG):
                        u, c, ch, j0, c0, cn = at(q0)
                        if j0 == 0:
                            pe.wait_ge(comb_kept, i * 6 + ch + 1)
                        for q in range(q0 + EG, min(q0 + 2 * EG, 2 * steps)):
                            hidden(q)
                        if j0 == 0:
                            pe.matmul(cps[0:32, ch % 2, 0:cn], b2[:, u, :], wT[:, bass.ds(i, 1), c0:c0 + cn],
                                      start=True, stop=False, tile_position=(0, 0), skip_group_check=True)
                        pe.wait_ge(wgel_done, base + q0 + EG + 3)
                        for e in range(EG):
                            j = j0 + e
                            pe.matmul(cps[32 * e:32 * e + 32, ch % 2, 0:cn],
                                      w2[:, u, j:j + 2, :].rearrange("p j r -> p (j r)"), wgel[:, (q0 + e) % W, 0:cn],
                                      start=(j0 == 0 and e > 0), stop=(j0 + EG == EJ), tile_position=(0, 32 * e),
                                      skip_group_check=True).then_inc(w2_done, 1)

            @block.scalar
            def _(act):
                act.nop().then_inc(gel_done, 3)
                with act.Fori(0, ES // 2) as i:
                    base = i * (2 * steps)
                    for q in range(2 * steps):
                        u, c, ch, j, c0, cn = at(q)
                        act.wait_ge(h_done, base + q + 1)
                        act.wait_ge(wgel_done, base + q + 1)
                        act.activation(gel[:, q % 3, 0:cn], hps[:, q % 3, 0:cn], ACT.Gelu_apprx_tanh).then_inc(gel_done, 1)

            @block.vector
            def _(dve):
                dve.nop().then_inc(wgel_done, 3)
                dve.nop().then_inc(comb_kept, 2)
                for u in range(2):
                    dve.memset(z[len(NPART) * ER:ZK, u, :], 1.0).then_inc(const_set, 1)
                    dve.memset(b2[(1 - u) * EM:(2 - u) * EM, u, 0:ER], 0.0).then_inc(const_set, 1)
                    dve.memset(b2[:, u, ER:32], 0.0).then_inc(const_set, 1)
                dve.memset(w2[:, :, EJ, :], 0.0).then_inc(const_set, 1)
                with dve.Fori(0, ES // 2) as i:
                    base = i * (2 * steps)

                    def keep_sums(ch):
                        u, c = ch // 3, ch % 3
                        c0, cn = chunk[c]
                        if c == 0:
                            dve.wait_ge(stored[u], i * 16 * EG + 16 * EG)
                        dve.wait_ge(w2_done, base + (ch + 1) * per_chunk + W)
                        dve.tensor_copy(comb[:, u, c0:c0 + cn], cps[:, ch % 2, 0:cn]).then_inc(comb_kept, 1)

                    for q in range(2 * steps):
                        u, c, ch, j, c0, cn = at(q)
                        if ch and j == 2 * EG:
                            keep_sums(ch - 1)
                        dve.wait_ge(gel_done, base + q + 4)
                        dve.wait_ge(w_done, base + q + 1)
                        if q % EG == 0:
                            dve.wait_ge(w2_done, base + q + EG)
                        dve.tensor_tensor(wgel[:, q % W, 0:cn], gel[:, q % 3, 0:cn], wps[:, q % 3, 0:cn],
                                          ALU.mult).then_inc(wgel_done, 1)
                    keep_sums(5)


def comb_stage(nc, comb_d, combT):
    with Stage(nc, "comb") as S:
        part = S.sb("part", [128, EG, N])
        part_ld, chain = [S.sem(f"part_ld{e}") for e in range(EG)], S.sem("chain")
        with nc.Block() as block:
            @block.sync
            def _(sp):
                for e in range(EG):
                    sp.dma_start(part[:, e, :], comb_d[e]).then_inc(part_ld[e], 16)

            @block.vector
            def _(dve):
                steps_done = Chain(dve, chain)
                dve.wait_ge(part_ld[0], 16)
                for e in range(1, EG):
                    dve.wait_ge(part_ld[e], 16)
                    if e > 1:
                        steps_done.wait()
                    steps_done.done(dve.tensor_tensor(combT[:], part[:, 0, :] if e == 1 else combT[:], part[:, e, :], ALU.add))


def load_rows_stage(nc, name, src_d, to):
    with Stage(nc, name) as S:
        loaded = S.sem("loaded")
        with nc.Block() as block:
            @block.sync
            def _(sp):
                sp.dma_start(to, src_d).then_inc(loaded, 16)
                sp.wait_ge(loaded, 16)


def bitlinear_stage(nc, ident, x_d, add_d, bias_d, win_d, wout_d, gin_d, gout_d, out_d):
    H = wout_d.shape[0]
    ROUND = 1.5 * 2.0 ** 23
    layers = ((win_d, KB, 2 * H), (wout_d, H // 128, D))
    with Stage(nc, "bit") as S:
        x = S.sb("x", [TP, NT, D])
        xn = S.sb("xn", [TP, NT, D])
        y = S.sb("y", [TP, NT, H])
        bias = S.sb("bias", [TP, D])
        gin = S.sb("gin", [TP, D])
        gout = S.sb("gout", [TP, H])
        win = S.sb("win", [128, KB, 2 * H])
        wout = S.sb("wout", [128, H // 128, D])
        winq = S.sb("winq", [128, KB, 2 * H], BF16)
        woutq = S.sb("woutq", [128, H // 128, D], BF16)
        stats = S.sb("stats", [TP, NT, 2, 6])
        mv = S.sb("mv", [TP, NT, 2])
        ssq = S.sb("ssq", [TP, 2, NT])
        std = S.sb("std", [TP, 3, NT])
        rstd = S.sb("rstd", [TP, 3, NT])
        epst = S.sb("epst", [128, 2])
        junk = S.sb("junk", [TP, 2, D])
        big = S.sb("big", [TP, 2, 2, NT])
        amax = S.sb("amax", [TP, 2, NT])
        ascale = S.sb("ascale", [TP, 2, NT])
        back = S.sb("back", [TP, 2, NT])
        wabs = S.sb("wabs", [128, 2])
        wmean = S.sb("wmean", [128, 2])
        wscale = S.sb("wscale", [128, 2])
        ones = S.sb("ones", [128, 128])
        identb = S.sb("identb", [128, 128], BF16)
        q = S.sb("q", [TP, 2, D], BF16)
        qT = S.sb("qT", [128, 2, KB, TP], BF16)
        sig = S.sb("sig", [TP, 2, H])
        tps = S.ps("tps", [128, 2, 1024], BF16)
        ups = S.ps("ups", [128, 2, 1024])
        mps = S.ps("mps", [128, 2])
        x_ld, add_ld, g_ld, w_ld, const_set = (S.sem(s) for s in ("x_ld", "add_ld", "g_ld", "w_ld", "const_set"))
        chain, x_ready, var_ready, std_ready, wsum_done, wmean_done, w_ready = (S.sem(s) for s in (
            "chain", "x_ready", "var_ready", "std_ready", "wsum_done", "wmean_done", "w_ready"))
        normed, sq_done, q_ready, turned, kept, up_done = (S.sem(s) for s in (
            "normed", "sq_done", "q_ready", "turned", "kept", "up_done"))
        sig_done, out_ready, stored, y_ready = (S.sem(s) for s in ("sig_done", "out_ready", "stored", "y_ready"))
        with nc.Block() as block:
            @block.sync
            def _(sp):
                sp.dma_start(win[:], kblocks(win_d)).then_inc(w_ld, 16)
                sp.dma_start(wout[:], kblocks(wout_d)).then_inc(w_ld, 16)
                sp.dma_start(x[:], tokens(x_d)).then_inc(x_ld, 16)
                sp.dma_start(xn[:], tokens(add_d)).then_inc(add_ld, 16)
                sp.dma_start(bias[:], row_bcast(bias_d, TP)).then_inc(add_ld, 16)
                sp.dma_start(gin[:], row_bcast(gin_d, TP)).then_inc(g_ld, 16)
                sp.dma_start(gout[:], row_bcast(gout_d, TP)).then_inc(g_ld, 16)
                for t in range(NT):
                    sp.wait_ge(out_ready, t + 1)
                    sp.dma_start(out_d[t * TP:(t + 1) * TP, :], x[:, t, :]).then_inc(stored, 16)
                sp.wait_ge(stored, 16 * NT)

            @block.tensor
            def _(pe):
                pe.wait_ge(const_set, 4)
                pe.wait_ge(wsum_done, 2)
                pe.matmul(mps[:, 0:2], ones[:], wabs[:], start=True, stop=True).then_inc(wmean_done, 1)
                pe.wait_ge(w_ready, 2)
                for r, wq in enumerate((winq, woutq)):
                    kb_n, cols = layers[r][1], layers[r][2]
                    cs = cols // 2
                    for t in range(NT):
                        n = r * NT + t
                        pe.wait_ge(q_ready, n + 1)
                        if n >= 2:
                            pe.wait_ge(kept, n - 1)
                        for kb in range(kb_n):
                            ins = pe.transpose(tps[:, n % 2, kb * 128:kb * 128 + TP], q[:, n % 2, kb * 128:(kb + 1) * 128],
                                               identb[0:TP, 0:TP])
                        ins.then_inc(turned, 1)
                        pe.wait_ge(kept, n + 1)
                        if n >= 2 and n - 2 < NT:
                            pe.wait_ge(y_ready, n - 1)
                        elif n >= 2:
                            pe.wait_ge(out_ready, n - 1 - NT)
                        for c in range(2):
                            for kb in range(kb_n):
                                ins = pe.matmul(ups[0:TP, n % 2, c * 512:c * 512 + cs], qT[:, n % 2, kb, :],
                                                wq[:, kb, c * cs:(c + 1) * cs], start=(kb == 0), stop=(kb == kb_n - 1))
                        ins.then_inc(up_done, 1)

            @block.scalar
            def _(act):
                act.wait_ge(const_set, 4)
                act.wait_ge(var_ready, NT)
                act.activation(std[:, 0, :], mv[:, :, 1], ACT.Sqrt, bias=epst[0:TP, 0:1]).then_inc(std_ready, 1)
                for r in range(2):
                    width = (D, H)[r]
                    for t in range(NT):
                        act.wait_ge(normed if r == 0 else y_ready, t + 1)
                        act.activation(junk[:, r, 0:width], xn[:, t, :] if r == 0 else y[:, t, :], ACT.Square,
                                       accum_out=ssq[:, r, t:t + 1]).then_inc(sq_done, 1)
                        act.wait_ge(sq_done, r * NT + t + 1)
                    act.activation(std[:, 1 + r, :], ssq[:, r, :], ACT.Sqrt, bias=epst[0:TP, 1:2],
                                   scale=1.0 / width).then_inc(std_ready, 1)
                    kb_n = layers[r][1]
                    for t in range(NT):
                        n = r * NT + t
                        act.wait_ge(turned, n + 1)
                        if n >= 2:
                            act.wait_ge(up_done, n - 1)
                        act.copy(qT[:, n % 2, 0:kb_n, :],
                                 tps[:, n % 2, 0:kb_n * 128].rearrange("p (kb n) -> p kb n", kb=kb_n)[:, :, 0:TP]).then_inc(kept, 1)
                        if r == 0:
                            act.wait_ge(up_done, n + 1)
                            if t >= 2:
                                act.wait_ge(y_ready, t - 1)
                            act.activation(sig[:, t % 2, :], ups[0:TP, n % 2, 512:512 + H], ACT.Silu,
                                           scale=back[:, 0, t:t + 1]).then_inc(sig_done, 1)

            @block.vector
            def _(dve):
                steps_done = Chain(dve, chain)
                dve.memset(epst[:, 0:1], 1e-5).then_inc(const_set, 1)
                dve.memset(epst[:, 1:2], 1e-6).then_inc(const_set, 1)
                dve.memset(ones[:], 1.0).then_inc(const_set, 1)
                dve.tensor_copy(identb[:], ident[:]).then_inc(const_set, 1)
                dve.wait_ge(w_ld, 32)
                for k, wt in enumerate((win, wout)):
                    dve.tensor_reduce(wabs[:, k:k + 1], wt[:], AX.XY, ALU.add, apply_absolute_value=True).then_inc(wsum_done, 1)
                dve.wait_ge(wmean_done, 1)
                for k, (_, kb_n, cols) in enumerate(layers):
                    steps_done.done(dve.tensor_scalar(wmean[:, k:k + 1], mps[:, k:k + 1], 1.0 / (kb_n * 128 * cols), 1e-5,
                                                      ALU.mult, ALU.max))
                steps_done.wait()
                steps_done.done(dve.reciprocal(wscale[:], wmean[:]))
                steps_done.wait()
                for k, (wt, wq) in enumerate(((win, winq), (wout, woutq))):
                    steps_done.done(dve.tensor_scalar(wt[:], wt[:], wscale[:, k:k + 1], ROUND, ALU.mult, ALU.add))
                    steps_done.wait()
                    steps_done.done(dve.tensor_scalar(wt[:], wt[:], ROUND, 1.0, ALU.subtract, ALU.min))
                    steps_done.wait()
                    dve.tensor_scalar(wq[:], wt[:], -1.0, None, ALU.max).then_inc(w_ready, 1)
                dve.wait_ge(x_ld, 16)
                dve.wait_ge(add_ld, 32)
                for t in range(NT):
                    steps_done.done(dve.tensor_tensor(xn[:, t, :], xn[:, t, :], bias[:], ALU.add))
                    steps_done.wait()
                    dve.tensor_tensor(x[:, t, :], x[:, t, :], xn[:, t, :], ALU.add).then_inc(x_ready, 1)
                    dve.wait_ge(x_ready, t + 1)
                    for k in range(2):
                        steps_done.done(dve.bn_stats(stats[:, t, k, :], x[:, t, k * 384:(k + 1) * 384]))
                    steps_done.wait()
                    dve.bn_aggr(mv[:, t, :], stats[:, t, :, :]).then_inc(var_ready, 1)
                dve.wait_ge(std_ready, 1)
                steps_done.done(dve.reciprocal(rstd[:, 0, :], std[:, 0, :]))
                steps_done.wait()
                dve.wait_ge(var_ready, NT)
                for t in range(NT):
                    dve.tensor_scalar(xn[:, t, :], x[:, t, :], mv[:, t, 0:1], rstd[:, 0, t:t + 1],
                                      ALU.subtract, ALU.mult).then_inc(normed, 1)
                dve.wait_ge(normed, NT)
                dve.wait_ge(g_ld, 32)
                for r in range(2):
                    rows, gain = ((xn, gin), (y, gout))[r]
                    width = (D, H)[r]
                    dve.wait_ge(std_ready, 2 + r)
                    steps_done.done(dve.reciprocal(rstd[:, 1 + r, :], std[:, 1 + r, :]))
                    steps_done.wait()
                    for t in range(NT):
                        steps_done.done(dve.scalar_tensor_tensor(out=rows[:, t, :], in0=rows[:, t, :],
                                                                 scalar=rstd[:, 1 + r, t:t + 1], in1=gain[:],
                                                                 op0=ALU.mult, op1=ALU.mult))
                    steps_done.wait()
                    steps_done.done(dve.tensor_reduce(amax[:, r, :], rows[:], AX.X, ALU.max, apply_absolute_value=True))
                    steps_done.wait()
                    steps_done.done(dve.tensor_scalar(amax[:, r, :], amax[:, r, :], 1e-5, None, ALU.max))
                    steps_done.wait()
                    steps_done.done(dve.reciprocal(ascale[:, r, :], amax[:, r, :]))
                    steps_done.done(dve.tensor_scalar(back[:, r, :], amax[:, r, :], wmean[0:TP, r:r + 1], 1.0 / 127.0,
                                                      ALU.mult, ALU.mult))
                    steps_done.wait()
                    steps_done.done(dve.tensor_scalar(ascale[:, r, :], ascale[:, r, :], 127.0, None, ALU.mult))
                    steps_done.wait()

                    def read_product(t):
                        n = r * NT + t
                        if r == 0:
                            dve.wait_ge(sig_done, t + 1)
                            ins = dve.scalar_tensor_tensor(out=y[:, t, :], in0=ups[0:TP, n % 2, 0:H],
                                                           scalar=back[:, 0, t:t + 1], in1=sig[:, t % 2, :],
                                                           op0=ALU.mult, op1=ALU.mult)
                            ins.then_inc(y_ready, 1)
                        else:
                            dve.wait_ge(up_done, n + 1)
                            got = ups[0:TP, n % 2, :].rearrange("p (c n) -> p c n", c=2)[:, :, 0:D // 2]
                            both = x[:, t, :].rearrange("p (c n) -> p c n", c=2)
                            dve.scalar_tensor_tensor(out=both, in0=got, scalar=back[:, 1, t:t + 1], in1=both,
                                                     op0=ALU.mult, op1=ALU.add).then_inc(out_ready, 1)

                    for t in range(NT):
                        n = r * NT + t
                        steps_done.done(dve.tensor_scalar(rows[:, t, :], rows[:, t, :], ascale[:, r, t:t + 1], ROUND,
                                                          ALU.mult, ALU.add))
                        steps_done.wait()
                        steps_done.done(dve.tensor_scalar(rows[:, t, :], rows[:, t, :], ROUND, 127.0, ALU.subtract, ALU.min))
                        steps_done.wait()
                        if n >= 2:
                            dve.wait_ge(turned, n - 1)
                        dve.tensor_scalar(q[:, n % 2, 0:width], rows[:, t, :], -128.0, None, ALU.max).then_inc(q_ready, 1)
                        if t:
                            read_product(t - 1)
                    read_product(NT - 1)


def gat_one_head(nc, name, ident, x_d, k, act_kind, bias_d, w_d, asrc_d, adst_d, counts, mask_d, rows_d, shift_d,
                 a_s, a_d, a_s02, mx, out_d):
    one = [buf[:, 0:1, :] for buf in (a_s, a_d, mx, a_s02)]
    with nc.sbuf_tensor(f"{name}_h", [TP, NT, 1, D + 1], F32) as h:
        with nc.sbuf_tensor(f"{name}_mask", [TP, NT, N], BF16) as mask:
            gat_project_stage(nc, f"{name}proj", ident, x_d, k, act_kind, bias_d, w_d, 1, D, asrc_d, adst_d, h,
                              one[0], one[1], rows_d, ahead=[(mask[:], tokens(mask_d))])
            gat_shift_stage(nc, f"{name}max", ident, 1, *one, shift_d, scan=(mask, rows_d, 1, one[2]))
        gat_attend_stage(nc, f"{name}att", counts, 1, D, h, one[0], one[3], shift_d, out_d)


def gps_two_layers(nc, inp, out_d):
    def dram(name, shape, dt=F32):
        return nc.dram_tensor(name, shape, dt).ap()

    xn_d, attn_d, sum_d, x1_d, x2_d = (dram(s, [N, D]) for s in ("xn_d", "attn_d", "sum_d", "x1_d", "x2_d"))
    counts_d = dram("counts_d", [N, N], I16)
    h0_d, h1_d = dram("h0_d", [N, 8 * 129]), dram("h1_d", [N, 8 * 97])
    adj_flat = dram("adj_d", [N * N + EXTRA])
    adj_d = adj_flat[0:N * N].rearrange("(s d) -> s d", d=N)
    mask_d = dram("mask_d", [N, N], BF16)
    g1a_d, g1b_d, g2_d = dram("g1a_d", [N, 1024]), dram("g1b_d", [N, D]), dram("g2_d", [N, D])
    rows_d, shift_d = dram("rows_d", [8 * N]), dram("shift_d", [2, 8 * N])
    z_parts_d = dram("z_parts_d", [3, 128, N], BF16)
    w1_parts_d = dram("w1_parts_d", [3, 128, EM * EH], BF16)
    b1_parts_d = dram("b1_parts_d", [3, ES, EM * EH], BF16)
    w_parts_d = dram("w_parts_d", [ES, 2 * EM, N], F16)
    comb_d = dram("comb_d", [EG, ES * ER, N])

    def sb(ctx, name, shape, dt=F32, side="left"):
        return ctx.enter_context(nc.sbuf_tensor(name, shape, dt, side=side))

    def high_low(ctx, name):
        return sb(ctx, f"{name}_hi", [128, KB, N], F32R), sb(ctx, f"{name}_lo", [128, KB, N], F32R)

    with ExitStack() as top:
        ident = sb(top, "ident", [128, 128])
        a_s, a_d, a_s02, mx = (sb(top, s, [TP, 8, NT]) for s in ("a_s", "a_d", "a_s02", "mx"))
        load_rows_stage(nc, "ident", inp["ident"], ident[:])

        with ExitStack() as ctx:
            key_off = sb(ctx, "key_off", [TP, EC], I32)
            key_val = sb(ctx, "key_val", [TP, EC])
            edge_stage(nc, ident, inp["src"], inp["dst"], inp["lower"], key_off, key_val, adj_flat)
            yT = sb(ctx, "yT0", [128, KB, N])
            norm_stage(nc, "ln0", ident, 1e-5, inp["x"], None, None, None, xn_d,
                       inp["L0_mix_ln1_g"], inp["L0_mix_ln1_b"], yT)
            performer_stage(nc, "perf0", yT, inp["L0_mix_qkv_w"], inp["L0_mix_qkv_b"], inp["L0_mix_v_b"],
                            inp["L0_mix_w_orf"], True, 384, HD ** -0.25, 1e-8, attn_d,
                            edges=(key_off, key_val, adj_flat.rearrange("(n a) -> n a", a=1)))
        mask_stage(nc, ident, adj_d, mask_d, counts_d)
        gat_project_stage(nc, "gat00proj", ident, xn_d, D, None, None, inp["L0_gnn_W1"], 8, 128,
                          inp["L0_gnn_att_src1"], inp["L0_gnn_att_dst1"], None, a_s, a_d, rows_d, h_d=h0_d)
        with ExitStack() as graph:
            with ExitStack() as mlp:
                with ExitStack() as ctx:
                    parts = high_low(ctx, "y")
                    proj_stage(nc, "proj0", ident, attn_d, inp["L0_mix_proj_w"], inp["L0_mix_proj_b"], xn_d, inp["x"], sum_d,
                               1e-5, inp["L0_mix_ln2_g"], inp["L0_mix_ln2_b"], parts)
                    hidden = sb(mlp, "hidden", [128, 4 * KB, N], side="right")
                    fc1_stage(nc, parts, inp["L0_mix_fc1_w"], inp["L0_mix_fc1_b"], hidden, mask_d, rows_d, mx)
                counts = sb(graph, "counts0", [TP, NT, N], I16)
                dense_add_stage(nc, "fc2", ident, hidden, 4 * KB, inp["L0_mix_fc2_w"], inp["L0_mix_fc2_b"], sum_d, sum_d,
                                ahead=[(counts[:], tokens(counts_d))])
            gat_shift_stage(nc, "gat00shift", ident, 8, a_s, a_d, mx, a_s02, shift_d)
            gat_attend_stage(nc, "gat00att", counts, 8, 128, None, a_s, a_s02, shift_d, g1a_d, h_d=h0_d)
            gat_one_head(nc, "gat01", ident, g1a_d, 1024, "relu", inp["L0_gnn_b1"], inp["L0_gnn_W2"],
                         inp["L0_gnn_att_src2"], inp["L0_gnn_att_dst2"], counts, mask_d, rows_d, shift_d,
                         a_s, a_d, a_s02, mx, g2_d)
        with ExitStack() as ctx:
            xT = sb(ctx, "xT0", [128, KB, N])
            norm_stage(nc, "ln1", ident, 1e-5, sum_d, g2_d, inp["L0_gnn_b2"], x1_d, None, None, None, xT)
            wT = sb(ctx, "wT", [128, 4, N])
            router_stage(nc, ident, xT, inp["L0_ffn_P"], inp["L0_ffn_C"], inp["L0_ffn_W1"], inp["L0_ffn_b1"],
                         z_parts_d, w1_parts_d, b1_parts_d, w_parts_d, wT)
            expert_stage(nc, z_parts_d, w1_parts_d, b1_parts_d, w_parts_d, inp["spread"], inp["L0_ffn_W2"],
                         inp["L0_ffn_b2"], wT, comb_d)
            combT = sb(ctx, "combT", [128, N])
            gT = sb(ctx, "gT", [128, 2, N])
            comb_stage(nc, comb_d, combT[:])
            dense_stage(nc, "mixup", combT, inp["L0_ffn_G1"], 2, inp["L0_ffn_g1b"], ACT.Gelu_apprx_tanh, gT)
            dense_add_stage(nc, "mixdown", ident, gT, 2, inp["L0_ffn_G2"], inp["L0_ffn_g2b"], x1_d, x2_d)
        with ExitStack() as ctx:
            yT = sb(ctx, "yT1", [128, KB, N])
            norm_stage(nc, "ln2", ident, 1e-5, x2_d, None, None, None, xn_d, None, None, yT)
            gat_project_stage(nc, "gat10proj", ident, xn_d, D, None, None, inp["L1_gnn_W1"], 8, 96,
                              inp["L1_gnn_a_src1"], inp["L1_gnn_a_dst1"], None, a_s, a_d, rows_d, h_d=h1_d)
            performer_stage(nc, "perf1", yT, inp["L1_mix_W_qkv"], None, None, inp["L1_mix_random_features"], False, 256,
                            1.0, 1e-6, attn_d, scan=(mask_d, rows_d, 8, mx))
        with ExitStack() as graph:
            counts = sb(graph, "counts1", [TP, NT, N], I16)
            proj_stage(nc, "proj1", ident, attn_d, inp["L1_mix_W_proj"], inp["L1_mix_b_proj"], xn_d, x2_d, sum_d,
                       1e-5, inp["L1_mix_gamma"], inp["L1_mix_beta"], None, ahead=[(counts[:], tokens(counts_d))])
            gat_shift_stage(nc, "gat10shift", ident, 8, a_s, a_d, mx, a_s02, shift_d)
            gat_attend_stage(nc, "gat10att", counts, 8, 96, None, a_s, a_s02, shift_d, g1b_d, h_d=h1_d)
            gat_one_head(nc, "gat11", ident, g1b_d, D, "elu", inp["L1_gnn_b1"], inp["L1_gnn_W2"],
                         inp["L1_gnn_a_src2"], inp["L1_gnn_a_dst2"], counts, mask_d, rows_d, shift_d,
                         a_s, a_d, a_s02, mx, g2_d)
        bitlinear_stage(nc, ident, sum_d, g2_d, inp["L1_gnn_b2"], inp["L1_ffn_w_in"], inp["L1_ffn_w_out"],
                        inp["L1_ffn_g_in"], inp["L1_ffn_g_out"], out_d)



def columns(a):
    return a.reshape(-1, 128).T


def layout(inputs):
    a = {k: np.asarray(v) for k, v in inputs.items()}
    a["L0_gnn_W1"] = a["L0_gnn_W1"].T
    a["L0_gnn_W2"] = a["L0_gnn_W2"].T
    for k in ("L0_gnn_att_src1", "L0_gnn_att_dst1", "L0_gnn_att_src2", "L0_gnn_att_dst2",
              "L1_gnn_a_src1", "L1_gnn_a_dst1", "L1_gnn_a_src2", "L1_gnn_a_dst2"):
        a[k] = a[k].reshape(-1)
    for k in ("L0_mix_ln1_g", "L0_mix_ln1_b", "L0_mix_ln2_g", "L0_mix_ln2_b", "L0_mix_fc1_b", "L0_mix_fc2_b",
              "L0_ffn_g1b", "L0_ffn_g2b"):
        a[k] = columns(a[k])
    a["L0_mix_v_b"] = a["L0_mix_qkv_b"][2 * D:]
    a["L0_mix_qkv_b"] = columns(a["L0_mix_qkv_b"][:2 * D])
    a["L0_ffn_P"] = a["L0_ffn_P"].transpose(1, 0, 2).reshape(D, ES * ER)
    a["L0_ffn_C"] = a["L0_ffn_C"].transpose(0, 2, 1)
    a["L0_ffn_W1"] = a["L0_ffn_W1"].transpose(0, 2, 1, 3).reshape(ES, ER, EM * EH)
    a["L0_ffn_b1"] = a["L0_ffn_b1"].reshape(ES, EM * EH)
    a["L0_ffn_W2"] = a["L0_ffn_W2"].reshape(ES, EJ, 128, ER).transpose(0, 2, 1, 3)
    a["L1_mix_random_features"] = a["L1_mix_random_features"].T
    a["L1_ffn_w_in"] = a["L1_ffn_w_in"].T
    a["L1_ffn_w_out"] = a["L1_ffn_w_out"].T
    a["ident"] = np.eye(128, dtype=np.float32)
    a["lower"] = np.tril(np.ones((128, 128), np.float32), -1)
    spread = np.zeros((2, EM, EJ, 4, EH), np.float16)
    for j in range(EJ):
        for m in range(4):
            spread[0, 4 * j + m, j, m, :] = 1.0
            spread[1, 4 * j + m, j, m, :] = 2.0 ** -12
    a["spread"] = spread.reshape(2 * EM, EJ * 128)
    return {k: np.ascontiguousarray(v) for k, v in a.items()}


def kernel(**inputs):
    import concourse.bacc as _bacc
    from concourse.bass_utils import run_bass_kernel_spmd as _run

    nc = _bacc.Bacc("TRN2", target_bir_lowering=False, num_devices=1)
    arrays, args = {}, {}
    for name, a in layout(inputs).items():
        arrays[f"in_{name}"] = a
        args[name] = nc.dram_tensor(f"in_{name}", a.shape, mybir.dt.from_np(a.dtype), kind="ExternalInput").ap()
    out = nc.dram_tensor("out", (N, D), F32, kind="ExternalOutput").ap()
    gps_two_layers(nc, args, out)
    r = _run(nc, [arrays], core_ids=[0])
    return r.results[0]["out"]
```

```python
from contextlib import ExitStack, contextmanager

import numpy as np

import concourse.bass as bass
from concourse import mybir

F32 = mybir.dt.float32
BF16 = mybir.dt.bfloat16
F32R = mybir.dt.float32r

F16 = mybir.dt.float16
I32 = mybir.dt.int32
I16 = mybir.dt.int16
ACT = mybir.ActivationFunctionType
ALU = mybir.AluOpType
AX = mybir.AxisListType

N = 1250
E = 20000
D = 768
NT = 10
TP = N // NT
KB = D // 128
HEADS = 12
HD = D // HEADS
HP = HEADS // 2
CHUNKS = [(0, 512), (512, 512), (1024, N - 1024)]
EC = E // TP
XS = 4
WS = 5
EB = 4
NEG = -3.0e38
ES, ER, EM, EH = 8, 16, 64, 32
EJ = EM * EH // 128
NPART = [(0, 0), (1, 0), (0, 1), (1, 1), (2, 0), (0, 2)]
ZK = len(NPART) * ER + 3
EG = 4
EXTRA = 128


class Stage:

    def __init__(self, nc, name):
        self.nc, self.name, self.sems = nc, name, []

    def __enter__(self):
        self.ctx = ExitStack()
        return self

    def sb(self, name, shape, dt=F32):
        return self.ctx.enter_context(self.nc.sbuf_tensor(f"{self.name}_{name}", shape, dt))

    def ps(self, name, shape, dt=F32):
        return self.ctx.enter_context(self.nc.psum_tensor(f"{self.name}_{name}", shape, dt))

    def sem(self, name):
        s = self.nc.alloc_semaphore(f"{self.name}_{name}")
        self.sems.append(s)
        return s

    def __exit__(self, kind, *rest):
        if kind is None:
            self.nc.clear_and_free_semaphores(self.sems)
            self.nc.all_engine_barrier()
        self.ctx.close()


class Chain:

    def __init__(self, eng, sem, base=0):
        self.eng, self.sem, self.base, self.n = eng, sem, base, 0

    def done(self, ins):
        self.n += 1
        return ins.then_inc(self.sem, 1)

    def wait(self):
        self.eng.wait_ge(self.sem, self.base + self.n)


def row_bcast(ap1d, parts):
    n = ap1d.shape[0]
    return bass.AP(ap1d.tensor, ap1d.offset, [[0, parts], [1, n]])


def tokens(ap2d):
    return ap2d.rearrange("(t p) d -> p t d", p=TP)


def kblocks(ap2d):
    return ap2d.rearrange("(kb p) n -> p kb n", p=128)


def split_tile(dve, full, parts, t, split):
    cols = slice(t * TP, (t + 1) * TP)
    dve.tensor_copy(parts[0][:, :, cols], full).then_inc(split, 1)
    dve.wait_ge(split, 2 * t + 1)
    dve.tensor_tensor(parts[1][:, :, cols], full, parts[0][:, :, cols].bitcast(F32), ALU.subtract).then_inc(split, 1)


def edge_stage(nc, ident, src, dst, lower, key_off, key_val, adj_d):
    with Stage(nc, "edge") as S:
        ends = S.sb("ends", [TP, 2, EC], I32)
        endf = S.sb("endf", [TP, 2, EC])
        key = S.sb("key", [TP, EC])
        low = S.sb("low", [TP, TP])
        ones = S.sb("ones", [TP, TP])
        one = S.sb("one", [TP, 1], BF16)
        diag = S.sb("diag", [TP, 8, EB, TP])
        eq = S.sb("eq", [TP, 4, EB, TP], BF16)
        below = S.sb("below", [TP, 4, EB, TP], BF16)
        lowb = S.sb("lowb", [TP, TP], BF16)
        cnt = S.sb("cnt", [TP, EC])
        last = S.sb("last", [TP, EC])
        spare = S.sb("spare", [TP, 1])
        offf = S.sb("offf", [TP, EC])
        zero = S.sb("zero", [TP, 6250])
        keys = S.ps("keys", [TP, 4, 512])
        sums = S.ps("sums", [TP, 2, EC])
        loaded, low_ld, chain, key_ready = S.sem("loaded"), S.sem("low_ld"), S.sem("chain"), S.sem("key_ready")
        diag_act, diag_dve, spread_done = S.sem("diag_act"), S.sem("diag_dve"), S.sem("spread_done")
        eq_done, below_done, summed = S.sem("eq_done"), S.sem("below_done"), S.sem("summed")
        zeroed, cleared, spare_set = S.sem("zeroed"), S.sem("cleared"), S.sem("spare_set")
        steps = EC // EB

        def cols(i):
            return slice(i * EB, (i + 1) * EB)

        with nc.Block() as block:
            @block.sync
            def _(sp):
                sp.dma_start(ends[:, 0, :], src.rearrange("(p c) -> p c", c=EC)).then_inc(loaded, 16)
                sp.dma_start(ends[:, 1, :], dst.rearrange("(p c) -> p c", c=EC)).then_inc(loaded, 16)
                sp.dma_start(low[:], lower[0:TP, 0:TP]).then_inc(low_ld, 16)
                sp.wait_ge(zeroed, 1)
                for half in range(2):
                    sp.dma_start(adj_d[half * TP * 6250:(half + 1) * TP * 6250].rearrange("(p n) -> p n", p=TP),
                                 zero[:]).then_inc(cleared, 16)
                sp.dma_start(adj_d[N * N:N * N + EXTRA].rearrange("(a n) -> a n", a=1),
                             zero[0:1, 0:EXTRA]).then_inc(cleared, 16)
                sp.wait_ge(cleared, 48)

            @block.gpsimd
            def _(pool):
                nc.gpsimd.memset(zero[:], 0.0).then_inc(zeroed, 1)
                nc.gpsimd.iota(key_off[:, 0:1], [[0, 1]], base=N * N, channel_multiplier=1).then_inc(spare_set, 1)

            @block.tensor
            def _(pe):
                def spread(i):
                    if i % 4 == 3:
                        pe.wait_ge(diag_dve, i // 4 + 1)
                    else:
                        pe.wait_ge(diag_act, i // 4 * 3 + i % 4 + 1)
                    if i >= 4:
                        pe.wait_ge(eq_done, i - 3)
                    pe.matmul(keys[:, i % 4, 0:EB * TP], ones[:, :], diag[:, i % 8], start=True, stop=True
                              ).then_inc(spread_done, 1)

                pe.wait_ge(chain, 2)
                spread(0)
                spread(1)
                for i in range(steps):
                    if i + 2 < steps:
                        spread(i + 2)
                    pe.wait_ge(below_done, i + 1)
                    for c in range(EB):
                        for r, what in enumerate((eq, below)):
                            ins = pe.matmul(sums[:, r, i * EB + c:i * EB + c + 1], what[:, i % 4, c, :], one[:],
                                            start=True, stop=True)
                    ins.then_inc(summed, 1)

            @block.scalar
            def _(act):
                act.wait_ge(key_ready, 1)
                for i in range(steps):
                    if i % 4 == 3:
                        continue
                    if i >= 8:
                        act.wait_ge(spread_done, i - 7)
                    for c in range(EB):
                        k = i * EB + c
                        ins = act.activation(diag[:, i % 8, c, :], ident[0:TP, 0:TP], ACT.Copy, scale=key[:, k:k + 1])
                    ins.then_inc(diag_act, 1)

            @block.vector
            def _(dve):
                steps_done = Chain(dve, chain)
                steps_done.done(dve.memset(ones[:], 1.0))
                steps_done.done(dve.memset(one[:], 1.0))
                dve.wait_ge(loaded, 32)
                steps_done.done(dve.tensor_copy(endf[:], ends[:]))
                steps_done.wait()
                dve.scalar_tensor_tensor(out=key[:], in0=endf[:, 0, :], scalar=float(N),
                                         in1=endf[:, 1, :], op0=ALU.mult, op1=ALU.add).then_inc(key_ready, 1)
                dve.wait_ge(low_ld, 16)
                steps_done.done(dve.tensor_copy(lowb[:], low[:]))
                steps_done.wait()
                dve.wait_ge(key_ready, 1)

                def set_diag(i):
                    if i >= 8:
                        dve.wait_ge(spread_done, i - 7)
                    dve.tensor_tensor(diag[:, i % 8], ident[0:TP, 0:TP].unsqueeze(1).to_broadcast([TP, EB, TP]),
                                      key[:, cols(i)].unsqueeze(2).to_broadcast([TP, EB, TP]),
                                      ALU.mult).then_inc(diag_dve, 1)

                def mark_below(i):
                    dve.wait_ge(eq_done, i + 1)
                    dve.tensor_tensor(below[:, i % 4], eq[:, i % 4], lowb[:].unsqueeze(1).to_broadcast([TP, EB, TP]),
                                      ALU.mult).then_inc(below_done, 1)

                set_diag(3)
                for i in range(steps):
                    if i % 4 == 0 and i + 7 < steps:
                        set_diag(i + 7)
                    dve.wait_ge(spread_done, i + 1)
                    if i >= 4:
                        dve.wait_ge(summed, i - 3)
                    dve.tensor_tensor(eq[:, i % 4], keys[:, i % 4, 0:EB * TP].rearrange("p (c e) -> p c e", c=EB),
                                      key[:, cols(i)].unsqueeze(2).to_broadcast([TP, EB, TP]),
                                      ALU.is_equal).then_inc(eq_done, 1)
                    if i:
                        mark_below(i - 1)
                mark_below(steps - 1)
                dve.wait_ge(spare_set, 1)
                steps_done.done(dve.tensor_copy(spare[:], key_off[:, 0:1]))
                dve.wait_ge(summed, steps)
                steps_done.done(dve.tensor_scalar(last[:], sums[:, 1, :], 0.0, None, ALU.is_equal))
                steps_done.done(dve.tensor_copy(cnt[:], sums[:, 0, :]))
                steps_done.wait()
                steps_done.done(dve.tensor_scalar(offf[:], key[:], spare[:, 0:1], None, ALU.subtract))
                steps_done.done(dve.tensor_tensor(key_val[:], cnt[:], last[:], ALU.mult))
                steps_done.wait()
                steps_done.done(dve.tensor_tensor(offf[:], offf[:], last[:], ALU.mult))
                steps_done.wait()
                steps_done.done(dve.tensor_scalar(key_off[:], offf[:], spare[:, 0:1], None, ALU.add))


def add_edges(nc, pool, key_off, key_val, added, adj_flat):
    for c in range(EC):
        if c:
            pool.wait_ge(added, c * 16)
        nc.gpsimd.indirect_dma_start(
            out=adj_flat, out_offset=bass.IndirectOffsetOnAxis(ap=key_off[:, c:c + 1], axis=0),
            in_=key_val[:, c:c + 1], in_offset=None, compute_op=ALU.add).then_inc(added, 16)
    pool.wait_ge(added, EC * 16)


def norm_stage(nc, name, ident, eps, x_d, normed_d, gain_cols, shift_cols, yT):
    parts = isinstance(yT, tuple)
    second = gain_cols is not None
    with Stage(nc, name) as S:
        x = S.sb("x", [TP, NT, D])
        cols = S.sb("cols", [128, 2, KB])
        stats = S.sb("stats", [TP, NT, 2, 6])
        mv = S.sb("mv", [TP, 2, NT, 2])
        std = S.sb("std", [TP, 2, NT])
        rstd = S.sb("rstd", [TP, 2, NT])
        epst = S.sb("epst", [TP, 1])
        full = S.sb("full", [128, 2, KB, TP]) if parts else None
        split = S.sem("split")
        tps = S.ps("tps", [128, 2, 1024])
        x_ld, cols_ld = [S.sem("x_ld0"), S.sem("x_ld1")], S.sem("cols_ld")
        chain, var_ready, std_ready = S.sem("chain"), S.sem("var_ready"), S.sem("std_ready")
        normed, final = S.sem("normed"), S.sem("final")
        turned, kept, stored = S.sem("turned"), S.sem("kept"), S.sem("stored")
        half = NT // 2
        with nc.Block() as block:
            @block.sync
            def _(sp):
                for h in range(2):
                    rows = slice(h * half, (h + 1) * half)
                    sp.dma_start(x[:, rows, :], tokens(x_d)[:, rows, :]).then_inc(x_ld[h], 16)
                if second:
                    sp.dma_start(cols[:, 0, :], gain_cols).then_inc(cols_ld, 16)
                    sp.dma_start(cols[:, 1, :], shift_cols).then_inc(cols_ld, 16)
                if normed_d is not None:
                    sp.wait_ge(normed, NT)
                    sp.dma_start(tokens(normed_d), x[:]).then_inc(stored, 16)
                    sp.wait_ge(stored, 16)

            @block.vector
            def _(dve):
                steps_done = Chain(dve, chain)
                steps_done.done(dve.memset(epst[:], eps))
                for t in range(NT):
                    if t % half == 0:
                        dve.wait_ge(x_ld[t // half], 16)
                    for k in range(2):
                        steps_done.done(dve.bn_stats(stats[:, t, k, :], x[:, t, k * 384:(k + 1) * 384]))
                    steps_done.wait()
                    dve.bn_aggr(mv[:, 0, t, :], stats[:, t, :, :]).then_inc(var_ready, 1)

                def normalise(r, signal):
                    dve.wait_ge(std_ready, r + 1)
                    steps_done.done(dve.reciprocal(rstd[:, r, :], std[:, r, :]))
                    steps_done.wait()
                    dve.wait_ge(var_ready, (r + 1) * NT)
                    for t in range(NT):
                        ins = dve.tensor_scalar(x[:, t, :], x[:, t, :], mv[:, r, t, 0:1], rstd[:, r, t:t + 1],
                                                ALU.subtract, ALU.mult)
                        ins.then_inc(signal, 1)

                if second:
                    normalise(0, normed)
                    for t in range(NT):
                        dve.wait_ge(normed, t + 1)
                        for k in range(2):
                            steps_done.done(dve.bn_stats(stats[:, t, k, :], x[:, t, k * 384:(k + 1) * 384]))
                        steps_done.wait()
                        dve.bn_aggr(mv[:, 1, t, :], stats[:, t, :, :]).then_inc(var_ready, 1)
                    if normed_d is not None:
                        dve.wait_ge(stored, 16)
                    normalise(1, final)
                else:
                    normalise(0, normed)
                if parts:
                    for t in range(NT):
                        dve.wait_ge(kept, t + 1)
                        split_tile(dve, full[:, t % 2], yT, t, split)

            @block.scalar
            def _(act):
                for r in range(2 if second else 1):
                    act.wait_ge(chain, 1)
                    act.wait_ge(var_ready, (r + 1) * NT)
                    act.activation(std[:, r, :], mv[:, r, :, 1], ACT.Sqrt, bias=epst[:, 0:1]).then_inc(std_ready, 1)
                if second:
                    act.wait_ge(cols_ld, 32)
                for t in range(NT):
                    act.wait_ge(turned, t + 1)
                    if parts and t >= 2:
                        act.wait_ge(split, 2 * t - 2)
                    tile = full[:, t % 2] if parts else yT[:, :, t * TP:(t + 1) * TP]
                    if second:
                        for kb in range(KB):
                            ins = act.activation(tile[:, kb, :], tps[:, t % 2, kb * 128:kb * 128 + TP], ACT.Identity,
                                                 scale=cols[:, 0, kb:kb + 1], bias=cols[:, 1, kb:kb + 1])
                    else:
                        ins = act.copy(tile, tps[:, t % 2, 0:KB * 128].rearrange("p (kb n) -> p kb n", kb=KB)[:, :, 0:TP])
                    ins.then_inc(kept, 1)

            @block.tensor
            def _(pe):
                for t in range(NT):
                    pe.wait_ge(final if second else normed, t + 1)
                    if t >= 2:
                        pe.wait_ge(kept, t - 1)
                    for kb in range(KB):
                        ins = pe.transpose(tps[:, t % 2, kb * 128:kb * 128 + TP], x[:, t, kb * 128:(kb + 1) * 128],
                                           ident[0:TP, 0:TP])
                    ins.then_inc(turned, 1)


def performer_stage(nc, name, y_parts, w_d, bias_cols, vbias_d, feat_d, per_head, m, scale, eps, out_d, edges=None, scan=None):
    mb_n = m // 128
    per = 512 // m
    n_k = NT // per
    n_phi = n_k + 3 * mb_n
    Q0, K0 = (0, n_k + n_phi), (3 * mb_n, n_phi)
    phi_banks = [3, 4, 0, 1, 2]
    ring = len(phi_banks)
    vw = HD + 1
    with Stage(nc, name) as S:
        w = S.sb("w", [128, 2, KB, 128])
        qk_parts = [S.sb(f"qk_{s}", [128, 2, KB, 128], F32R) for s in ("hi", "lo")]
        v_parts = [S.sb(f"v_{s}", [128, 2, KB, 128], F32R) for s in ("hi", "lo")]
        feat = S.sb("feat", [128, 2, 2, m])
        qs = S.sb("qs", [128, 2, N])
        ks = S.sb("ks", [128, 2, N])
        v = S.sb("v", [TP, NT, 4, vw])
        kphi = S.sb("kphi", [TP, 2, NT, m])
        qphi = S.sb("qphi", [128, 2, mb_n, N])
        ktv = S.sb("ktv", [128, 2, mb_n, vw])
        den = S.sb("den", [TP, NT])
        rden = S.sb("rden", [TP, NT])
        o = S.sb("o", [TP, NT, 128])
        lnm = S.sb("lnm", [128, 1])
        wide = S.ps("wide", [128, 5, 512])
        proj = wide[:, 0:3, :].rearrange("p b n -> p (b n)")
        ktv_ps = S.ps("ktv_ps", [128, 512])
        o_ps = S.ps("o_ps", [128, 2, 512])
        feat_ld = [S.sem("feat_ld0"), S.sem("feat_ld1")]
        w_ld, w_high, w_split, o_st = S.sem("w_ld"), S.sem("w_high"), S.sem("w_split"), S.sem("o_st")
        bias_ld, const_set = S.sem("bias_ld"), S.sem("const_set")
        proj_done, plain_done, square_done, v_proj, v_done = (S.sem(s) for s in (
            "proj_done", "plain_done", "square_done", "v_proj", "v_done"))
        phi_done, exp_done, ktv_done, ktv_kept, o_done, o_kept, chain = (S.sem(s) for s in (
            "phi_done", "exp_done", "ktv_done", "ktv_kept", "o_done", "o_kept", "chain"))
        added = S.sem("added")
        o_tiles = [(0, 0, 7), (1, 7, 3)]
        biased = bias_cols is not None
        bcols = S.sb("bcols", [128, 12]) if biased else None
        vbias = S.sb("vbias", [TP, D]) if biased else None
        passes = ((0, 1), (1, 0), (0, 0))
        scan = MaxScan(S, *scan, slots=1) if scan is not None else None

        with nc.Block() as block:
            if scan is not None:
                @block.gpsimd
                def _(pool):
                    scan.load(pool)

            if edges is not None:
                @block.gpsimd
                def _(pool):
                    add_edges(nc, pool, edges[0], edges[1], added, edges[2])

            @block.sync
            def _(sp):
                sp.nop().then_inc(o_st, 16)
                if biased:
                    sp.dma_start(bcols[:], bias_cols).then_inc(bias_ld, 16)
                    sp.dma_start(vbias[:], row_bcast(vbias_d, TP)).then_inc(bias_ld, 16)

                def load_w(c0, c1):
                    for k, c in enumerate((c0, c1)):
                        sp.dma_start(w[:, k], kblocks(w_d)[:, :, bass.ds(c, 128)]).then_inc(w_ld, 16)

                def load_qk(g):
                    load_w(g * 128, g * 128 + D)

                def load_v(i):
                    load_w(i * 256 + 2 * D, i * 256 + 2 * D + 128)

                def load_features(g, u):
                    for x in range(2):
                        f = feat_d[bass.ds(g * 2 + x, 1), :, :].rearrange("a c m -> (a c) m") if per_head else feat_d
                        sp.dma_start(feat[64 * x:64 * x + 64, u, x, :], f).then_inc(feat_ld[u], 16)

                def store(g):
                    sp.wait_ge(o_kept, g * 4 + 5)
                    sp.dma_start(tokens(out_d)[:, :, bass.ds(g * 128, 128)], o[:]).then_inc(o_st, 16)

                load_v(0)
                sp.wait_ge(w_split, 1)
                load_qk(0)
                load_features(0, 0)
                load_features(1, 1)
                sp.wait_ge(w_split, 2)
                load_qk(1)
                with sp.Fori(0, HP // 2 - 1) as i:
                    sp.wait_ge(w_split, i * 3 + 3)
                    load_v(i + 1)
                    sp.wait_ge(o_done, i * 4 + 1)
                    load_features(i * 2 + 2, 0)
                    store(i * 2)
                    sp.wait_ge(w_split, i * 3 + 4)
                    load_qk(i * 2 + 2)
                    sp.wait_ge(w_split, i * 3 + 5)
                    load_qk(i * 2 + 3)
                    sp.wait_ge(o_done, i * 4 + 3)
                    load_features(i * 2 + 3, 1)
                    store(i * 2 + 1)
                store(HP - 2)
                store(HP - 1)
                sp.wait_ge(o_st, 16 * HP + 16)

            @block.tensor
            def _(pe):
                pe.wait_ge(const_set, 6)
                with pe.Fori(0, HP // 2) as i:
                    for u in range(2):
                        g = i * 2 + u
                        pe.wait_ge(exp_done, g * (2 * n_phi) + 1)
                        if u == 0:
                            pe.wait_ge(w_split, i * 3 + 1)
                            for t in range(NT):
                                for kb in range(KB):
                                    for n, (yp, wp) in enumerate(passes):
                                        ins = pe.matmul(wide[0:TP, t // 2, t % 2 * 256:t % 2 * 256 + 256],
                                                        y_parts[yp][:, kb, t * TP:(t + 1) * TP], v_parts[wp][:, :, kb, :],
                                                        start=(kb == 0 and n == 0), stop=(kb == KB - 1 and n == 2))
                                if t % 2 == 1:
                                    ins.then_inc(v_proj, 1)
                        pe.wait_ge(w_split, i * 3 + 2 + u)
                        for k in range(2):
                            for c, (c0, cn) in enumerate(CHUNKS):
                                if k == 1:
                                    pe.wait_ge(plain_done, g * 12 + 2 * c + 2)
                                elif u == 0:
                                    pe.wait_ge(v_done, i * 5 + c + 1)
                                for kb in range(KB):
                                    for n, (wp, yp) in enumerate(passes):
                                        ins = pe.matmul(proj[:, c0:c0 + cn], qk_parts[wp][:, k, kb, :],
                                                        y_parts[yp][:, kb, c0:c0 + cn],
                                                        start=(kb == 0 and n == 0), stop=(kb == KB - 1 and n == 2))
                                ins.then_inc(proj_done, 1)

                        def features(j, products):
                            if 2 <= j < ring:
                                pe.wait_ge(plain_done, g * 12 + 6 + 2 * (j - 1))
                            elif j >= ring:
                                pe.wait_ge(exp_done, g * (2 * n_phi) + j - ring + 2)
                            for out, lhsT, rhs in products:
                                ins = pe.matmul(out, lhsT, rhs, start=True, stop=True)
                            ins.then_inc(phi_done, 1)

                        def k_features(x):
                            for n in range(n_k):
                                j = K0[x] + n
                                features(j, [(wide[0:TP, phi_banks[j % ring], y * m:(y + 1) * m],
                                              ks[:, x, (n * per + y) * TP:(n * per + y + 1) * TP], feat[:, u, x, :])
                                             for y in range(per)])

                        def q_features(x):
                            j = Q0[x]
                            for mb in range(mb_n):
                                for c0, cn in CHUNKS:
                                    features(j, [(wide[:, phi_banks[j % ring], 0:cn],
                                                  feat[:, u, x, mb * 128:(mb + 1) * 128], qs[:, x, c0:c0 + cn])])
                                    j += 1

                        def k_t_v(x):
                            pe.wait_ge(exp_done, g * (2 * n_phi) + K0[x] + n_k + 1)
                            pe.wait_ge(v_done, i * 5 + 5)
                            pe.wait_ge(ktv_kept, g * 2 + x + 1)
                            for mb in range(mb_n):
                                for t in range(NT):
                                    ins = pe.matmul(ktv_ps[:, mb * vw:(mb + 1) * vw],
                                                    kphi[:, x, t, mb * 128:(mb + 1) * 128], v[:, t, 2 * u + x, :],
                                                    start=(t == 0), stop=(t == NT - 1))
                            ins.then_inc(ktv_done, 1)

                        def outputs(x):
                            pe.wait_ge(exp_done, g * (2 * n_phi) + Q0[x] + 3 * mb_n + 1)
                            pe.wait_ge(ktv_kept, g * 2 + x + 2)
                            pe.wait_ge(o_kept, g * 4 + 2 * x + 1)
                            for bank, t0, tn in o_tiles:
                                for t in range(t0, t0 + tn):
                                    for mb in range(mb_n):
                                        ins = pe.matmul(o_ps[0:TP, bank, (t - t0) * vw:(t - t0 + 1) * vw],
                                                        qphi[:, x, mb, t * TP:(t + 1) * TP], ktv[:, x, mb, :],
                                                        start=(mb == 0), stop=(mb == mb_n - 1))
                            return ins

                        pe.wait_ge(feat_ld[u], i * 32 + 32)
                        pe.wait_ge(square_done, g * 12 + 6)
                        q_features(0)
                        pe.wait_ge(square_done, g * 12 + 12)
                        k_features(0)
                        k_features(1)
                        k_t_v(0)
                        q_features(1)
                        outputs(0).then_inc(o_done, 1)
                        k_t_v(1)
                        outputs(1).then_inc(o_done, 1)

            @block.scalar
            def _(act):
                act.wait_ge(const_set, 6)
                act.nop().then_inc(exp_done, 1)
                with act.Fori(0, HP // 2) as i:
                    for u in range(2):
                        g = i * 2 + u
                        def exps(j, out, in_, parts):
                            act.wait_ge(phi_done, g * (2 * n_phi) + j + 1)
                            act.activation(out, in_, ACT.Exp, bias=lnm[0:parts, 0:1], scale=scale).then_inc(exp_done, 1)

                        def k_exps(x):
                            for n in range(n_k):
                                j = K0[x] + n
                                got = wide[0:TP, phi_banks[j % ring], 0:per * m].rearrange("p (y m) -> p y m", y=per)
                                exps(j, kphi[:, x, n * per:(n + 1) * per, :], got, TP)

                        def q_exps(x):
                            j = Q0[x]
                            for mb in range(mb_n):
                                for c0, cn in CHUNKS:
                                    exps(j, qphi[:, x, mb, c0:c0 + cn], wide[:, phi_banks[j % ring], 0:cn], 128)
                                    j += 1

                        q_exps(0)
                        k_exps(0)
                        k_exps(1)
                        q_exps(1)

            @block.vector
            def _(dve):
                for s in (ktv_kept, o_kept):
                    dve.nop().then_inc(s, 1)
                for u in range(2):
                    dve.memset(feat[64:128, u, 0, :], -0.5 * scale).then_inc(const_set, 1)
                    dve.memset(feat[0:64, u, 1, :], -0.5 * scale).then_inc(const_set, 1)
                dve.memset(lnm[:], -0.5 * float(np.log(m))).then_inc(const_set, 1)
                dve.memset(v[:, :, :, HD:vw], 1.0).then_inc(const_set, 1)

                def split_w(parts, n):
                    dve.wait_ge(w_ld, n * 32 + 32)
                    dve.tensor_copy(parts[0][:], w[:]).then_inc(w_high, 1)
                    dve.wait_ge(w_high, n + 1)
                    dve.tensor_tensor(parts[1][:], w[:], parts[0][:].bitcast(F32), ALU.subtract).then_inc(w_split, 1)

                def pairs(i, last):
                    for b in range(NT // 2):
                        dve.wait_ge(v_proj, i * 5 + b + 1)
                        got = wide[0:TP, b, :].rearrange("p (t x c) -> p t x c", t=2, x=4)
                        to = v[:, 2 * b:2 * b + 2, :, 0:HD]
                        if biased:
                            vb = vbias[:, bass.ds(i * 256, 256)].rearrange("p (x c) -> p x c", x=4)
                            ins = dve.tensor_tensor(to, got, vb.unsqueeze(1).to_broadcast([TP, 2, 4, HD]), ALU.add)
                        else:
                            ins = dve.tensor_copy(to, got)
                        ins.then_inc(v_done, 1)
                    for u in range(2):
                        g = i * 2 + u
                        steps_done = Chain(dve, chain, g * 6)
                        for k, dest in enumerate((qs, ks)):
                            for c, (c0, cn) in enumerate(CHUNKS):
                                dve.wait_ge(proj_done, g * 6 + k * 3 + c + 1)
                                for x in range(2):
                                    rows = slice(64 * x, 64 * x + 64)
                                    if biased:
                                        ins = dve.tensor_scalar(dest[rows, x, c0:c0 + cn], proj[rows, c0:c0 + cn],
                                                                bcols[rows, bass.ds(g + k * KB, 1)], None, ALU.add)
                                    else:
                                        ins = dve.tensor_copy(dest[rows, x, c0:c0 + cn], proj[rows, c0:c0 + cn])
                                    ins.then_inc(plain_done, 1)
                                dve.wait_ge(plain_done, g * 12 + k * 6 + 2 * c + 2)
                                for x in range(2):
                                    rows, other = slice(64 * x, 64 * x + 64), slice(64 - 64 * x, 128 - 64 * x)
                                    got = dest[rows, x, c0:c0 + cn]
                                    dve.tensor_tensor(dest[other, x, c0:c0 + cn], got, got, ALU.mult).then_inc(square_done, 1)
                        if u == 0:
                            split_w(qk_parts, i * 3 + 2)
                        elif not last:
                            split_w(v_parts, i * 3 + 3)
                        if scan is not None:
                            scan.head(dve, g + 1, 0, g + 1)

                        def keep_ktv(x):
                            dve.wait_ge(ktv_done, g * 2 + x + 1)
                            dve.tensor_copy(ktv[:, x], ktv_ps[:, 0:mb_n * vw].rearrange("p (a b) -> p a b", a=mb_n)
                                            ).then_inc(ktv_kept, 1)

                        def keep_out(x):
                            dve.wait_ge(o_done, g * 2 + x + 1)
                            if x == 0:
                                dve.wait_ge(o_st, g * 16 + 16)
                            got = [o_ps[0:TP, b, 0:tn * vw].rearrange("p (t w) -> p t w", t=tn) for b, _, tn in o_tiles]
                            for (_, t0, tn), a in zip(o_tiles, got):
                                steps_done.done(dve.tensor_scalar(den[:, t0:t0 + tn], a[:, :, HD], eps, None, ALU.add))
                            steps_done.wait()
                            steps_done.done(dve.reciprocal(rden[:], den[:]))
                            steps_done.wait()
                            for (_, t0, tn), a in zip(o_tiles, got):
                                dve.tensor_tensor(o[:, t0:t0 + tn, x * HD:(x + 1) * HD], a[:, :, 0:HD],
                                                  rden[:, t0:t0 + tn].unsqueeze(2).to_broadcast([TP, tn, HD]),
                                                  ALU.mult).then_inc(o_kept, 1)

                        keep_ktv(0)
                        if u == 1 and not last:
                            split_w(qk_parts, i * 3 + 4)
                        keep_out(0)
                        keep_ktv(1)
                        keep_out(1)

                split_w(v_parts, 0)
                split_w(qk_parts, 1)
                if biased:
                    dve.wait_ge(bias_ld, 32)
                if scan is not None:
                    dve.wait_ge(scan.mask_ld, 16)
                    scan.head(dve, 0, 0, 0)
                with dve.Fori(0, HP // 2 - 1) as i:
                    pairs(i, False)
                pairs(HP // 2 - 1, True)
                if scan is not None:
                    scan.head(dve, HP + 1, 0, HP + 1)


def proj_stage(nc, name, ident, attn_d, w_d, bias_d, xn_d, x_d, sum_d, eps, gain, shift, yT, ahead=()):
    turn = yT is not None
    with Stage(nc, name) as S:
        a = S.sb("a", [TP, NT, D])
        h = S.sb("h", [TP, NT, D])
        x = S.sb("x", [TP, NT, D])
        w = S.sb("w", [128, KB, D])
        aT = S.sb("aT", [128, 2, KB, TP])
        bias = S.sb("bias", [TP, D])
        rows = S.sb("rows", [128, 2, KB if turn else D])
        stats = S.sb("stats", [TP, NT, 2, 6])
        mv = S.sb("mv", [TP, NT, 2])
        std = S.sb("std", [TP, NT])
        rstd = S.sb("rstd", [TP, NT])
        epst = S.sb("epst", [TP, 1])
        full = S.sb("full", [128, 2, KB, TP]) if turn else None
        tps = S.ps("tps", [128, 2, 1024])
        hps = S.ps("hps", [128, 2, 1024])
        split, full_ready = S.sem("split"), S.sem("full_ready")
        a_ld, xn_ld, x_ld = ([S.sem(f"{s}{half}") for half in range(2)] for s in ("a_ld", "xn_ld", "x_ld"))
        w_ld, bias_ld = S.sem("w_ld"), S.sem("bias_ld")
        rows_ld, chain = S.sem("rows_ld"), S.sem("chain")
        turned, kept, h_done, h_read, var_ready, std_ready = (S.sem(s) for s in (
            "turned", "kept", "h_done", "h_read", "var_ready", "std_ready"))
        normed, sum_ready, stored = S.sem("normed"), S.sem("sum_ready"), S.sem("stored")
        ahead_ld = S.sem("ahead_ld")
        with nc.Block() as block:
            @block.sync
            def _(sp):
                sp.dma_start(w[:], kblocks(w_d)).then_inc(w_ld, 16)
                sp.dma_start(bias[:], row_bcast(bias_d, TP)).then_inc(bias_ld, 16)
                for k, r in enumerate((gain, shift)):
                    if turn:
                        sp.dma_start(rows[:, k, :], r).then_inc(rows_ld, 16)
                    else:
                        sp.dma_start(rows[0:TP, k, :], row_bcast(r, TP)).then_inc(rows_ld, 16)
                for to, src_d, sem, half in ((a, attn_d, a_ld, 0), (h, xn_d, xn_ld, 0), (a, attn_d, a_ld, 1),
                                             (x, x_d, x_ld, 0), (h, xn_d, xn_ld, 1), (x, x_d, x_ld, 1)):
                    tiles = slice(half * NT // 2, (half + 1) * NT // 2)
                    sp.dma_start(to[:, tiles, :], tokens(src_d)[:, tiles, :]).then_inc(sem[half], 16)
                for to, src_d in ahead:
                    sp.dma_start(to, src_d).then_inc(ahead_ld, 16)
                for t in range(1, NT, 2):
                    sp.wait_ge(sum_ready, t + 1)
                    sp.dma_start(tokens(sum_d)[:, t - 1:t + 1, :], x[:, t - 1:t + 1, :]).then_inc(stored, 16)
                sp.wait_ge(stored, 16 * NT // 2)
                if ahead:
                    sp.wait_ge(ahead_ld, 16 * len(ahead))

            @block.tensor
            def _(pe):
                def turn_tile(t):
                    if t in (0, NT // 2):
                        pe.wait_ge(a_ld[2 * t // NT], 16)
                    if t >= 2:
                        pe.wait_ge(kept, t - 1)
                    for kb in range(KB):
                        ins = pe.transpose(tps[:, t % 2, kb * 128:kb * 128 + TP], a[:, t % NT, kb * 128:(kb + 1) * 128],
                                           ident[0:TP, 0:TP])
                    ins.then_inc(turned, 1)

                turn_tile(0)
                pe.wait_ge(w_ld, 16)
                for t in range(NT):
                    if t + 1 < NT:
                        turn_tile(t + 1)
                    pe.wait_ge(kept, t + 1)
                    if t >= 2:
                        pe.wait_ge(h_read, t - 1)
                    for c in range(2):
                        for kb in range(KB):
                            ins = pe.matmul(hps[0:TP, t % 2, c * 512:c * 512 + 384], aT[:, t % 2, kb, :],
                                            w[:, kb, c * 384:(c + 1) * 384], start=(kb == 0), stop=(kb == KB - 1))
                    ins.then_inc(h_done, 1)
                if turn:
                    for t in range(NT):
                        pe.wait_ge(normed, t + 1)
                        turn_tile(NT + t)

            @block.scalar
            def _(act):
                def root(t):
                    act.wait_ge(var_ready, t + 1)
                    act.activation(std[:, t:t + 1], mv[:, t, 1:2], ACT.Sqrt, bias=epst[:, 0:1]).then_inc(std_ready, 1)

                act.wait_ge(chain, 1)
                for t in range(NT):
                    act.wait_ge(turned, t + 1)
                    if t >= 2:
                        act.wait_ge(h_done, t - 1)
                    act.copy(aT[:, t % 2], tps[:, t % 2, 0:KB * 128].rearrange("p (kb n) -> p kb n", kb=KB)[:, :, 0:TP]
                             ).then_inc(kept, 1)
                    if t >= 2:
                        root(t - 2)
                root(NT - 2)
                root(NT - 1)
                if turn:
                    act.wait_ge(rows_ld, 32)
                    for t in range(NT):
                        act.wait_ge(turned, NT + t + 1)
                        if t >= 2:
                            act.wait_ge(split, 2 * t - 2)
                        for kb in range(KB):
                            ins = act.activation(full[:, t % 2, kb, :],
                                                 tps[:, t % 2, kb * 128:kb * 128 + TP], ACT.Identity,
                                                 scale=rows[:, 0, kb:kb + 1], bias=rows[:, 1, kb:kb + 1])
                        ins.then_inc(kept, 1)

            @block.vector
            def _(dve):
                steps_done = Chain(dve, chain)
                steps_done.done(dve.memset(epst[:], eps))
                dve.wait_ge(bias_ld, 16)
                if not turn:
                    dve.wait_ge(rows_ld, 32)

                def project(t):
                    if t in (0, NT // 2):
                        dve.wait_ge(xn_ld[2 * t // NT], 16)
                    steps_done.done(dve.tensor_tensor(h[:, t, :], h[:, t, :], bias[:], ALU.add))
                    dve.wait_ge(h_done, t + 1)
                    steps_done.wait()
                    both = h[:, t, :].rearrange("p (c n) -> p c n", c=2)
                    got = hps[0:TP, t % 2, :].rearrange("p (c n) -> p c n", c=2)[:, :, 0:384]
                    dve.tensor_tensor(both, both, got, ALU.add).then_inc(h_read, 1)
                    dve.wait_ge(h_read, t + 1)
                    for k in range(2):
                        steps_done.done(dve.bn_stats(stats[:, t, k, :], h[:, t, k * 384:(k + 1) * 384]))
                    steps_done.wait()
                    dve.bn_aggr(mv[:, t, :], stats[:, t, :, :]).then_inc(var_ready, 1)

                def normalise(t):
                    if t in (0, NT // 2):
                        dve.wait_ge(x_ld[2 * t // NT], 16)
                    if turn:
                        dve.tensor_tensor(x[:, t, :], x[:, t, :], h[:, t, :], ALU.add).then_inc(sum_ready, 1)
                    dve.wait_ge(std_ready, t + 1)
                    steps_done.done(dve.reciprocal(rstd[:, t:t + 1], std[:, t:t + 1]))
                    steps_done.wait()
                    dst = a[:, t, :] if turn else h[:, t, :]
                    dve.tensor_scalar(dst, h[:, t, :], mv[:, t, 0:1], rstd[:, t:t + 1],
                                      ALU.subtract, ALU.mult).then_inc(normed, 1)
                    if not turn:
                        dve.wait_ge(normed, t + 1)
                        steps_done.done(dve.tensor_tensor(h[:, t, :], h[:, t, :], rows[0:TP, 0, :], ALU.mult))
                        steps_done.done(dve.tensor_tensor(x[:, t, :], x[:, t, :], rows[0:TP, 1, :], ALU.add))
                        steps_done.wait()
                        dve.tensor_tensor(x[:, t, :], x[:, t, :], h[:, t, :], ALU.add).then_inc(sum_ready, 1)

                for t in range(NT):
                    project(t)
                    if t:
                        normalise(t - 1)
                normalise(NT - 1)
                if turn:
                    for t in range(NT):
                        dve.wait_ge(kept, NT + t + 1)
                        split_tile(dve, full[:, t % 2], yT, t, split)


def dense_stage(nc, name, xT, w_d, ob_n, bias_cols, func, outT):
    with Stage(nc, name) as S:
        w = S.sb("w", [128, ob_n, 128])
        bias = S.sb("bias", [128, ob_n])
        ps = S.ps("ps", [128, 2, 1536])
        in_ld, done, kept = S.sem("in_ld"), S.sem("done"), S.sem("kept")
        with nc.Block() as block:
            @block.sync
            def _(sp):
                sp.dma_start(w[:], w_d.rearrange("p (g n) -> p g n", g=ob_n)).then_inc(in_ld, 16)
                sp.dma_start(bias[:], bias_cols).then_inc(in_ld, 16)

            @block.tensor
            def _(pe):
                pe.wait_ge(in_ld, 32)
                for g in range(ob_n):
                    if g >= 2:
                        pe.wait_ge(kept, g - 1)
                    for c0, cn in CHUNKS:
                        ins = pe.matmul(ps[:, g % 2, c0:c0 + cn], w[:, g, :], xT[:, c0:c0 + cn], start=True, stop=True)
                    ins.then_inc(done, 1)

            @block.scalar
            def _(act):
                act.wait_ge(in_ld, 32)
                for g in range(ob_n):
                    act.wait_ge(done, g + 1)
                    act.activation(outT[:, g, :], ps[:, g % 2, 0:N], func, bias=bias[:, g:g + 1]).then_inc(kept, 1)


def fc1_stage(nc, yT, w_d, bias_cols, hidden, mask_d, rows_d, mx):
    ob_n, SB = 4 * KB, 16
    over = [hidden[0:TP, k0:k1].rearrange("p b n -> p (b n)") for k0, k1 in ((16, 21), (21, 23), (23, 24))]
    room = (over[0].bitcast(BF16).rearrange("p (t n) -> p t n", t=NT), over[1].rearrange("p (u n) -> p u n", u=2),
            over[2].bitcast(BF16).rearrange("p (u n) -> p u n", u=2))
    with Stage(nc, "fc1") as S:
        w = S.sb("w", [128, 2, KB, 128])
        w_hi, w_lo = S.sb("w_hi", [128, 2, KB, 128], F32R), S.sb("w_lo", [128, 2, KB, 128], F32R)
        bias = S.sb("bias", [128, ob_n])
        ps = S.ps("ps", [128, 2, 1536])
        w_ld = [S.sem("w_ld0"), S.sem("w_ld1")]
        bias_ld, w_high, w_split, done, kept = (S.sem(s) for s in ("bias_ld", "w_high", "w_split", "done", "kept"))
        scan = MaxScan(S, mask_d, rows_d, 8, mx, room)
        with nc.Block() as block:
            @block.sync
            def _(sp):
                sp.dma_start(bias[:], bias_cols).then_inc(bias_ld, 16)

                def load(g, u):
                    sp.dma_start(w[:, u], kblocks(w_d)[:, :, bass.ds(g * 128, 128)]).then_inc(w_ld[u], 16)

                load(0, 0)
                load(1, 1)
                with sp.Fori(0, ob_n // 2 - 1) as i:
                    for u in range(2):
                        sp.wait_ge(w_split, i * 2 + u + 1)
                        load(i * 2 + u + 2, u)

            @block.gpsimd
            def _(pool):
                scan.load(pool)

            @block.tensor
            def _(pe):
                with pe.Fori(0, ob_n // 2) as i:
                    for u in range(2):
                        pe.wait_ge(w_split, i * 2 + u + 1)
                        pe.wait_ge(kept, i * 2 + u + 1)
                        for c0, cn in CHUNKS:
                            for kb in range(KB):
                                for n, (wp, yp) in enumerate(((w_hi, 1), (w_lo, 0), (w_hi, 0))):
                                    ins = pe.matmul(ps[:, u, c0:c0 + cn], wp[:, u, kb, :], yT[yp][:, kb, c0:c0 + cn],
                                                    start=(kb == 0 and n == 0), stop=(kb == KB - 1 and n == 2))
                        ins.then_inc(done, 1)

            @block.scalar
            def _(act):
                def high(g, u, n):
                    act.wait_ge(w_ld[u], n * 16 + 16)
                    if not (isinstance(g, int) and g < 2):
                        act.wait_ge(done, g - 1)
                    act.copy(w_hi[:, u], w[:, u]).then_inc(w_high, 1)

                def gelu(g, u):
                    act.wait_ge(done, g + 1)
                    act.activation(hidden[:, bass.ds(g, 1), :], ps[:, u:u + 1, 0:N], ACT.Gelu_apprx_tanh,
                                   bias=bias[:, bass.ds(g, 1)]).then_inc(kept, 1)

                act.wait_ge(bias_ld, 16)
                act.nop().then_inc(kept, 2)
                high(0, 0, 0)
                high(1, 1, 0)
                gelu(0, 0)
                with act.Fori(0, SB // 2 - 1) as i:
                    for u in range(2):
                        high(i * 2 + u + 2, u, i + 1)
                        gelu(i * 2 + u + 1, 1 - u)
                act.wait_ge(scan.scanned, 8)
                with act.Fori(SB // 2 - 1, ob_n // 2 - 1) as i:
                    for u in range(2):
                        high(i * 2 + u + 2, u, i + 1)
                        gelu(i * 2 + u + 1, 1 - u)
                gelu(ob_n - 1, 1)

            @block.vector
            def _(dve):
                def low(g, u):
                    dve.wait_ge(w_high, g + 1)
                    dve.tensor_tensor(w_lo[:, u], w[:, u], w_hi[:, u].bitcast(F32), ALU.subtract).then_inc(w_split, 1)

                low(0, 0)
                low(1, 1)
                dve.wait_ge(scan.mask_ld, 16)
                scan.start(dve, 0, 0, 0)
                scan.tiles(dve, 0, 0, 0, NT // 2)
                low(2, 0)
                scan.tiles(dve, 0, 0, NT // 2, NT)
                scan.finish(dve, 0, 0)
                low(3, 1)
                scan.head(dve, 1, 1, 0)
                with dve.Fori(1, 4) as i:
                    for x in range(2):
                        hd = i * 2 + x
                        scan.start(dve, hd, x, i)
                        for half in range(2):
                            low(i * 4 + 2 * x + half, half)
                            scan.tiles(dve, hd, x, half * NT // 2, (half + 1) * NT // 2)
                        scan.finish(dve, hd, x)
                with dve.Fori(SB // 2, ob_n // 2) as i:
                    for u in range(2):
                        low(i * 2 + u, u)


def dense_add_stage(nc, name, ident, xT, kb_n, w_d, bias_cols, sum_d, out_d, ahead=()):
    ob_n = KB
    AS = 3
    with Stage(nc, name) as S:
        w = S.sb("w", [128, 2, kb_n, 128])
        bias = S.sb("bias", [128, ob_n])
        y = S.sb("y", [128, 2, N])
        acc = S.sb("acc", [TP, AS, NT, 128])
        ps = S.ps("ps", [128, 1536])
        tps = S.ps("tps", [128, 1536])
        w_ld = [S.sem("w_ld0"), S.sem("w_ld1")]
        acc_ld, stored = ([S.sem(f"{s}{u}") for u in range(AS)] for s in ("acc_ld", "stored"))
        bias_ld, done, kept, turned, summed = (S.sem(s) for s in ("bias_ld", "done", "kept", "turned", "summed"))
        ahead_ld = S.sem("ahead_ld")
        with nc.Block() as block:
            @block.sync
            def _(sp):
                sp.dma_start(bias[:], bias_cols).then_inc(bias_ld, 16)
                for g in range(ob_n + 2):
                    u = g % 2
                    cols = slice(g * 128, (g + 1) * 128)
                    if g < ob_n:
                        if g >= 2:
                            sp.wait_ge(done, 3 * (g - 1))
                        sp.dma_start(w[:, u], kblocks(w_d)[:, :, cols]).then_inc(w_ld[u], 16)
                        if g >= AS:
                            sp.wait_ge(stored[g % AS], 16 * (g // AS))
                        sp.dma_start(acc[:, g % AS], tokens(sum_d)[:, :, cols]).then_inc(acc_ld[g % AS], 16)
                    if g >= 2:
                        old = slice((g - 2) * 128, (g - 1) * 128)
                        sp.wait_ge(summed, g - 1)
                        sp.dma_start(tokens(out_d)[:, :, old], acc[:, (g - 2) % AS]).then_inc(stored[(g - 2) % AS], 16)
                    if g == 1:
                        for to, src_d in ahead:
                            sp.dma_start(to, src_d).then_inc(ahead_ld, 16)
                for u in range(AS):
                    sp.wait_ge(stored[u], 16 * (ob_n // AS))
                if ahead:
                    sp.wait_ge(ahead_ld, 16 * len(ahead))

            @block.tensor
            def _(pe):
                def turn_back(g):
                    pe.wait_ge(kept, 3 * (g + 1))
                    if g:
                        pe.wait_ge(summed, g)
                    for t in range(NT):
                        ins = pe.transpose(tps[0:TP, t * 128:(t + 1) * 128], y[:, g % 2, t * TP:(t + 1) * TP], ident[:])
                    ins.then_inc(turned, 1)

                for g in range(ob_n):
                    pe.wait_ge(w_ld[g % 2], 16 * (g // 2 + 1))
                    for c, (c0, cn) in enumerate(CHUNKS):
                        if g:
                            pe.wait_ge(kept, 3 * (g - 1) + c + 1)
                        for kb in range(kb_n):
                            ins = pe.matmul(ps[:, c0:c0 + cn], w[:, g % 2, kb, :], xT[:, kb, c0:c0 + cn],
                                            start=(kb == 0), stop=(kb == kb_n - 1))
                        ins.then_inc(done, 1)
                    if g:
                        turn_back(g - 1)
                turn_back(ob_n - 1)

            @block.scalar
            def _(act):
                act.wait_ge(bias_ld, 16)
                for g in range(ob_n):
                    for c, (c0, cn) in enumerate(CHUNKS):
                        act.wait_ge(done, 3 * g + c + 1)
                        if g >= 2:
                            act.wait_ge(turned, g - 1)
                        act.activation(y[:, g % 2, c0:c0 + cn], ps[:, c0:c0 + cn], ACT.Identity,
                                       bias=bias[:, g:g + 1]).then_inc(kept, 1)

            @block.vector
            def _(dve):
                for g in range(ob_n):
                    dve.wait_ge(turned, g + 1)
                    dve.wait_ge(acc_ld[g % AS], 16 * (g // AS + 1))
                    dve.tensor_tensor(acc[:, g % AS], acc[:, g % AS],
                                      tps[0:TP, 0:NT * 128].rearrange("p (t n) -> p t n", t=NT), ALU.add).then_inc(summed, 1)


def mask_stage(nc, ident, adj_d, mask_d, counts_d):
    with Stage(nc, "mask") as S:
        adj = S.sb("adj", [TP, NT, N])
        mask = S.sb("mask", [TP, NT, N], BF16)
        counts = S.sb("counts", [TP, NT, N], I16)
        tps = S.ps("tps", [128, 2, 2048])
        adj_ld = [S.sem(f"adj_ld{g}") for g in range(NT // 2)]
        turned, kept, stored = S.sem("turned"), S.sem("kept"), S.sem("stored")
        counted = S.sem("counted")
        with nc.Block() as block:
            @block.sync
            def _(sp):
                for g in range(NT // 2):
                    sp.dma_start(adj[:, 2 * g:2 * g + 2, :], tokens(adj_d)[:, 2 * g:2 * g + 2, :]).then_inc(adj_ld[g], 16)
                sp.wait_ge(counted, NT)
                sp.dma_start(tokens(counts_d), counts[:]).then_inc(stored, 16)
                sp.wait_ge(kept, NT)
                sp.dma_start(tokens(mask_d), mask[:]).then_inc(stored, 16)
                sp.wait_ge(stored, 32)

            @block.scalar
            def _(act):
                for s in range(NT):
                    act.wait_ge(adj_ld[s // 2], 16)
                    act.copy(counts[:, s, :], adj[:, s, :]).then_inc(counted, 1)

            @block.tensor
            def _(pe):
                for s in range(NT):
                    pe.wait_ge(adj_ld[s // 2], 16)
                    if s >= 2:
                        pe.wait_ge(kept, s - 1)
                    for d in range(NT):
                        ins = pe.transpose(tps[0:TP, s % 2, d * 128:d * 128 + TP], adj[:, s, d * TP:(d + 1) * TP],
                                           ident[0:TP, 0:TP])
                    ins.then_inc(turned, 1)

            @block.vector
            def _(dve):
                for s in range(NT):
                    dve.wait_ge(turned, s + 1)
                    dve.tensor_scalar(mask[:, :, s * TP:(s + 1) * TP],
                                      tps[0:TP, s % 2, 0:NT * 128].rearrange("p (d n) -> p d n", d=NT)[:, :, 0:TP],
                                      0.0, NEG, ALU.is_equal, ALU.mult).then_inc(kept, 1)


def gat_project_stage(nc, name, ident, x_d, k, act_kind, bias_d, w_d, heads, width, asrc_d, adst_d, h, a_s, a_d, rows_d,
                      ahead=(), h_d=None):
    kb_n = k // 128
    oc = heads * width
    half = oc // 2
    hh = max(heads // 2, 1)
    with Stage(nc, name) as S:
        w = S.sb("w", [128, WS, oc])
        w_hi, w_lo = S.sb("w_hi", [128, kb_n, oc], F32R), S.sb("w_lo", [128, kb_n, oc], F32R)
        x = S.sb("x", [TP, XS, k])
        neg = S.sb("neg", [TP, 2, k])
        bias = S.sb("bias", [TP, k])
        xT_hi, xT_lo = S.sb("xT_hi", [128, 2, kb_n, TP], F32R), S.sb("xT_lo", [128, 2, kb_n, TP], F32R)
        att = S.sb("att", [TP, 2, oc])
        prod = S.sb("prod", [TP, 2, oc])
        rows = S.sb("rows", [heads * NT, TP])
        tps = S.ps("tps", [128, 2, 1024])
        hps = S.ps("hps", [128, 2, 1024])
        x_ld = [S.sem(f"x_ld{u}") for u in range(XS)]
        ahead_ld, h_st = S.sem("ahead_ld"), S.sem("h_st")
        if h is None:
            h = S.sb("h", [TP, NT, heads, width + 1])
        w_ld, att_ld, bias_ld = [S.sem(f"w_ld{u}") for u in range(WS)], S.sem("att_ld"), S.sem("bias_ld")
        w_high, w_split, x_high = S.sem("w_high"), S.sem("w_split"), S.sem("x_high")
        x_ready, exp_ready, low_ready, chain = S.sem("x_ready"), S.sem("exp_ready"), S.sem("low_ready"), S.sem("chain")
        turned, kept, h_done, h_kept, reduced = (S.sem(s) for s in ("turned", "kept", "h_done", "h_kept", "reduced"))
        rows_turned, rows_kept, stored, ones_set = (S.sem(s) for s in ("rows_turned", "rows_kept", "stored", "ones_set"))
        plain = act_kind is None

        def turned_tile(t):
            return tps[:, t % 2, 0:kb_n * 128].rearrange("p (kb n) -> p kb n", kb=kb_n)[:, :, 0:TP]

        with nc.Block() as block:
            @block.sync
            def _(sp):
                if not plain:
                    sp.dma_start(bias[:], row_bcast(bias_d, TP)).then_inc(bias_ld, 16)
                for t in range(NT):
                    if t >= XS:
                        sp.wait_ge(turned, t - XS + 1)
                    sp.dma_start(x[:, t % XS, :], x_d[t * TP:(t + 1) * TP, :]).then_inc(x_ld[t % XS], 16)
                    if t == 1:
                        for kb in range(kb_n):
                            if kb >= WS:
                                sp.wait_ge(w_split, kb - WS + 1)
                            sp.dma_start(w[:, kb % WS, :], w_d[kb * 128:(kb + 1) * 128, :]).then_inc(w_ld[kb % WS], 16)
                        sp.dma_start(att[:, 0, :], row_bcast(asrc_d, TP)).then_inc(att_ld, 16)
                        sp.dma_start(att[:, 1, :], row_bcast(adst_d, TP)).then_inc(att_ld, 16)
                if h_d is not None:
                    sp.wait_ge(ones_set, 1)
                    for t in range(NT):
                        sp.wait_ge(h_kept, t + 1)
                        sp.dma_start(h_d[t * TP:(t + 1) * TP, :], h[:, t].rearrange("p h w -> p (h w)")).then_inc(h_st, 16)
                sp.wait_ge(rows_kept, 1)
                sp.dma_start(rows_d[0:heads * N].rearrange("(a n) -> a n", n=TP), rows[:]).then_inc(stored, 16)
                sp.wait_ge(stored, 16)
                if ahead:
                    sp.wait_ge(ahead_ld, 16 * len(ahead))
                if h_d is not None:
                    sp.wait_ge(h_st, 16 * NT)

            @block.gpsimd
            def _(pool):
                nc.gpsimd.memset(h[:, :, :, width:width + 1], 1.0).then_inc(ones_set, 1)

            @block.tensor
            def _(pe):
                def turn_tile(t):
                    if plain:
                        pe.wait_ge(x_ld[t % XS], 16 * (t // XS + 1))
                    else:
                        pe.wait_ge(x_ready, t + 1)
                    if t >= 2:
                        pe.wait_ge(kept, t - 1)
                    for kb in range(kb_n):
                        ins = pe.transpose(tps[:, t % 2, kb * 128:kb * 128 + TP], x[:, t % XS, kb * 128:(kb + 1) * 128],
                                           ident[0:TP, 0:TP])
                    ins.then_inc(turned, 1)

                turn_tile(0)
                for t in range(NT):
                    if t + 1 < NT:
                        turn_tile(t + 1)
                    pe.wait_ge(kept, t + 1)
                    if t >= 2:
                        pe.wait_ge(h_kept, t - 1)
                    for c in range(2):
                        cols = slice(c * half, (c + 1) * half)
                        for kb in range(kb_n):
                            if t == 0 and c == 0:
                                pe.wait_ge(w_split, kb + 1)
                            for n, (xp, wp) in enumerate(((xT_hi, w_lo), (xT_lo, w_hi), (xT_hi, w_hi))):
                                ins = pe.matmul(hps[0:TP, t % 2, c * 512:c * 512 + half], xp[:, t % 2, kb, :],
                                                wp[:, kb, cols], start=(kb == 0 and n == 0),
                                                stop=(kb == kb_n - 1 and n == 2))
                    ins.then_inc(h_done, 1)
                pe.wait_ge(reduced, NT * 2)
                pe.transpose(tps[0:heads * NT, 0, 0:TP], a_s[:].rearrange("p h t -> p (h t)"),
                             ident[0:TP, 0:TP]).then_inc(rows_turned, 1)

            @block.scalar
            def _(act):
                def keep_h(t):
                    act.wait_ge(h_done, t + 1)
                    for c in range(2):
                        got = hps[0:TP, t % 2, c * 512:c * 512 + half].rearrange("p (h c) -> p h c", h=hh)
                        to = h[:, t, c * hh:(c + 1) * hh, 0:width] if heads > 1 else h[:, t, :, c * half:(c + 1) * half]
                        ins = act.copy(to, got)
                    ins.then_inc(h_kept, 1)

                def exp_low(t):
                    act.wait_ge(low_ready, t + 1)
                    act.activation(neg[:, t % 2, :], neg[:, t % 2, :], ACT.Exp).then_inc(exp_ready, 1)

                def high(t):
                    act.wait_ge(turned, t + 1)
                    if t >= 2:
                        act.wait_ge(h_done, t - 1)
                    act.copy(xT_hi[:, t % 2], turned_tile(t)).then_inc(x_high, 1)

                if act_kind == "elu":
                    exp_low(0)
                    exp_low(1)
                high(0)
                for kb in range(kb_n):
                    act.wait_ge(w_ld[kb % WS], 16 * (kb // WS + 1))
                    act.copy(w_hi[:, kb, :], w[:, kb % WS, :]).then_inc(w_high, 1)
                for t in range(NT):
                    if act_kind == "elu" and t + 2 < NT:
                        exp_low(t + 2)
                    if t:
                        high(t)
                    if t == 1:
                        for to, src_d in ahead:
                            act.dma_start(to, src_d).then_inc(ahead_ld, 16)
                    if t:
                        keep_h(t - 1)
                keep_h(NT - 1)
                act.wait_ge(rows_turned, 1)
                act.copy(rows[:], tps[0:heads * NT, 0, 0:TP]).then_inc(rows_kept, 1)

            @block.vector
            def _(dve):
                steps_done = Chain(dve, chain)

                def terms(t):
                    dve.wait_ge(h_kept, t + 1)
                    for r, to in enumerate((a_s, a_d)):
                        steps_done.done(dve.tensor_tensor(
                            prod[:, r, :].rearrange("p (h c) -> p h c", h=heads), h[:, t, :, 0:width],
                            att[:, r, :].rearrange("p (h c) -> p h c", h=heads), ALU.mult))
                    steps_done.wait()
                    for r, to in enumerate((a_s, a_d)):
                        dve.tensor_reduce(to[:, :, t], prod[:, r, :].rearrange("p (h c) -> p h c", h=heads),
                                          AX.X, ALU.add).then_inc(reduced, 1)
                    dve.wait_ge(reduced, 2 * t + 2)

                def prepare(t):
                    dve.wait_ge(x_ld[t % XS], 16 * (t // XS + 1))
                    xt = x[:, t % XS, :]
                    steps_done.done(dve.tensor_tensor(xt, xt, bias[:], ALU.add))
                    steps_done.wait()
                    if act_kind == "relu":
                        dve.tensor_scalar(xt, xt, 0.0, None, ALU.max).then_inc(x_ready, 1)
                    else:
                        dve.tensor_scalar(neg[:, t % 2, :], xt, 0.0, None, ALU.min).then_inc(low_ready, 1)
                        dve.wait_ge(low_ready, t + 1)
                        steps_done.done(dve.tensor_scalar(xt, xt, 0.0, None, ALU.max))
                        steps_done.wait()
                        dve.wait_ge(exp_ready, t + 1)
                        steps_done.done(dve.tensor_scalar(neg[:, t % 2, :], neg[:, t % 2, :], -1.0, None, ALU.add))
                        steps_done.wait()
                        dve.tensor_tensor(xt, xt, neg[:, t % 2, :], ALU.add).then_inc(x_ready, 1)

                def low(t):
                    dve.wait_ge(x_high, t + 1)
                    dve.tensor_tensor(xT_lo[:, t % 2], turned_tile(t), xT_hi[:, t % 2].bitcast(F32),
                                      ALU.subtract).then_inc(kept, 1)

                if not plain:
                    dve.wait_ge(bias_ld, 16)
                    prepare(0)
                    prepare(1)
                low(0)
                for kb in range(kb_n):
                    dve.wait_ge(w_high, kb + 1)
                    dve.tensor_tensor(w_lo[:, kb, :], w[:, kb % WS, :], w_hi[:, kb, :].bitcast(F32),
                                      ALU.subtract).then_inc(w_split, 1)
                dve.wait_ge(att_ld, 32)
                for t in range(NT):
                    if not plain and t + 2 < NT:
                        prepare(t + 2)
                    if t:
                        low(t)
                    if t >= 2:
                        terms(t - 2)
                terms(NT - 2)
                terms(NT - 1)


class MaxScan:

    def __init__(self, S, mask, rows_d, heads, mx, room=None, slots=2):
        self.rows_d, self.heads, self.mx, self.slots = rows_d, heads, mx, slots
        self.mask_d = None if len(mask.shape) == 3 else mask
        if room is not None:
            self.mask, self.row, self.sums = room
        else:
            self.mask = mask if self.mask_d is None else S.sb("mask", [TP, NT, N], BF16)
            self.row = S.sb("row", [TP, slots, N])
            self.sums = S.sb("sums", [TP, 2, N], BF16)
        self.top = S.sb("top", [TP, 2, NT])
        self.mask_ld, self.row_ld = S.sem("mask_ld"), [S.sem("row_ld0"), S.sem("row_ld1")]
        self.top_done, self.scanned, self.paced = S.sem("top_done"), S.sem("scanned"), S.sem("paced")

    def load(self, eng):
        for hd in range(self.heads):
            u = hd % self.slots
            if hd >= self.slots:
                eng.wait_ge(self.top_done, (hd - self.slots + 1) * NT)
            eng.dma_start(self.row[:, u, :], row_bcast(self.rows_d[hd * N:(hd + 1) * N], TP)).then_inc(self.row_ld[u], 16)
            if hd == 0 and self.mask_d is not None:
                eng.dma_start(self.mask[:], tokens(self.mask_d)).then_inc(self.mask_ld, 16)

    def start(self, dve, hd, u, n):
        dve.wait_ge(self.row_ld[u], n * 16 + 16)
        if not (isinstance(hd, int) and hd == 0):
            dve.wait_ge(self.scanned, hd)
        dve.nop().then_inc(self.paced, 1)

    def tiles(self, dve, hd, u, d0, d1):
        for d in range(d0, d1):
            dve.tensor_tensor_reduce(self.sums[:, d % 2, :], self.mask[:, d, :], self.row[:, u, :], 1.0, NEG,
                                     ALU.add, ALU.max, self.top[:, u, d:d + 1]).then_inc(self.top_done, 1)
            if d % 2 == 1:
                dve.wait_ge(self.top_done, hd * NT + d + 1)
                dve.nop().then_inc(self.paced, 1)

    def finish(self, dve, hd, u):
        dve.tensor_copy(self.mx[:, bass.ds(hd, 1), :], self.top[:, u:u + 1, :]).then_inc(self.scanned, 1)

    def head(self, dve, hd, u, n):
        self.start(dve, hd, u, n)
        self.tiles(dve, hd, u, 0, NT)
        self.finish(dve, hd, u)


def gat_shift_stage(nc, name, ident, heads, a_s, a_d, mx, a_s02, shift_d, scan=None):
    with Stage(nc, name) as S:
        m = S.sb("m", [TP, heads, NT])
        shift = S.sb("shift", [TP, 2, heads, NT])
        rows = S.sb("rows", [heads * NT, 2, TP])
        tps = S.ps("tps", [128, 2, 512])
        chain, shift_ready = S.sem("chain"), S.sem("shift_ready")
        turned, kept, stored = S.sem("turned"), S.sem("kept"), S.sem("stored")
        scan = MaxScan(S, *scan) if scan is not None else None
        with nc.Block() as block:
            @block.sync
            def _(sp):
                if scan is not None:
                    scan.load(sp)
                sp.wait_ge(kept, 2)
                sp.dma_start(shift_d[:, 0:heads * N].rearrange("r (a n) -> a r n", n=TP), rows[:]).then_inc(stored, 16)
                sp.wait_ge(stored, 16)

            @block.vector
            def _(dve):
                steps_done = Chain(dve, chain)
                if scan is not None:
                    for hd in range(heads):
                        scan.head(dve, hd, hd % 2, hd // 2)
                    dve.wait_ge(scan.scanned, heads)
                steps_done.done(dve.tensor_tensor(mx[:], mx[:], a_d[:], ALU.add))
                steps_done.done(dve.tensor_scalar(a_s02[:], a_s[:], 0.2, None, ALU.mult))
                steps_done.wait()
                steps_done.done(dve.scalar_tensor_tensor(out=m[:], in0=mx[:], scalar=0.2, in1=mx[:],
                                                         op0=ALU.mult, op1=ALU.max))
                steps_done.wait()
                dve.tensor_tensor(shift[:, 0], a_d[:], m[:], ALU.subtract).then_inc(shift_ready, 1)
                dve.scalar_tensor_tensor(out=shift[:, 1], in0=a_d[:], scalar=0.2, in1=m[:],
                                         op0=ALU.mult, op1=ALU.subtract).then_inc(shift_ready, 1)
                for r in range(2):
                    dve.wait_ge(turned, r + 1)
                    dve.tensor_copy(rows[:, r, :], tps[0:heads * NT, r, 0:TP]).then_inc(kept, 1)

            @block.tensor
            def _(pe):
                pe.wait_ge(shift_ready, 2)
                for r in range(2):
                    pe.transpose(tps[0:heads * NT, r, 0:TP], shift[:, r].rearrange("p h t -> p (h t)"),
                                 ident[0:TP, 0:TP]).then_inc(turned, 1)


def gat_attend_stage(nc, name, adj, heads, width, h, a_s, a_s02, shift_d, out_d, h_d=None, base_d=None, bias_d=None):
    per = width if heads > 1 else 128
    starts = [0] if heads > 1 else list(range(width - per, -1, -per))
    banks = [(0, 3), (3, 3), (6, 3), (9, 1)]
    n_out = heads * len(starts)
    ES4 = 4
    with Stage(nc, name) as S:
        if h is None:
            h = S.sb("h", [TP, NT, heads, width + 1])
        h_ld = [S.sem(f"h_ld{t}") for t in range(NT)] if h_d is not None else None
        sh = S.sb("sh", [TP, min(heads, 2), 2, N])
        e1 = S.sb("e1", [TP, ES4, N])
        e2 = S.sb("e2", [TP, ES4, N])
        p = S.sb("p", [TP, NT, N])
        den = S.sb("den", [TP, NT])
        rden = S.sb("rden", [TP, NT])
        o = S.sb("o", [TP, 2, NT, per])
        ops = S.ps("ops", [128, 2, 4, 512])
        sh_ld, o_st = [S.sem("sh_ld0"), S.sem("sh_ld1")], [S.sem("o_st0"), S.sem("o_st1")]
        e_done, larger, p_done, p_used = S.sem("e_done"), S.sem("larger"), S.sem("p_done"), S.sem("p_used")
        chain, o_done, o_kept = S.sem("chain"), S.sem("o_done"), S.sem("o_kept")
        if heads == 1:
            base, bias = S.sb("base", [TP, 2, NT, per]), S.sb("bias", [TP, width])
            base_ld, bias_ld = [S.sem("base_ld0"), S.sem("base_ld1")], S.sem("bias_ld")
            based, o_sum = S.sem("based"), S.sem("o_sum")

        def span(k):
            return per + 1 if k == 0 else per

        def loop(eng, body):
            if heads == 1:
                body(0, 0)
            else:
                with eng.Fori(0, heads // 2) as i:
                    for u in range(2):
                        body(i * 2 + u, u)

        with nc.Block() as block:
            @block.sync
            def _(sp):
                for u in range(2):
                    sp.nop().then_inc(o_st[u], 16)

                def load(hd, u):
                    for r in range(2):
                        src = shift_d[r, bass.ds(hd * N, N)]
                        sp.dma_start(sh[:, u, r, :], row_bcast(src, TP)).then_inc(sh_ld[u], 16)

                load(0, 0)
                if h_d is not None:
                    for t in range(NT):
                        sp.dma_start(h[:, t].rearrange("p h w -> p (h w)"), h_d[t * TP:(t + 1) * TP, :]).then_inc(h_ld[t], 16)
                if heads > 1:
                    load(1, 1)

                def store(k, u, c0):
                    sp.dma_start(tokens(out_d)[:, :, bass.ds(c0, per)], o[:, u]).then_inc(o_st[u], 16)

                if heads == 1:
                    def load_base(k):
                        c0 = starts[k]
                        sp.dma_start(base[:, k % 2], tokens(base_d)[:, :, c0:c0 + per]).then_inc(base_ld[k % 2], 16)

                    sp.dma_start(bias[:], row_bcast(bias_d, TP)).then_inc(bias_ld, 16)
                    load_base(0)
                    load_base(1)
                    for k, c0 in enumerate(starts):
                        sp.wait_ge(o_sum, k + 1)
                        store(k, k % 2, c0)
                        if k + 2 < len(starts):
                            load_base(k + 2)
                else:
                    with sp.Fori(0, heads // 2 - 1) as i:
                        for u in range(2):
                            sp.wait_ge(e_done, (i * 2 + u + 1) * 2 * NT)
                            load(i * 2 + u + 2, u)
                            sp.wait_ge(o_kept, (i * 2 + u + 3) * 4)
                            store(i * 2 + u, u, (i * 2 + u) * per)
                    for u in range(2):
                        sp.wait_ge(o_kept, (heads + 1 + u) * 4)
                        store(heads - 2 + u, u, (heads - 2 + u) * per)
                for u in range(2):
                    sp.wait_ge(o_st[u], 16 * (n_out // 2) + 16)

            @block.scalar
            def _(act):
                def body(hd, u):
                    act.wait_ge(sh_ld[u], (hd - u) * 16 + 32)
                    for s in range(NT):
                        n = (u * NT + s) % ES4
                        act.wait_ge(p_done, hd * NT + s + 1)
                        act.activation(e1[:, n, :], sh[:, u, 0, :], ACT.Exp,
                                       bias=a_s[:, bass.ds(hd, 1), s]).then_inc(e_done, 1)
                        act.activation(e2[:, n, :], sh[:, u, 1, :], ACT.Exp,
                                       bias=a_s02[:, bass.ds(hd, 1), s]).then_inc(e_done, 1)

                loop(act, body)

            @block.vector
            def _(dve):
                dve.nop().then_inc(p_done, ES4)
                dve.nop().then_inc(o_kept, 8)

                def normalise(hd, k, u):
                    n = hd * len(starts) + k
                    w = span(k)
                    steps_done = Chain(dve, chain, hd * 5)
                    if heads > 1:
                        dve.wait_ge(p_used, (hd + 2) * NT)
                    else:
                        dve.wait_ge(o_done, n + 1)
                    dve.wait_ge(o_st[u], (n - u) * 8 + 16)
                    got = [ops[0:TP, u, b, 0:tn * w].rearrange("p (t w) -> p t w", t=tn) for b, (_, tn) in enumerate(banks)]
                    if k == 0:
                        for (t0, tn), a in zip(banks, got):
                            steps_done.done(dve.tensor_scalar(den[:, t0:t0 + tn], a[:, :, per], 1e-16, None, ALU.add))
                        steps_done.wait()
                        steps_done.done(dve.reciprocal(rden[:], den[:]))
                        steps_done.wait()
                    for (t0, tn), a in zip(banks, got):
                        dve.tensor_tensor(o[:, u, t0:t0 + tn, :], a[:, :, 0:per],
                                          rden[:, t0:t0 + tn].unsqueeze(2).to_broadcast([TP, tn, per]),
                                          ALU.mult).then_inc(o_kept, 1)

                def add_base(k):
                    cols = bias[:, starts[k]:starts[k] + per].unsqueeze(1).to_broadcast([TP, NT, per])
                    dve.wait_ge(base_ld[k % 2], 16 * (k // 2 + 1))
                    dve.tensor_tensor(base[:, k % 2], base[:, k % 2], cols, ALU.add).then_inc(based, 1)
                    dve.wait_ge(o_kept, 4 * (k + 3))
                    dve.wait_ge(based, k + 1)
                    dve.tensor_tensor(o[:, k % 2], o[:, k % 2], base[:, k % 2], ALU.add).then_inc(o_sum, 1)

                def larger_of(hd, u, s):
                    n = (u * NT + s) % ES4
                    dve.wait_ge(e_done, (hd * NT + s) * 2 + 2)
                    dve.tensor_tensor(e1[:, n, :], e1[:, n, :], e2[:, n, :], ALU.max).then_inc(larger, 1)

                def weights(hd, u, before=None):
                    larger_of(hd, u, 0)
                    for s in range(NT):
                        if s == 4 and before is not None:
                            normalise(*before)
                        if s + 1 < NT:
                            larger_of(hd, u, s + 1)
                        dve.wait_ge(p_used, hd * NT + s + 1)
                        dve.wait_ge(larger, hd * NT + s + 1)
                        dve.scalar_tensor_tensor(out=p[:, s, :], in0=e1[:, (u * NT + s) % ES4, :], scalar=1.0,
                                                 in1=adj[:, s, :], op0=ALU.min, op1=ALU.mult).then_inc(p_done, 1)

                weights(0, 0)
                if heads == 1:
                    dve.wait_ge(bias_ld, 16)
                    for k in range(len(starts)):
                        normalise(0, k, k % 2)
                        add_base(k)
                else:
                    with dve.Fori(0, heads // 2 - 1) as i:
                        for u in range(2):
                            weights(i * 2 + u + 1, 1 - u, (i * 2 + u, 0, u))
                    weights(heads - 1, 1, (heads - 2, 0, 0))
                    normalise(heads - 1, 0, 1)

            @block.tensor
            def _(pe):
                def block_sums(hd, k, c0, u):
                    n = hd * len(starts) + k
                    w = span(k)
                    if heads > 1:
                        pe.wait_ge(o_kept, (n - u) * 4 + 4 * u + 4)
                    elif k >= 2:
                        pe.wait_ge(o_kept, (k + 1) * 4)
                    for s in range(NT):
                        pe.wait_ge(p_done, hd * NT + s + 1 + ES4)
                        if h_d is not None:
                            pe.wait_ge(h_ld[s], 16)
                        rhs = h[:, s, bass.ds(hd, 1), c0:c0 + w]
                        for b, (t0, tn) in enumerate(banks):
                            for t in range(tn):
                                ins = pe.matmul(ops[0:TP, u, b, t * w:(t + 1) * w],
                                                p[:, s, (t0 + t) * TP:(t0 + t + 1) * TP], rhs,
                                                start=(s == 0 and t == 0), stop=(s == NT - 1), skip_group_check=True)
                        if heads > 1:
                            ins.then_inc(p_used, 1)
                    if heads == 1:
                        ins.then_inc(o_done, 1)

                def body(hd, u):
                    for k, c0 in enumerate(starts):
                        block_sums(hd, k, c0, u if heads > 1 else k % 2)

                pe.nop().then_inc(p_used, NT)
                loop(pe, body)


def router_stage(nc, ident, xT, p_d, c_d, w1_d, b1_d, z_parts_d, w1_parts_d, b1_parts_d, w_parts_d, wT):
    sm = ES * EM
    with Stage(nc, "router") as S:
        pw = S.sb("pw", [128, KB, 128])
        cb = S.sb("cb", [128, sm])
        zT = S.sb("zT", [128, N])
        zp = S.sb("zp", [128, 3, N], BF16)
        raw = S.sb("raw", [TP, 2, 2, ES, EM])
        e = S.sb("e", [TP, 2, 2, ES, EM])
        top = S.sb("top", [TP, 2, ES, 8])
        tot = S.sb("tot", [TP, ES])
        rtot = S.sb("rtot", [TP, ES])
        wgt = S.sb("wgt", [TP, 2, sm])
        w16 = S.sb("w16", [128, 2, 4, N], F16)
        rest = S.sb("rest", [128, 4, N])
        w1 = S.sb("w1", [128, EM * EH])
        w1p = S.sb("w1p", [128, 3, EM * EH], BF16)
        b1 = S.sb("b1", [ES, EM * EH])
        b1p = S.sb("b1p", [ES, 3, EM * EH], BF16)
        zps = S.ps("zps", [128, 1536])
        sps = S.ps("sps", [128, 2, 512])
        wps = S.ps("wps", [128, 2, 512])
        p_ld, c_ld, w1_ld, b1_ld, cb_zero = (S.sem(s) for s in ("p_ld", "c_ld", "w1_ld", "b1_ld", "cb_zero"))
        z_done, z_kept, s_done, s_kept = (S.sem(s) for s in ("z_done", "z_kept", "s_done", "s_kept"))
        diff, exp_done, chosen, turned, w_kept = (S.sem(s) for s in ("diff", "exp_done", "chosen", "turned", "w_kept"))
        chain, z_split, w_split, w1_split, b1_split, stored, pchain = (S.sem(s) for s in (
            "chain", "z_split", "w_split", "w1_split", "b1_split", "stored", "pchain"))
        with nc.Block() as block:
            @block.sync
            def _(sp):
                sp.dma_start(pw[:], kblocks(p_d)).then_inc(p_ld, 16)
                sp.wait_ge(cb_zero, 1)
                for s in range(ES):
                    sp.dma_start(cb[s * ER:(s + 1) * ER, s * EM:(s + 1) * EM], c_d[s]).then_inc(c_ld, 16)
                sp.dma_start(w1[:], w1_d.rearrange("s r n -> (s r) n")).then_inc(w1_ld, 16)
                sp.dma_start(b1[:], b1_d).then_inc(b1_ld, 16)
                sp.wait_ge(z_split, 3)
                sp.dma_start(z_parts_d.rearrange("k p n -> p k n"), zp[:]).then_inc(stored, 16)
                sp.wait_ge(w1_split, 3)
                sp.dma_start(w1_parts_d.rearrange("k p n -> p k n"), w1p[:]).then_inc(stored, 16)
                sp.wait_ge(b1_split, 3)
                sp.dma_start(b1_parts_d.rearrange("k p n -> p k n"), b1p[:]).then_inc(stored, 16)
                sp.wait_ge(w_split, 2)
                to = w_parts_d.rearrange("(b two) (k m) n -> two k m b n", two=2, k=2)
                for two in range(2):
                    for k in range(2):
                        sp.dma_start(to[two, k], w16[two * EM:(two + 1) * EM, k]).then_inc(stored, 16)
                sp.wait_ge(stored, 16 * 7)

            @block.gpsimd
            def _(pool):
                steps_done = Chain(pool, pchain)
                for src, parts, ld, split in ((w1, w1p, w1_ld, w1_split), (b1, b1p, b1_ld, b1_split)):
                    pool.wait_ge(ld, 16)
                    for k in range(3):
                        nc.gpsimd.tensor_copy(parts[:, k, :], src[:]).then_inc(split, 1)
                        pool.wait_ge(split, k + 1)
                        if k < 2:
                            steps_done.done(nc.gpsimd.tensor_tensor(src[:], src[:], parts[:, k, :], ALU.subtract))
                            steps_done.wait()

            @block.tensor
            def _(pe):
                pe.wait_ge(p_ld, 16)
                for c0, cn in CHUNKS:
                    for kb in range(KB):
                        ins = pe.matmul(zps[:, c0:c0 + cn], pw[:, kb, :], xT[:, kb, c0:c0 + cn],
                                        start=(kb == 0), stop=(kb == KB - 1))
                ins.then_inc(z_done, 1)
                pe.wait_ge(z_kept, 1)
                pe.wait_ge(c_ld, 16 * ES)

                def scores(t):
                    if t >= 2:
                        pe.wait_ge(s_kept, t - 1)
                    pe.matmul(sps[0:TP, t % 2, :], zT[:, t * TP:(t + 1) * TP], cb[:], start=True, stop=True).then_inc(s_done, 1)

                scores(0)
                for t in range(NT):
                    if t + 1 < NT:
                        scores(t + 1)
                    pe.wait_ge(chosen, t + 1)
                    if t >= 2:
                        pe.wait_ge(w_kept, t - 1)
                    for b in range(4):
                        ins = pe.transpose(wps[:, t % 2, b * 128:b * 128 + TP], wgt[:, t % 2, b * 128:(b + 1) * 128],
                                           ident[0:TP, 0:TP])
                    ins.then_inc(turned, 1)

            @block.scalar
            def _(act):
                act.wait_ge(z_done, 1)
                act.copy(zT[:], zps[:, 0:N]).then_inc(z_kept, 1)

                def keep_scores(t):
                    act.wait_ge(s_done, t + 1)
                    if t >= 2:
                        act.wait_ge(exp_done, t - 1)
                    act.copy(raw[:, t % 2, 0].rearrange("p s m -> p (s m)"), sps[0:TP, t % 2, :]).then_inc(s_kept, 1)

                keep_scores(0)
                for t in range(NT):
                    if t + 1 < NT:
                        keep_scores(t + 1)
                    act.wait_ge(diff, 2 * t + 2)
                    if t >= 2:
                        act.wait_ge(chosen, t - 1)
                    act.activation(e[:, t % 2], raw[:, t % 2], ACT.Exp).then_inc(exp_done, 1)
                    act.wait_ge(turned, t + 1)
                    act.copy(wT[:, :, t * TP:(t + 1) * TP],
                             wps[:, t % 2, :].rearrange("p (b n) -> p b n", b=4)[:, :, 0:TP]).then_inc(w_kept, 1)

            @block.vector
            def _(dve):
                steps_done = Chain(dve, chain)
                dve.memset(cb[:], 0.0).then_inc(cb_zero, 1)
                dve.wait_ge(z_kept, 1)
                for t in range(NT):
                    u = t % 2
                    sc, less = raw[:, u, 0], raw[:, u, 1]
                    dve.wait_ge(s_kept, t + 1)
                    for s in range(ES):
                        steps_done.done(dve.max(top[:, u, s, :], sc[:, s, :]))
                    steps_done.wait()
                    steps_done.done(dve.memset(top[:, u, :, 4:8], -NEG))
                    steps_done.wait()
                    for s in range(ES):
                        steps_done.done(dve.match_replace(less[:, s, :], top[:, u, s, :], sc[:, s, :], NEG))
                    steps_done.wait()
                    best = top[:, u, :, 0:1].to_broadcast([TP, ES, EM])
                    for k in range(2):
                        dve.tensor_tensor(raw[:, u, k], raw[:, u, k], best, ALU.subtract).then_inc(diff, 1)
                    dve.wait_ge(exp_done, t + 1)
                    steps_done.done(dve.tensor_tensor(e[:, u, 0], e[:, u, 0], e[:, u, 1], ALU.subtract))
                    steps_done.wait()
                    steps_done.done(dve.tensor_reduce(tot[:], e[:, u, 0], AX.X, ALU.add))
                    steps_done.wait()
                    steps_done.done(dve.reciprocal(rtot[:], tot[:]))
                    steps_done.wait()
                    if t >= 2:
                        dve.wait_ge(turned, t - 1)
                    dve.tensor_tensor(wgt[:, u, :].rearrange("p (s m) -> p s m", s=ES), e[:, u, 0],
                                      rtot[:].unsqueeze(2).to_broadcast([TP, ES, EM]), ALU.mult).then_inc(chosen, 1)
                dve.wait_ge(s_done, NT)
                for k in range(3):
                    dve.tensor_copy(zp[:, k, :], zT[:]).then_inc(z_split, 1)
                    dve.wait_ge(z_split, k + 1)
                    if k < 2:
                        steps_done.done(dve.tensor_tensor(zT[:], zT[:], zp[:, k, :], ALU.subtract))
                        steps_done.wait()
                dve.wait_ge(w_kept, NT)
                dve.tensor_copy(w16[:, 0], wT[:]).then_inc(w_split, 1)
                dve.wait_ge(w_split, 1)
                steps_done.done(dve.tensor_tensor(rest[:], wT[:], w16[:, 0], ALU.subtract))
                steps_done.wait()
                dve.tensor_scalar(w16[:, 1], rest[:], 4096.0, None, ALU.mult).then_inc(w_split, 1)


def expert_stage(nc, z_parts_d, w1_parts_d, b1_parts_d, w_parts_d, spread_d, w2_d, b2_d, wT, comb_d):
    chunk = [(0, 417), (417, 417), (834, 416)]
    per_chunk = EJ
    steps = 3 * per_chunk
    LEAD = 2
    W = 3 * EG
    with Stage(nc, "expert") as S:
        z = S.sb("z", [128, 2, N], BF16)
        w1 = S.sb("w1", [128, 2, EM * EH], BF16)
        wp = S.sb("wp", [128, 2, N], F16)
        spread = S.sb("spread", [128, EJ, 128], F16)
        w2 = S.sb("w2", [128, 2, EJ + 1, ER])
        b2 = S.sb("b2", [128, 2, 32])
        gel = S.sb("gel", [128, 3, 512])
        wgel = S.sb("wgel", [128, W, 512])
        comb = S.sb("comb", [128, 2, N])
        hps = S.ps("hps", [128, 3, 512])
        wps = S.ps("wps", [128, 3, 512])
        cps = S.ps("cps", [128, 2, 512])
        in_ld, stored = [S.sem("in_ld0"), S.sem("in_ld1")], [S.sem("stored0"), S.sem("stored1")]
        spread_ld, const_set = S.sem("spread_ld"), S.sem("const_set")
        h_done, w_done, gel_done, wgel_done, w2_done, comb_kept = (S.sem(s) for s in (
            "h_done", "w_done", "gel_done", "wgel_done", "w2_done", "comb_kept"))
        n_in = len(NPART) * 2 + 3 + 3

        def at(q):
            u, c, j = q // steps, q % steps // per_chunk, q % per_chunk
            return u, c, 3 * u + c, j, chunk[c][0], chunk[c][1]

        with nc.Block() as block:
            @block.sync
            def _(sp):
                for u in range(2):
                    sp.nop().then_inc(stored[u], 16 * EG)
                sp.dma_start(spread[:], spread_d.rearrange("p (j n) -> p j n", j=EJ)).then_inc(spread_ld, 16)
                sp.wait_ge(const_set, 7)

                def load(s, u):
                    rows = bass.ds(s * ER, ER)
                    for k, (a, b) in enumerate(NPART):
                        sp.dma_start(z[k * ER:(k + 1) * ER, u, :], z_parts_d[a, rows, :]).then_inc(in_ld[u], 16)
                        sp.dma_start(w1[k * ER:(k + 1) * ER, u, :], w1_parts_d[b, rows, :]).then_inc(in_ld[u], 16)
                    for k in range(3):
                        sp.dma_start(w1[len(NPART) * ER + k:len(NPART) * ER + k + 1, u, :],
                                     b1_parts_d[k, bass.ds(s, 1), :]).then_inc(in_ld[u], 16)
                    sp.dma_start(wp[:, u, :], w_parts_d[bass.ds(s, 1), :, :].rearrange("a p n -> (a p) n")).then_inc(in_ld[u], 16)
                    sp.dma_start(w2[:, u, 0:EJ, :], w2_d[bass.ds(s, 1)].rearrange("a p j r -> (a p) j r")).then_inc(in_ld[u], 16)
                    sp.dma_start(b2[u * EM:(u + 1) * EM, u, 0:ER],
                                 b2_d[bass.ds(s, 1)].rearrange("a m r -> (a m) r")).then_inc(in_ld[u], 16)

                def store(s, u):
                    for e in range(EG):
                        sp.dma_start(comb_d[e, bass.ds(s * ER, ER), :], comb[32 * e:32 * e + ER, u, :]).then_inc(stored[u], 16)

                load(0, 0)
                load(1, 1)
                with sp.Fori(0, ES // 2 - 1) as i:
                    for u in range(2):
                        sp.wait_ge(w2_done, i * 2 * steps + (u + 1) * steps + W)
                        load(i * 2 + u + 2, u)
                        sp.wait_ge(comb_kept, i * 6 + 3 * u + 5)
                        store(i * 2 + u, u)
                for u in range(2):
                    sp.wait_ge(comb_kept, 3 * (ES - 1 + u) + 2)
                    store(ES - 2 + u, u)
                for u in range(2):
                    sp.wait_ge(stored[u], 16 * EG * (ES // 2) + 16 * EG)

            @block.tensor
            def _(pe):
                pe.wait_ge(spread_ld, 16)
                pe.wait_ge(const_set, 7)
                pe.nop().then_inc(w2_done, W)
                with pe.Fori(0, ES // 2) as i:
                    base = i * (2 * steps)

                    def hidden(q):
                        u, c, ch, j, c0, cn = at(q)
                        if q % steps == 0:
                            pe.wait_ge(in_ld[u], i * 16 * n_in + 16 * n_in)
                        pe.wait_ge(gel_done, base + q + 1)
                        pe.matmul(hps[:, q % 3, 0:cn], w1[0:ZK, u, j * 128:(j + 1) * 128], z[0:ZK, u, c0:c0 + cn],
                                  start=True, stop=True).then_inc(h_done, 1)

                    def weights(q):
                        u, c, ch, j, c0, cn = at(q)
                        pe.wait_ge(wgel_done, base + q + 1)
                        pe.matmul(wps[:, q % 3, 0:cn], spread[:, j, :], wp[:, u, c0:c0 + cn],
                                  start=True, stop=True).then_inc(w_done, 1)

                    def sums(q0):
                        u, c, ch, j0, c0, cn = at(q0)
                        if j0 == 0:
                            pe.matmul(cps[0:32, ch % 2, 0:cn], b2[:, u, :], wT[:, bass.ds(i, 1), c0:c0 + cn],
                                      start=True, stop=False, tile_position=(0, 0), skip_group_check=True)
                        pe.wait_ge(wgel_done, base + q0 + EG + 3)
                        for e in range(EG):
                            j = j0 + e
                            pe.matmul(cps[32 * e:32 * e + 32, ch % 2, 0:cn],
                                      w2[:, u, j:j + 2, :].rearrange("p j r -> p (j r)"), wgel[:, (q0 + e) % W, 0:cn],
                                      start=(j0 == 0 and e > 0), stop=(j0 + EG == EJ), tile_position=(0, 32 * e),
                                      skip_group_check=True).then_inc(w2_done, 1)

                    hidden(0)
                    hidden(1)
                    for q0 in range(0, 2 * steps, EG):
                        _, _, ch, j0, _, _ = at(max(q0 - 2 * EG, 0))
                        if q0 >= 2 * EG and j0 == 0:
                            pe.wait_ge(comb_kept, i * 6 + ch + 1)
                        for e in range(EG):
                            if e == LEAD and q0 >= 2 * EG:
                                sums(q0 - 2 * EG)
                            if q0 + e + 2 < 2 * steps:
                                hidden(q0 + e + 2)
                            weights(q0 + e)
                    sums(2 * steps - 2 * EG)
                    sums(2 * steps - EG)

            @block.scalar
            def _(act):
                act.nop().then_inc(gel_done, 3)
                with act.Fori(0, ES // 2) as i:
                    base = i * (2 * steps)
                    for q in range(2 * steps):
                        u, c, ch, j, c0, cn = at(q)
                        act.wait_ge(h_done, base + q + 1)
                        act.wait_ge(wgel_done, base + q + 1)
                        act.activation(gel[:, q % 3, 0:cn], hps[:, q % 3, 0:cn], ACT.Gelu_apprx_tanh).then_inc(gel_done, 1)

            @block.vector
            def _(dve):
                dve.nop().then_inc(wgel_done, 3)
                dve.nop().then_inc(comb_kept, 2)
                for u in range(2):
                    dve.memset(z[len(NPART) * ER:ZK, u, :], 1.0).then_inc(const_set, 1)
                    dve.memset(b2[(1 - u) * EM:(2 - u) * EM, u, 0:ER], 0.0).then_inc(const_set, 1)
                    dve.memset(b2[:, u, ER:32], 0.0).then_inc(const_set, 1)
                dve.memset(w2[:, :, EJ, :], 0.0).then_inc(const_set, 1)
                with dve.Fori(0, ES // 2) as i:
                    base = i * (2 * steps)

                    def keep_sums(ch):
                        u, c = ch // 3, ch % 3
                        c0, cn = chunk[c]
                        if c == 0:
                            dve.wait_ge(stored[u], i * 16 * EG + 16 * EG)
                        dve.wait_ge(w2_done, base + (ch + 1) * per_chunk + W)
                        dve.tensor_copy(comb[:, u, c0:c0 + cn], cps[:, ch % 2, 0:cn]).then_inc(comb_kept, 1)

                    for q in range(2 * steps):
                        u, c, ch, j, c0, cn = at(q)
                        if ch and j == 2 * EG:
                            keep_sums(ch - 1)
                        dve.wait_ge(gel_done, base + q + 4)
                        dve.wait_ge(w_done, base + q + 1)
                        if q % EG == 0:
                            dve.wait_ge(w2_done, base + q + EG)
                        dve.tensor_tensor(wgel[:, q % W, 0:cn], gel[:, q % 3, 0:cn], wps[:, q % 3, 0:cn],
                                          ALU.mult).then_inc(wgel_done, 1)
                    keep_sums(5)


def comb_stage(nc, comb_d, combT):
    with Stage(nc, "comb") as S:
        part = S.sb("part", [128, EG, N])
        part_ld, chain = [S.sem(f"part_ld{e}") for e in range(EG)], S.sem("chain")
        with nc.Block() as block:
            @block.sync
            def _(sp):
                for e in range(EG):
                    sp.dma_start(part[:, e, :], comb_d[e]).then_inc(part_ld[e], 16)

            @block.vector
            def _(dve):
                steps_done = Chain(dve, chain)
                dve.wait_ge(part_ld[0], 16)
                for e in range(1, EG):
                    dve.wait_ge(part_ld[e], 16)
                    if e > 1:
                        steps_done.wait()
                    steps_done.done(dve.tensor_tensor(combT[:], part[:, 0, :] if e == 1 else combT[:], part[:, e, :], ALU.add))


def load_rows_stage(nc, name, src_d, to):
    with Stage(nc, name) as S:
        loaded = S.sem("loaded")
        with nc.Block() as block:
            @block.sync
            def _(sp):
                sp.dma_start(to, src_d).then_inc(loaded, 16)
                sp.wait_ge(loaded, 16)


def bitlinear_stage(nc, ident, x_d, win_d, wout_d, gin_d, gout_d, out_d):
    H = wout_d.shape[0]
    ROUND = 1.5 * 2.0 ** 23
    layers = ((win_d, KB, 2 * H), (wout_d, H // 128, D))
    with Stage(nc, "bit") as S:
        x = S.sb("x", [TP, NT, D])
        xn = S.sb("xn", [TP, NT, D])
        y = S.sb("y", [TP, NT, H])
        gin = S.sb("gin", [TP, D])
        gout = S.sb("gout", [TP, H])
        win = S.sb("win", [128, KB, 2 * H])
        wout = S.sb("wout", [128, H // 128, D])
        winq = S.sb("winq", [128, KB, 2 * H], BF16)
        woutq = S.sb("woutq", [128, H // 128, D], BF16)
        stats = S.sb("stats", [TP, NT, 2, 6])
        mv = S.sb("mv", [TP, NT, 2])
        ssq = S.sb("ssq", [TP, 2, NT])
        std = S.sb("std", [TP, 3, NT])
        rstd = S.sb("rstd", [TP, 3, NT])
        epst = S.sb("epst", [128, 2])
        junk = S.sb("junk", [TP, 2, D])
        big = S.sb("big", [TP, 2, 2, NT])
        amax = S.sb("amax", [TP, 2, NT])
        ascale = S.sb("ascale", [TP, 2, NT])
        back = S.sb("back", [TP, 2, NT])
        wabs = S.sb("wabs", [128, 2])
        wmean = S.sb("wmean", [128, 2])
        wscale = S.sb("wscale", [128, 2])
        ones = S.sb("ones", [128, 128])
        identb = S.sb("identb", [128, 128], BF16)
        q = S.sb("q", [TP, 2, D], BF16)
        qT = S.sb("qT", [128, 2, KB, TP], BF16)
        sig = S.sb("sig", [TP, 2, H])
        tps = S.ps("tps", [128, 2, 1024], BF16)
        ups = S.ps("ups", [128, 2, 1024])
        mps = S.ps("mps", [128, 2])
        x_ld, g_ld, w_ld, const_set = [S.sem("x_ld0"), S.sem("x_ld1")], S.sem("g_ld"), S.sem("w_ld"), S.sem("const_set")
        chain, var_ready, std_ready, wsum_done, wmean_done, w_ready = (S.sem(s) for s in (
            "chain", "var_ready", "std_ready", "wsum_done", "wmean_done", "w_ready"))
        normed, sq_done, q_ready, turned, kept, up_done = (S.sem(s) for s in (
            "normed", "sq_done", "q_ready", "turned", "kept", "up_done"))
        sig_done, out_ready, stored, y_ready = (S.sem(s) for s in ("sig_done", "out_ready", "stored", "y_ready"))
        with nc.Block() as block:
            @block.sync
            def _(sp):
                for half in range(2):
                    tiles = slice(half * NT // 2, (half + 1) * NT // 2)
                    sp.dma_start(x[:, tiles, :], tokens(x_d)[:, tiles, :]).then_inc(x_ld[half], 16)
                sp.dma_start(win[:], kblocks(win_d)).then_inc(w_ld, 16)
                sp.dma_start(wout[:], kblocks(wout_d)).then_inc(w_ld, 16)
                sp.dma_start(gin[:], row_bcast(gin_d, TP)).then_inc(g_ld, 16)
                sp.dma_start(gout[:], row_bcast(gout_d, TP)).then_inc(g_ld, 16)
                for t in range(NT):
                    sp.wait_ge(out_ready, t + 1)
                    sp.dma_start(out_d[t * TP:(t + 1) * TP, :], x[:, t, :]).then_inc(stored, 16)
                sp.wait_ge(stored, 16 * NT)

            @block.tensor
            def _(pe):
                pe.wait_ge(const_set, 4)
                pe.wait_ge(wsum_done, 2)
                pe.matmul(mps[:, 0:2], ones[:], wabs[:], start=True, stop=True).then_inc(wmean_done, 1)
                pe.wait_ge(w_ready, 2)
                for r, wq in enumerate((winq, woutq)):
                    kb_n, cols = layers[r][1], layers[r][2]
                    cs = cols // 2
                    for t in range(NT):
                        n = r * NT + t
                        pe.wait_ge(q_ready, n + 1)
                        if n >= 2:
                            pe.wait_ge(kept, n - 1)
                        for kb in range(kb_n):
                            ins = pe.transpose(tps[:, n % 2, kb * 128:kb * 128 + TP], q[:, n % 2, kb * 128:(kb + 1) * 128],
                                               identb[0:TP, 0:TP])
                        ins.then_inc(turned, 1)
                        pe.wait_ge(kept, n + 1)
                        if n >= 2 and n - 2 < NT:
                            pe.wait_ge(y_ready, n - 1)
                        elif n >= 2:
                            pe.wait_ge(out_ready, n - 1 - NT)
                        for c in range(2):
                            for kb in range(kb_n):
                                ins = pe.matmul(ups[0:TP, n % 2, c * 512:c * 512 + cs], qT[:, n % 2, kb, :],
                                                wq[:, kb, c * cs:(c + 1) * cs], start=(kb == 0), stop=(kb == kb_n - 1))
                        ins.then_inc(up_done, 1)

            @block.scalar
            def _(act):
                act.wait_ge(const_set, 4)
                act.wait_ge(var_ready, NT)
                act.activation(std[:, 0, :], mv[:, :, 1], ACT.Sqrt, bias=epst[0:TP, 0:1]).then_inc(std_ready, 1)
                for r in range(2):
                    width = (D, H)[r]
                    for t in range(NT):
                        act.wait_ge(normed if r == 0 else y_ready, t + 1)
                        act.activation(junk[:, r, 0:width], xn[:, t, :] if r == 0 else y[:, t, :], ACT.Square,
                                       accum_out=ssq[:, r, t:t + 1]).then_inc(sq_done, 1)
                        act.wait_ge(sq_done, r * NT + t + 1)
                    act.activation(std[:, 1 + r, :], ssq[:, r, :], ACT.Sqrt, bias=epst[0:TP, 1:2],
                                   scale=1.0 / width).then_inc(std_ready, 1)
                    kb_n = layers[r][1]
                    for t in range(NT):
                        n = r * NT + t
                        act.wait_ge(turned, n + 1)
                        if n >= 2:
                            act.wait_ge(up_done, n - 1)
                        act.copy(qT[:, n % 2, 0:kb_n, :],
                                 tps[:, n % 2, 0:kb_n * 128].rearrange("p (kb n) -> p kb n", kb=kb_n)[:, :, 0:TP]).then_inc(kept, 1)
                        if r == 0:
                            act.wait_ge(up_done, n + 1)
                            if t >= 2:
                                act.wait_ge(y_ready, t - 1)
                            act.activation(sig[:, t % 2, :], ups[0:TP, n % 2, 512:512 + H], ACT.Silu,
                                           scale=back[:, 0, t:t + 1]).then_inc(sig_done, 1)

            @block.vector
            def _(dve):
                steps_done = Chain(dve, chain)
                dve.memset(epst[:, 0:1], 1e-5).then_inc(const_set, 1)
                dve.memset(epst[:, 1:2], 1e-6).then_inc(const_set, 1)
                dve.memset(ones[:], 1.0).then_inc(const_set, 1)
                dve.tensor_copy(identb[:], ident[:]).then_inc(const_set, 1)
                for t in range(NT):
                    if t in (0, NT // 2):
                        dve.wait_ge(x_ld[2 * t // NT], 16)
                    for k in range(2):
                        steps_done.done(dve.bn_stats(stats[:, t, k, :], x[:, t, k * 384:(k + 1) * 384]))
                    steps_done.wait()
                    dve.bn_aggr(mv[:, t, :], stats[:, t, :, :]).then_inc(var_ready, 1)
                dve.wait_ge(std_ready, 1)
                steps_done.done(dve.reciprocal(rstd[:, 0, :], std[:, 0, :]))
                steps_done.wait()
                dve.wait_ge(var_ready, NT)
                for t in range(NT):
                    dve.tensor_scalar(xn[:, t, :], x[:, t, :], mv[:, t, 0:1], rstd[:, 0, t:t + 1],
                                      ALU.subtract, ALU.mult).then_inc(normed, 1)
                dve.wait_ge(normed, NT)
                dve.wait_ge(w_ld, 32)
                for k, wt in enumerate((win, wout)):
                    dve.tensor_reduce(wabs[:, k:k + 1], wt[:], AX.XY, ALU.add, apply_absolute_value=True).then_inc(wsum_done, 1)
                dve.wait_ge(wmean_done, 1)
                for k, (_, kb_n, cols) in enumerate(layers):
                    steps_done.done(dve.tensor_scalar(wmean[:, k:k + 1], mps[:, k:k + 1], 1.0 / (kb_n * 128 * cols), 1e-5,
                                                      ALU.mult, ALU.max))
                steps_done.wait()
                steps_done.done(dve.reciprocal(wscale[:], wmean[:]))
                steps_done.wait()
                for k, (wt, wq) in enumerate(((win, winq), (wout, woutq))):
                    steps_done.done(dve.tensor_scalar(wt[:], wt[:], wscale[:, k:k + 1], ROUND, ALU.mult, ALU.add))
                    steps_done.wait()
                    steps_done.done(dve.tensor_scalar(wt[:], wt[:], ROUND, 1.0, ALU.subtract, ALU.min))
                    steps_done.wait()
                    dve.tensor_scalar(wq[:], wt[:], -1.0, None, ALU.max).then_inc(w_ready, 1)
                dve.wait_ge(g_ld, 32)
                for r in range(2):
                    rows, gain = ((xn, gin), (y, gout))[r]
                    width = (D, H)[r]
                    dve.wait_ge(std_ready, 2 + r)
                    steps_done.done(dve.reciprocal(rstd[:, 1 + r, :], std[:, 1 + r, :]))
                    steps_done.wait()
                    for t in range(NT):
                        steps_done.done(dve.scalar_tensor_tensor(out=rows[:, t, :], in0=rows[:, t, :],
                                                                 scalar=rstd[:, 1 + r, t:t + 1], in1=gain[:],
                                                                 op0=ALU.mult, op1=ALU.mult))
                    steps_done.wait()
                    steps_done.done(dve.tensor_reduce(amax[:, r, :], rows[:], AX.X, ALU.max, apply_absolute_value=True))
                    steps_done.wait()
                    steps_done.done(dve.tensor_scalar(amax[:, r, :], amax[:, r, :], 1e-5, None, ALU.max))
                    steps_done.wait()
                    steps_done.done(dve.reciprocal(ascale[:, r, :], amax[:, r, :]))
                    steps_done.done(dve.tensor_scalar(back[:, r, :], amax[:, r, :], wmean[0:TP, r:r + 1], 1.0 / 127.0,
                                                      ALU.mult, ALU.mult))
                    steps_done.wait()
                    steps_done.done(dve.tensor_scalar(ascale[:, r, :], ascale[:, r, :], 127.0, None, ALU.mult))
                    steps_done.wait()

                    def read_product(t):
                        n = r * NT + t
                        if r == 0:
                            dve.wait_ge(sig_done, t + 1)
                            ins = dve.scalar_tensor_tensor(out=y[:, t, :], in0=ups[0:TP, n % 2, 0:H],
                                                           scalar=back[:, 0, t:t + 1], in1=sig[:, t % 2, :],
                                                           op0=ALU.mult, op1=ALU.mult)
                            ins.then_inc(y_ready, 1)
                        else:
                            dve.wait_ge(up_done, n + 1)
                            got = ups[0:TP, n % 2, :].rearrange("p (c n) -> p c n", c=2)[:, :, 0:D // 2]
                            both = x[:, t, :].rearrange("p (c n) -> p c n", c=2)
                            dve.scalar_tensor_tensor(out=both, in0=got, scalar=back[:, 1, t:t + 1], in1=both,
                                                     op0=ALU.mult, op1=ALU.add).then_inc(out_ready, 1)

                    for t in range(NT):
                        n = r * NT + t
                        steps_done.done(dve.tensor_scalar(rows[:, t, :], rows[:, t, :], ascale[:, r, t:t + 1], ROUND,
                                                          ALU.mult, ALU.add))
                        steps_done.wait()
                        steps_done.done(dve.tensor_scalar(rows[:, t, :], rows[:, t, :], ROUND, 127.0, ALU.subtract, ALU.min))
                        steps_done.wait()
                        if n >= 2:
                            dve.wait_ge(turned, n - 1)
                        dve.tensor_scalar(q[:, n % 2, 0:width], rows[:, t, :], -128.0, None, ALU.max).then_inc(q_ready, 1)
                        if t:
                            read_product(t - 1)
                    read_product(NT - 1)


def gat_one_head(nc, name, ident, x_d, k, act_kind, bias_d, w_d, asrc_d, adst_d, counts, mask_d, rows_d, shift_d,
                 a_s, a_d, a_s02, mx, base_d, out_bias_d, out_d):
    one = [buf[:, 0:1, :] for buf in (a_s, a_d, mx, a_s02)]
    with nc.sbuf_tensor(f"{name}_h", [TP, NT, 1, D + 1], F32) as h:
        with nc.sbuf_tensor(f"{name}_mask", [TP, NT, N], BF16) as mask:
            gat_project_stage(nc, f"{name}proj", ident, x_d, k, act_kind, bias_d, w_d, 1, D, asrc_d, adst_d, h,
                              one[0], one[1], rows_d, ahead=[(mask[:], tokens(mask_d))])
            gat_shift_stage(nc, f"{name}max", ident, 1, *one, shift_d, scan=(mask, rows_d, 1, one[2]))
        gat_attend_stage(nc, f"{name}att", counts, 1, D, h, one[0], one[3], shift_d, out_d, base_d=base_d, bias_d=out_bias_d)


def gps_two_layers(nc, inp, out_d):
    def dram(name, shape, dt=F32):
        return nc.dram_tensor(name, shape, dt).ap()

    xn_d, attn_d, sum_d, x1_d, x2_d, x3_d = (dram(s, [N, D]) for s in ("xn_d", "attn_d", "sum_d", "x1_d", "x2_d", "x3_d"))
    counts_d = dram("counts_d", [N, N], I16)
    h0_d, h1_d = dram("h0_d", [N, 8 * 129]), dram("h1_d", [N, 8 * 97])
    adj_flat = dram("adj_d", [N * N + EXTRA])
    adj_d = adj_flat[0:N * N].rearrange("(s d) -> s d", d=N)
    mask_d = dram("mask_d", [N, N], BF16)
    g1a_d, g1b_d = dram("g1a_d", [N, 1024]), dram("g1b_d", [N, D])
    rows_d, shift_d = dram("rows_d", [8 * N]), dram("shift_d", [2, 8 * N])
    z_parts_d = dram("z_parts_d", [3, 128, N], BF16)
    w1_parts_d = dram("w1_parts_d", [3, 128, EM * EH], BF16)
    b1_parts_d = dram("b1_parts_d", [3, ES, EM * EH], BF16)
    w_parts_d = dram("w_parts_d", [ES, 2 * EM, N], F16)
    comb_d = dram("comb_d", [EG, ES * ER, N])

    def sb(ctx, name, shape, dt=F32, side="left"):
        return ctx.enter_context(nc.sbuf_tensor(name, shape, dt, side=side))

    def high_low(ctx, name):
        return sb(ctx, f"{name}_hi", [128, KB, N], F32R), sb(ctx, f"{name}_lo", [128, KB, N], F32R)

    with ExitStack() as top:
        ident = sb(top, "ident", [128, 128])
        a_s, a_d, a_s02, mx = (sb(top, s, [TP, 8, NT]) for s in ("a_s", "a_d", "a_s02", "mx"))
        load_rows_stage(nc, "ident", inp["ident"], ident[:])

        with ExitStack() as ctx:
            key_off = sb(ctx, "key_off", [TP, EC], I32)
            key_val = sb(ctx, "key_val", [TP, EC])
            edge_stage(nc, ident, inp["src"], inp["dst"], inp["lower"], key_off, key_val, adj_flat)
            parts = high_low(ctx, "y0")
            norm_stage(nc, "ln0", ident, 1e-5, inp["x"], xn_d, inp["L0_mix_ln1_g"], inp["L0_mix_ln1_b"], parts)
            performer_stage(nc, "perf0", parts, inp["L0_mix_qkv_w"], inp["L0_mix_qkv_b"], inp["L0_mix_v_b"],
                            inp["L0_mix_w_orf"], True, 384, HD ** -0.25, 1e-8, attn_d,
                            edges=(key_off, key_val, adj_flat.rearrange("(n a) -> n a", a=1)))
        mask_stage(nc, ident, adj_d, mask_d, counts_d)
        gat_project_stage(nc, "gat00proj", ident, xn_d, D, None, None, inp["L0_gnn_W1"], 8, 128,
                          inp["L0_gnn_att_src1"], inp["L0_gnn_att_dst1"], None, a_s, a_d, rows_d, h_d=h0_d)
        with ExitStack() as graph:
            with ExitStack() as mlp:
                with ExitStack() as ctx:
                    parts = high_low(ctx, "y")
                    proj_stage(nc, "proj0", ident, attn_d, inp["L0_mix_proj_w"], inp["L0_mix_proj_b"], xn_d, inp["x"], sum_d,
                               1e-5, inp["L0_mix_ln2_g"], inp["L0_mix_ln2_b"], parts)
                    hidden = sb(mlp, "hidden", [128, 4 * KB, N], side="right")
                    fc1_stage(nc, parts, inp["L0_mix_fc1_w"], inp["L0_mix_fc1_b"], hidden, mask_d, rows_d, mx)
                counts = sb(graph, "counts0", [TP, NT, N], I16)
                dense_add_stage(nc, "fc2", ident, hidden, 4 * KB, inp["L0_mix_fc2_w"], inp["L0_mix_fc2_b"], sum_d, sum_d,
                                ahead=[(counts[:], tokens(counts_d))])
            gat_shift_stage(nc, "gat00shift", ident, 8, a_s, a_d, mx, a_s02, shift_d)
            gat_attend_stage(nc, "gat00att", counts, 8, 128, None, a_s, a_s02, shift_d, g1a_d, h_d=h0_d)
            gat_one_head(nc, "gat01", ident, g1a_d, 1024, "relu", inp["L0_gnn_b1"], inp["L0_gnn_W2"],
                         inp["L0_gnn_att_src2"], inp["L0_gnn_att_dst2"], counts, mask_d, rows_d, shift_d,
                         a_s, a_d, a_s02, mx, sum_d, inp["L0_gnn_b2"], x1_d)
        with ExitStack() as ctx:
            xT = sb(ctx, "xT0", [128, KB, N])
            norm_stage(nc, "ln1", ident, 1e-5, x1_d, None, None, None, xT)
            wT = sb(ctx, "wT", [128, 4, N])
            router_stage(nc, ident, xT, inp["L0_ffn_P"], inp["L0_ffn_C"], inp["L0_ffn_W1"], inp["L0_ffn_b1"],
                         z_parts_d, w1_parts_d, b1_parts_d, w_parts_d, wT)
            expert_stage(nc, z_parts_d, w1_parts_d, b1_parts_d, w_parts_d, inp["spread"], inp["L0_ffn_W2"],
                         inp["L0_ffn_b2"], wT, comb_d)
            combT = sb(ctx, "combT", [128, N])
            gT = sb(ctx, "gT", [128, 2, N])
            comb_stage(nc, comb_d, combT[:])
            dense_stage(nc, "mixup", combT, inp["L0_ffn_G1"], 2, inp["L0_ffn_g1b"], ACT.Gelu_apprx_tanh, gT)
            dense_add_stage(nc, "mixdown", ident, gT, 2, inp["L0_ffn_G2"], inp["L0_ffn_g2b"], x1_d, x2_d)
        with ExitStack() as ctx:
            parts = high_low(ctx, "y1")
            norm_stage(nc, "ln2", ident, 1e-5, x2_d, xn_d, None, None, parts)
            gat_project_stage(nc, "gat10proj", ident, xn_d, D, None, None, inp["L1_gnn_W1"], 8, 96,
                              inp["L1_gnn_a_src1"], inp["L1_gnn_a_dst1"], None, a_s, a_d, rows_d, h_d=h1_d)
            performer_stage(nc, "perf1", parts, inp["L1_mix_W_qkv"], None, None, inp["L1_mix_random_features"], False, 256,
                            1.0, 1e-6, attn_d, scan=(mask_d, rows_d, 8, mx))
        with ExitStack() as graph:
            counts = sb(graph, "counts1", [TP, NT, N], I16)
            proj_stage(nc, "proj1", ident, attn_d, inp["L1_mix_W_proj"], inp["L1_mix_b_proj"], xn_d, x2_d, sum_d,
                       1e-5, inp["L1_mix_gamma"], inp["L1_mix_beta"], None, ahead=[(counts[:], tokens(counts_d))])
            gat_shift_stage(nc, "gat10shift", ident, 8, a_s, a_d, mx, a_s02, shift_d)
            gat_attend_stage(nc, "gat10att", counts, 8, 96, None, a_s, a_s02, shift_d, g1b_d, h_d=h1_d)
            gat_one_head(nc, "gat11", ident, g1b_d, D, "elu", inp["L1_gnn_b1"], inp["L1_gnn_W2"],
                         inp["L1_gnn_a_src2"], inp["L1_gnn_a_dst2"], counts, mask_d, rows_d, shift_d,
                         a_s, a_d, a_s02, mx, sum_d, inp["L1_gnn_b2"], x3_d)
        bitlinear_stage(nc, ident, x3_d, inp["L1_ffn_w_in"], inp["L1_ffn_w_out"],
                        inp["L1_ffn_g_in"], inp["L1_ffn_g_out"], out_d)



def columns(a):
    return a.reshape(-1, 128).T


def layout(inputs):
    a = {k: np.asarray(v) for k, v in inputs.items()}
    a["L0_gnn_W1"] = a["L0_gnn_W1"].T
    a["L0_gnn_W2"] = a["L0_gnn_W2"].T
    for k in ("L0_gnn_att_src1", "L0_gnn_att_dst1", "L0_gnn_att_src2", "L0_gnn_att_dst2",
              "L1_gnn_a_src1", "L1_gnn_a_dst1", "L1_gnn_a_src2", "L1_gnn_a_dst2"):
        a[k] = a[k].reshape(-1)
    for k in ("L0_mix_ln1_g", "L0_mix_ln1_b", "L0_mix_ln2_g", "L0_mix_ln2_b", "L0_mix_fc1_b", "L0_mix_fc2_b",
              "L0_ffn_g1b", "L0_ffn_g2b"):
        a[k] = columns(a[k])
    a["L0_mix_v_b"] = a["L0_mix_qkv_b"][2 * D:]
    a["L0_mix_qkv_b"] = columns(a["L0_mix_qkv_b"][:2 * D])
    a["L0_ffn_P"] = a["L0_ffn_P"].transpose(1, 0, 2).reshape(D, ES * ER)
    a["L0_ffn_C"] = a["L0_ffn_C"].transpose(0, 2, 1)
    a["L0_ffn_W1"] = a["L0_ffn_W1"].transpose(0, 2, 1, 3).reshape(ES, ER, EM * EH)
    a["L0_ffn_b1"] = a["L0_ffn_b1"].reshape(ES, EM * EH)
    a["L0_ffn_W2"] = a["L0_ffn_W2"].reshape(ES, EJ, 128, ER).transpose(0, 2, 1, 3)
    a["L1_mix_random_features"] = a["L1_mix_random_features"].T
    a["L1_ffn_w_in"] = a["L1_ffn_w_in"].T
    a["L1_ffn_w_out"] = a["L1_ffn_w_out"].T
    a["ident"] = np.eye(128, dtype=np.float32)
    a["lower"] = np.tril(np.ones((128, 128), np.float32), -1)
    spread = np.zeros((2, EM, EJ, 4, EH), np.float16)
    for j in range(EJ):
        for m in range(4):
            spread[0, 4 * j + m, j, m, :] = 1.0
            spread[1, 4 * j + m, j, m, :] = 2.0 ** -12
    a["spread"] = spread.reshape(2 * EM, EJ * 128)
    return {k: np.ascontiguousarray(v) for k, v in a.items()}


def kernel(**inputs):
    import concourse.bacc as _bacc
    from concourse.bass_utils import run_bass_kernel_spmd as _run

    nc = _bacc.Bacc("TRN2", target_bir_lowering=False, num_devices=1)
    arrays, args = {}, {}
    for name, a in layout(inputs).items():
        arrays[f"in_{name}"] = a
        args[name] = nc.dram_tensor(f"in_{name}", a.shape, mybir.dt.from_np(a.dtype), kind="ExternalInput").ap()
    out = nc.dram_tensor("out", (N, D), F32, kind="ExternalOutput").ap()
    gps_two_layers(nc, args, out)
    r = _run(nc, [arrays], core_ids=[0])
    return r.results[0]["out"]
```
